# Optimizing a Trainium2 kernel written in Bass

```python
import numpy as np
import jax
import jax.numpy as jnp

def _softmax(x, axis=-1):
    return jax.nn.softmax(x, axis=axis)

def _gelu(x):
    return jax.nn.gelu(x, approximate=True)

def _silu(x):
    return jax.nn.silu(x)

def _sigmoid(x):
    return jax.nn.sigmoid(x)

def _layernorm(x, axis=-1, eps=1e-05):
    m = jnp.mean(x, axis=axis, keepdims=True)
    v = jnp.var(x, axis=axis, keepdims=True)
    return (x - m) / jnp.sqrt(v + eps)

def _scatter_add(tgt, idx, src, axis=0):
    return tgt.at[idx].add(src)

def _segment_sum(src, seg, n):
    return jax.ops.segment_sum(src, seg, n)
kernel_name = 'mk_hybrid_d2_jaxref_r8_0eefcc'

def setup_inputs(seed: int=0):
    np.random.seed(seed)
    _w = jnp.asarray

    def _L0_attn_a_setup():
        import jax, jax.numpy as jnp
        import numpy as np
        B_, L_, DIM_, DIN_, N_, DTR_, DCONV_ = (2, 256, 128, 256, 16, 64, 4)

        def _ssm_scan(deltaA, deltaB_u):

            def combine(e1, e2):
                a1, b1 = e1
                a2, b2 = e2
                return (a2 * a1, a2 * b1 + b2)
            _, hs = jax.lax.associative_scan(combine, (deltaA, deltaB_u), axis=1)
            return hs
        key = jax.random.key(seed)
        ks = jax.random.split(key, 7)
        s = 0.02
        inp = {'x': jax.random.normal(ks[0], (B_, L_, DIM_), dtype=jnp.float32), 'W_in': jax.random.normal(ks[1], (DIM_, 2 * DIN_), dtype=jnp.float32) * s, 'conv_w': jax.random.normal(ks[2], (DIN_, 1, DCONV_), dtype=jnp.float32) * s, 'conv_b': jnp.zeros((DIN_,), dtype=jnp.float32), 'W_x': jax.random.normal(ks[3], (DIN_, DTR_ + 2 * N_), dtype=jnp.float32) * s, 'W_dt': jax.random.normal(ks[4], (DTR_, DIN_), dtype=jnp.float32) * s, 'b_dt': jnp.zeros((DIN_,), dtype=jnp.float32), 'W_out': jax.random.normal(ks[5], (DIN_, DIM_), dtype=jnp.float32) * s, 'A_log': jnp.log(jnp.broadcast_to(jnp.arange(1, N_ + 1, dtype=jnp.float32), (DIN_, N_))), 'D': jnp.ones((DIN_,), dtype=jnp.float32)}
        return inp
    _L0_attn_a_in = _L0_attn_a_setup()

    def _L0_attn_b_setup():
        import jax, jax.numpy as jnp
        import numpy as np
        D_MODEL = 128
        D_STATE = 64
        BATCH = 4
        SEQ_L = 512
        LN_EPS = 1e-05

        def _reference_tuple_inner(u, A_log, B, C, D, delta, gamma, beta, freq_align, reward):
            b, L, d = u.shape
            A = -jnp.exp(A_log)
            k_idx = jnp.arange(L, dtype=u.dtype)
            powers = jnp.exp(k_idx[:, None] * (delta[0] * A)[None, :])
            K = jnp.einsum('ln,dn->ld', powers, C)
            fft_size = 1 << int(np.ceil(np.log2(2 * L)))
            u_fft = jnp.fft.fft(u, n=fft_size, axis=1)
            K_fft = jnp.fft.fft(K, n=fft_size, axis=0)
            y = jnp.fft.ifft(u_fft * K_fft[None], axis=1).real[:, :L, :]
            y = y + u * D
            y_fft = jnp.fft.fft(y, axis=1)
            y = jnp.fft.ifft(y_fft * freq_align + reward, axis=1).real
            mean = y.mean(-1, keepdims=True)
            var = y.var(-1, keepdims=True)
            y = (y - mean) / jnp.sqrt(var + LN_EPS) * gamma + beta
            delta_mean = delta.mean()
            A_bar_s = jnp.exp(delta_mean * A)
            A_safe = A + 1e-08 * jnp.sign(A)
            B_bar = ((A_bar_s - 1.0) / A_safe)[:, None] * B
            state = jnp.zeros((b, A.shape[0]), u.dtype)
            final_state = A_bar_s * state + jnp.einsum('nd,bd->bn', B_bar, u[:, -1, :])
            return (y, final_state)
        key = jax.random.key(seed)
        ks = jax.random.split(key, 8)
        u = jax.random.normal(ks[0], (BATCH, SEQ_L, D_MODEL), jnp.float32)
        A_log = jax.random.uniform(ks[1], (D_STATE,), jnp.float32, -2.0, -0.1)
        xav = float(np.sqrt(6.0 / (D_STATE + D_MODEL)))
        B = jax.random.uniform(ks[2], (D_STATE, D_MODEL), jnp.float32, -xav, xav) * 0.1
        C = jax.random.uniform(ks[3], (D_MODEL, D_STATE), jnp.float32, -xav, xav) * 0.1
        D = jnp.zeros((D_MODEL,), jnp.float32)
        delta = jax.random.uniform(ks[4], (D_MODEL,), jnp.float32, 0.001, 0.1)
        gamma = jnp.ones((D_MODEL,), jnp.float32)
        beta = jnp.zeros((D_MODEL,), jnp.float32)
        freq_align = jax.random.normal(ks[5], (D_MODEL,), jnp.float32)
        reward = jax.random.normal(ks[6], (D_MODEL,), jnp.float32)
        return dict(u=u, A_log=A_log, B=B, C=C, D=D, delta=delta, gamma=gamma, beta=beta, freq_align=freq_align, reward=reward)
    _L0_attn_b_in = _L0_attn_b_setup()

    def _L0_ffn_setup():
        import jax, jax.numpy as jnp
        import numpy as np
        B, S, D, F, E, R = (4, 256, 128, 512, 8, 4)
        key = jax.random.key(seed)
        ks = jax.random.split(key, 8)
        s_in = 1.0 / np.sqrt(D)
        s_ff = 1.0 / np.sqrt(F)
        return {'hidden_states': jax.random.normal(ks[0], (B, S, D), jnp.float32), 'gate_W': jax.random.normal(ks[1], (E, D), jnp.float32) * s_in, 'gate_b': jnp.zeros((E,), jnp.float32), 'wi_W': jax.random.normal(ks[2], (F, D), jnp.float32) * s_in, 'wi_b': jnp.zeros((F,), jnp.float32), 'wo_W': jax.random.normal(ks[3], (D, F), jnp.float32) * s_ff, 'wo_b': jnp.zeros((D,), jnp.float32), 'lora_A': jax.random.normal(ks[4], (E, R, D), jnp.float32) * s_in, 'lora_B': jax.random.normal(ks[5], (E, F, R), jnp.float32) * 0.02}
    _L0_ffn_in = _L0_ffn_setup()

    def _L1_attn_a_setup():
        import jax, jax.numpy as jnp
        import numpy as np
        DIM = 128
        NUM_HEADS = 16
        HEAD_DIM = DIM // NUM_HEADS

        def _rope_tables(seq_len, dim, dtype):
            inv_freq = 1.0 / 10000.0 ** (jnp.arange(0, dim, 2, dtype=jnp.float32) / dim)
            t = jnp.arange(seq_len, dtype=jnp.float32)
            freqs = jnp.outer(t, inv_freq)
            return (jnp.cos(freqs).astype(dtype), jnp.sin(freqs).astype(dtype))

        def _apply_rope(x, cos_emb, sin_emb):
            x1 = x[..., 0::2]
            x2 = x[..., 1::2]
            return jnp.concatenate((x1 * cos_emb - x2 * sin_emb, x1 * sin_emb + x2 * cos_emb), axis=-1)
        key = jax.random.key(seed)
        k_x, k_qkv, k_out, k_b = jax.random.split(key, 4)
        B, S, D = (2, 256, DIM)
        x = jax.random.normal(k_x, (B, S, D), dtype=jnp.float32)
        w_qkv = jax.random.normal(k_qkv, (3 * D, D), dtype=jnp.float32) * (1.0 / np.sqrt(D))
        w_out = jax.random.normal(k_out, (D, D), dtype=jnp.float32) * (1.0 / np.sqrt(D))
        b_out = jax.random.normal(k_b, (D,), dtype=jnp.float32) * 0.01
        return {'x': x, 'w_qkv': w_qkv, 'w_out': w_out, 'b_out': b_out}
    _L1_attn_a_in = _L1_attn_a_setup()

    def _L1_attn_b_setup():
        import jax, jax.numpy as jnp
        import numpy as np
        CHUNK_FRAMES = 100
        LOOKAHEAD_FRAMES = 50
        NUM_HEADS = 16

        def _allowed_mask(T):
            pos = jnp.arange(T)
            chunk = pos // CHUNK_FRAMES
            chunk_ok = chunk[None, :] <= chunk[:, None]
            look_ok = pos[None, :] <= pos[:, None] + LOOKAHEAD_FRAMES
            return chunk_ok | look_ok
        key = jax.random.key(seed)
        ks = jax.random.split(key, 8)
        B, T, D = (4, 1500, 128)
        s = 1.0 / np.sqrt(D)
        return {'hidden_states': jax.random.normal(ks[0], (B, T, D), jnp.float32), 'Wq': jax.random.normal(ks[1], (D, D), jnp.float32) * s, 'bq': jax.random.normal(ks[2], (D,), jnp.float32) * 0.02, 'Wk': jax.random.normal(ks[3], (D, D), jnp.float32) * s, 'Wv': jax.random.normal(ks[4], (D, D), jnp.float32) * s, 'bv': jax.random.normal(ks[5], (D,), jnp.float32) * 0.02, 'Wo': jax.random.normal(ks[6], (D, D), jnp.float32) * s, 'bo': jax.random.normal(ks[7], (D,), jnp.float32) * 0.02}
    _L1_attn_b_in = _L1_attn_b_setup()

    def _L1_ffn_setup():
        import jax, jax.numpy as jnp
        import numpy as np
        D = 128
        H = 4
        DF = 512
        E = 8
        EPS = 1e-05

        def _layer_norm(x, g, b):
            mu = jnp.mean(x, axis=-1, keepdims=True)
            var = jnp.mean(jnp.square(x - mu), axis=-1, keepdims=True)
            return (x - mu) * jax.lax.rsqrt(var + EPS) * g + b

        def _mha(x, Wqkv, bqkv, Wo, bo):
            S, B, _ = x.shape
            hd = D // H
            qkv = x @ Wqkv.T + bqkv
            q, k, v = jnp.split(qkv, 3, axis=-1)
            to_heads = lambda t: t.reshape(S, B, H, hd).transpose(1, 2, 0, 3)
            q, k, v = (to_heads(q), to_heads(k), to_heads(v))
            scores = jnp.einsum('bhqd,bhkd->bhqk', q, k) * (1.0 / np.sqrt(hd))
            att = jax.nn.softmax(scores, axis=-1)
            o = jnp.einsum('bhqk,bhkd->bhqd', att, v)
            o = o.transpose(2, 0, 1, 3).reshape(S, B, D)
            return o @ Wo.T + bo

        def _moe(x, Wg, W1, b1, W2, b2):
            S, B, _ = x.shape
            xf = x.reshape(S * B, D)
            logits = xf @ Wg.T
            idx = jnp.argmax(logits, axis=-1)
            out = jnp.zeros_like(xf)
            for e in range(E):
                m = (idx == e)[:, None].astype(xf.dtype)
                h = jax.nn.relu(xf @ W1[e] + b1[e])
                out = out + m * (h @ W2[e] + b2[e])
            return out.reshape(S, B, D)
        key = jax.random.key(seed)
        ks = jax.random.split(key, 16)
        S, B = (64, 8)
        s = lambda k, shape, fan: jax.random.normal(k, shape, jnp.float32) * (1.0 / np.sqrt(fan))
        return {'x': jax.random.normal(ks[0], (S, B, D), jnp.float32), 'Wqkv': s(ks[1], (3 * D, D), D), 'bqkv': jnp.zeros((3 * D,), jnp.float32), 'Wo': s(ks[2], (D, D), D), 'bo': jnp.zeros((D,), jnp.float32), 'g1': jnp.ones((D,), jnp.float32), 'be1': jnp.zeros((D,), jnp.float32), 'g2': jnp.ones((D,), jnp.float32), 'be2': jnp.zeros((D,), jnp.float32), 'Wg': s(ks[3], (E, D), D), 'W1': s(ks[4], (E, D, DF), D), 'b1': jnp.zeros((E, DF), jnp.float32), 'W2': s(ks[5], (E, DF, D), DF), 'b2': jnp.zeros((E, D), jnp.float32)}
    _L1_ffn_in = _L1_ffn_setup()
    _d = {'L0_attn_a_x': _L0_attn_a_in['x'], 'L0_attn_a_W_in': _L0_attn_a_in['W_in'], 'L0_attn_a_conv_w': _L0_attn_a_in['conv_w'], 'L0_attn_a_conv_b': _L0_attn_a_in['conv_b'], 'L0_attn_a_W_x': _L0_attn_a_in['W_x'], 'L0_attn_a_W_dt': _L0_attn_a_in['W_dt'], 'L0_attn_a_b_dt': _L0_attn_a_in['b_dt'], 'L0_attn_a_W_out': _L0_attn_a_in['W_out'], 'L0_attn_a_A_log': _L0_attn_a_in['A_log'], 'L0_attn_a_D': _L0_attn_a_in['D'], 'L0_attn_b_A_log': _L0_attn_b_in['A_log'], 'L0_attn_b_B': _L0_attn_b_in['B'], 'L0_attn_b_C': _L0_attn_b_in['C'], 'L0_attn_b_D': _L0_attn_b_in['D'], 'L0_attn_b_delta': _L0_attn_b_in['delta'], 'L0_attn_b_gamma': _L0_attn_b_in['gamma'], 'L0_attn_b_beta': _L0_attn_b_in['beta'], 'L0_attn_b_freq_align': _L0_attn_b_in['freq_align'], 'L0_attn_b_reward': _L0_attn_b_in['reward'], 'L0_ffn_gate_W': _L0_ffn_in['gate_W'], 'L0_ffn_gate_b': _L0_ffn_in['gate_b'], 'L0_ffn_wi_W': _L0_ffn_in['wi_W'], 'L0_ffn_wi_b': _L0_ffn_in['wi_b'], 'L0_ffn_wo_W': _L0_ffn_in['wo_W'], 'L0_ffn_wo_b': _L0_ffn_in['wo_b'], 'L0_ffn_lora_A': _L0_ffn_in['lora_A'], 'L0_ffn_lora_B': _L0_ffn_in['lora_B'], 'L1_attn_a_w_qkv': _L1_attn_a_in['w_qkv'], 'L1_attn_a_w_out': _L1_attn_a_in['w_out'], 'L1_attn_a_b_out': _L1_attn_a_in['b_out'], 'L1_attn_b_Wq': _L1_attn_b_in['Wq'], 'L1_attn_b_bq': _L1_attn_b_in['bq'], 'L1_attn_b_Wk': _L1_attn_b_in['Wk'], 'L1_attn_b_Wv': _L1_attn_b_in['Wv'], 'L1_attn_b_bv': _L1_attn_b_in['bv'], 'L1_attn_b_Wo': _L1_attn_b_in['Wo'], 'L1_attn_b_bo': _L1_attn_b_in['bo'], 'L1_ffn_Wqkv': _L1_ffn_in['Wqkv'], 'L1_ffn_bqkv': _L1_ffn_in['bqkv'], 'L1_ffn_Wo': _L1_ffn_in['Wo'], 'L1_ffn_bo': _L1_ffn_in['bo'], 'L1_ffn_g1': _L1_ffn_in['g1'], 'L1_ffn_be1': _L1_ffn_in['be1'], 'L1_ffn_g2': _L1_ffn_in['g2'], 'L1_ffn_be2': _L1_ffn_in['be2'], 'L1_ffn_Wg': _L1_ffn_in['Wg'], 'L1_ffn_W1': _L1_ffn_in['W1'], 'L1_ffn_b1': _L1_ffn_in['b1'], 'L1_ffn_W2': _L1_ffn_in['W2'], 'L1_ffn_b2': _L1_ffn_in['b2']}
    _x0 = _d['L0_attn_a_x']
    _d['L0_attn_a_x'] = jax.random.normal(jax.random.fold_in(jax.random.key(seed), 1), (8, 256, 128), dtype=_x0.dtype)
    del _x0
    return _d

def reference(L0_attn_a_x, L0_attn_a_W_in, L0_attn_a_conv_w, L0_attn_a_conv_b, L0_attn_a_W_x, L0_attn_a_W_dt, L0_attn_a_b_dt, L0_attn_a_W_out, L0_attn_a_A_log, L0_attn_a_D, L0_attn_b_A_log, L0_attn_b_B, L0_attn_b_C, L0_attn_b_D, L0_attn_b_delta, L0_attn_b_gamma, L0_attn_b_beta, L0_attn_b_freq_align, L0_attn_b_reward, L0_ffn_gate_W, L0_ffn_gate_b, L0_ffn_wi_W, L0_ffn_wi_b, L0_ffn_wo_W, L0_ffn_wo_b, L0_ffn_lora_A, L0_ffn_lora_B, L1_attn_a_w_qkv, L1_attn_a_w_out, L1_attn_a_b_out, L1_attn_b_Wq, L1_attn_b_bq, L1_attn_b_Wk, L1_attn_b_Wv, L1_attn_b_bv, L1_attn_b_Wo, L1_attn_b_bo, L1_ffn_Wqkv, L1_ffn_bqkv, L1_ffn_Wo, L1_ffn_bo, L1_ffn_g1, L1_ffn_be1, L1_ffn_g2, L1_ffn_be2, L1_ffn_Wg, L1_ffn_W1, L1_ffn_b1, L1_ffn_W2, L1_ffn_b2):

    def _L0_attn_a_ref(x, W_in, conv_w, conv_b, W_x, W_dt, b_dt, W_out, A_log, D):
        import jax, jax.numpy as jnp
        import numpy as np
        B_, L_, DIM_, DIN_, N_, DTR_, DCONV_ = (2, 256, 128, 256, 16, 64, 4)

        def _ssm_scan(deltaA, deltaB_u):

            def combine(e1, e2):
                a1, b1 = e1
                a2, b2 = e2
                return (a2 * a1, a2 * b1 + b2)
            _, hs = jax.lax.associative_scan(combine, (deltaA, deltaB_u), axis=1)
            return hs
        b, l, dim = x.shape
        d_in, n = A_log.shape
        dt_rank = W_dt.shape[0]
        d_conv = conv_w.shape[-1]
        xr = x @ W_in
        xs, res = (xr[..., :d_in], xr[..., d_in:])
        xc = jax.lax.conv_general_dilated(xs.transpose(0, 2, 1), conv_w, (1,), [(d_conv - 1, 0)], dimension_numbers=('NCH', 'OIH', 'NCH'), feature_group_count=d_in) + conv_b[None, :, None]
        u = jax.nn.silu(xc.transpose(0, 2, 1))
        x_dbl = u @ W_x
        delta = jax.nn.softplus(x_dbl[..., :dt_rank] @ W_dt + b_dt)
        Bm = x_dbl[..., dt_rank:dt_rank + n]
        Cm = x_dbl[..., dt_rank + n:]
        A = -jnp.exp(A_log)
        deltaA = jnp.exp(delta[..., None] * A)
        deltaB_u = delta[..., None] * Bm[:, :, None, :] * u[..., None]
        hs = _ssm_scan(deltaA, deltaB_u)
        y = jnp.einsum('bldn,bln->bld', hs, Cm) + u * D
        y = y * jax.nn.silu(res)
        return y @ W_out

    def _L0_attn_b_ref(u, A_log, B, C, D, delta, gamma, beta, freq_align, reward):
        import jax, jax.numpy as jnp
        import numpy as np
        D_MODEL = 128
        D_STATE = 64
        BATCH = 4
        SEQ_L = 512
        LN_EPS = 1e-05

        def _reference_tuple_inner(u, A_log, B, C, D, delta, gamma, beta, freq_align, reward):
            b, L, d = u.shape
            A = -jnp.exp(A_log)
            k_idx = jnp.arange(L, dtype=u.dtype)
            powers = jnp.exp(k_idx[:, None] * (delta[0] * A)[None, :])
            K = jnp.einsum('ln,dn->ld', powers, C)
            fft_size = 1 << int(np.ceil(np.log2(2 * L)))
            u_fft = jnp.fft.fft(u, n=fft_size, axis=1)
            K_fft = jnp.fft.fft(K, n=fft_size, axis=0)
            y = jnp.fft.ifft(u_fft * K_fft[None], axis=1).real[:, :L, :]
            y = y + u * D
            y_fft = jnp.fft.fft(y, axis=1)
            y = jnp.fft.ifft(y_fft * freq_align + reward, axis=1).real
            mean = y.mean(-1, keepdims=True)
            var = y.var(-1, keepdims=True)
            y = (y - mean) / jnp.sqrt(var + LN_EPS) * gamma + beta
            delta_mean = delta.mean()
            A_bar_s = jnp.exp(delta_mean * A)
            A_safe = A + 1e-08 * jnp.sign(A)
            B_bar = ((A_bar_s - 1.0) / A_safe)[:, None] * B
            state = jnp.zeros((b, A.shape[0]), u.dtype)
            final_state = A_bar_s * state + jnp.einsum('nd,bd->bn', B_bar, u[:, -1, :])
            return (y, final_state)
        return _reference_tuple_inner(u, A_log, B, C, D, delta, gamma, beta, freq_align, reward)[0]

    def _L0_ffn_ref(hidden_states, gate_W, gate_b, wi_W, wi_b, wo_W, wo_b, lora_A, lora_B):
        import jax, jax.numpy as jnp
        import numpy as np
        B, S, D, F, E, R = (4, 256, 128, 512, 8, 4)
        x = hidden_states
        logits = jnp.einsum('bsd,ed->bse', x, gate_W) + gate_b
        top1 = jnp.argmax(jax.nn.softmax(logits, axis=-1), axis=-1)
        base = jnp.einsum('bsd,fd->bsf', x, wi_W) + wi_b
        out = jnp.zeros_like(x)
        for i in range(lora_A.shape[0]):
            lora = jnp.einsum('bsr,fr->bsf', jnp.einsum('bsd,rd->bsr', x, lora_A[i]), lora_B[i])
            inter = jax.nn.relu(base + lora)
            expert_out = jnp.einsum('bsf,df->bsd', inter, wo_W) + wo_b
            mask = (top1 == i).astype(x.dtype)[..., None]
            out = out + mask * expert_out
        return out

    def _L1_attn_a_ref(x, w_qkv, w_out, b_out):
        import jax, jax.numpy as jnp
        import numpy as np
        DIM = 128
        NUM_HEADS = 16
        HEAD_DIM = DIM // NUM_HEADS

        def _rope_tables(seq_len, dim, dtype):
            inv_freq = 1.0 / 10000.0 ** (jnp.arange(0, dim, 2, dtype=jnp.float32) / dim)
            t = jnp.arange(seq_len, dtype=jnp.float32)
            freqs = jnp.outer(t, inv_freq)
            return (jnp.cos(freqs).astype(dtype), jnp.sin(freqs).astype(dtype))

        def _apply_rope(x, cos_emb, sin_emb):
            x1 = x[..., 0::2]
            x2 = x[..., 1::2]
            return jnp.concatenate((x1 * cos_emb - x2 * sin_emb, x1 * sin_emb + x2 * cos_emb), axis=-1)
        B, S, D = x.shape
        H, hd = (NUM_HEADS, HEAD_DIM)
        qkv = jnp.einsum('bsd,ed->bse', x, w_qkv)
        q, k, v = jnp.split(qkv, 3, axis=-1)
        q, k, v = (t.reshape(B, S, H, hd).transpose(0, 2, 1, 3) for t in (q, k, v))
        cos_emb, sin_emb = _rope_tables(S, hd, x.dtype)
        q = _apply_rope(q, cos_emb, sin_emb)
        k = _apply_rope(k, cos_emb, sin_emb)
        scores = jnp.einsum('bhqd,bhkd->bhqk', q, k) / jnp.sqrt(jnp.asarray(hd, x.dtype))
        attn = jax.nn.softmax(scores, axis=-1)
        out = jnp.einsum('bhqk,bhkd->bhqd', attn, v)
        out = out.transpose(0, 2, 1, 3).reshape(B, S, D)
        return jnp.einsum('bsd,ed->bse', out, w_out) + b_out

    def _L1_attn_b_ref(hidden_states, Wq, bq, Wk, Wv, bv, Wo, bo):
        import jax, jax.numpy as jnp
        import numpy as np
        CHUNK_FRAMES = 100
        LOOKAHEAD_FRAMES = 50
        NUM_HEADS = 16

        def _allowed_mask(T):
            pos = jnp.arange(T)
            chunk = pos // CHUNK_FRAMES
            chunk_ok = chunk[None, :] <= chunk[:, None]
            look_ok = pos[None, :] <= pos[:, None] + LOOKAHEAD_FRAMES
            return chunk_ok | look_ok
        B, T, D = hidden_states.shape
        H = NUM_HEADS
        hd = D // H
        scale = hd ** (-0.5)
        q = (hidden_states @ Wq + bq) * scale
        k = hidden_states @ Wk
        v = hidden_states @ Wv + bv
        q = q.reshape(B, T, H, hd)
        k = k.reshape(B, T, H, hd)
        v = v.reshape(B, T, H, hd)
        scores = jnp.einsum('bqhd,bkhd->bhqk', q, k)
        allowed = _allowed_mask(T)
        neg = jnp.asarray(jnp.finfo(scores.dtype).min, scores.dtype)
        scores = jnp.where(allowed[None, None, :, :], scores, neg)
        attn = jax.nn.softmax(scores, axis=-1)
        out = jnp.einsum('bhqk,bkhd->bqhd', attn, v).reshape(B, T, D)
        return out @ Wo + bo

    def _L1_ffn_ref(x, Wqkv, bqkv, Wo, bo, g1, be1, g2, be2, Wg, W1, b1, W2, b2):
        import jax, jax.numpy as jnp
        import numpy as np
        D = 128
        H = 4
        DF = 512
        E = 8
        EPS = 1e-05

        def _layer_norm(x, g, b):
            mu = jnp.mean(x, axis=-1, keepdims=True)
            var = jnp.mean(jnp.square(x - mu), axis=-1, keepdims=True)
            return (x - mu) * jax.lax.rsqrt(var + EPS) * g + b

        def _mha(x, Wqkv, bqkv, Wo, bo):
            S, B, _ = x.shape
            hd = D // H
            qkv = x @ Wqkv.T + bqkv
            q, k, v = jnp.split(qkv, 3, axis=-1)
            to_heads = lambda t: t.reshape(S, B, H, hd).transpose(1, 2, 0, 3)
            q, k, v = (to_heads(q), to_heads(k), to_heads(v))
            scores = jnp.einsum('bhqd,bhkd->bhqk', q, k) * (1.0 / np.sqrt(hd))
            att = jax.nn.softmax(scores, axis=-1)
            o = jnp.einsum('bhqk,bhkd->bhqd', att, v)
            o = o.transpose(2, 0, 1, 3).reshape(S, B, D)
            return o @ Wo.T + bo

        def _moe(x, Wg, W1, b1, W2, b2):
            S, B, _ = x.shape
            xf = x.reshape(S * B, D)
            logits = xf @ Wg.T
            idx = jnp.argmax(logits, axis=-1)
            out = jnp.zeros_like(xf)
            for e in range(E):
                m = (idx == e)[:, None].astype(xf.dtype)
                h = jax.nn.relu(xf @ W1[e] + b1[e])
                out = out + m * (h @ W2[e] + b2[e])
            return out.reshape(S, B, D)
        y = _layer_norm(x + _mha(x, Wqkv, bqkv, Wo, bo), g1, be1)
        z = _layer_norm(y + _moe(y, Wg, W1, b1, W2, b2), g2, be2)
        return z
    x = L0_attn_a_x
    x = x + _L0_attn_a_ref(_layernorm(x, axis=-1), L0_attn_a_W_in, L0_attn_a_conv_w, L0_attn_a_conv_b, L0_attn_a_W_x, L0_attn_a_W_dt, L0_attn_a_b_dt, L0_attn_a_W_out, L0_attn_a_A_log, L0_attn_a_D)
    x = x + _L0_ffn_ref(_layernorm(x, axis=-1), L0_ffn_gate_W, L0_ffn_gate_b, L0_ffn_wi_W, L0_ffn_wi_b, L0_ffn_wo_W, L0_ffn_wo_b, L0_ffn_lora_A, L0_ffn_lora_B)
    x = x + _L0_attn_b_ref(_layernorm(x, axis=-1), L0_attn_b_A_log, L0_attn_b_B, L0_attn_b_C, L0_attn_b_D, L0_attn_b_delta, L0_attn_b_gamma, L0_attn_b_beta, L0_attn_b_freq_align, L0_attn_b_reward)
    x = x + _L0_ffn_ref(_layernorm(x, axis=-1), L0_ffn_gate_W, L0_ffn_gate_b, L0_ffn_wi_W, L0_ffn_wi_b, L0_ffn_wo_W, L0_ffn_wo_b, L0_ffn_lora_A, L0_ffn_lora_B)
    x = x + _L1_attn_a_ref(_layernorm(x, axis=-1), L1_attn_a_w_qkv, L1_attn_a_w_out, L1_attn_a_b_out)
    x = x + _L1_ffn_ref(_layernorm(x, axis=-1), L1_ffn_Wqkv, L1_ffn_bqkv, L1_ffn_Wo, L1_ffn_bo, L1_ffn_g1, L1_ffn_be1, L1_ffn_g2, L1_ffn_be2, L1_ffn_Wg, L1_ffn_W1, L1_ffn_b1, L1_ffn_W2, L1_ffn_b2)
    x = x + _L1_attn_b_ref(_layernorm(x, axis=-1), L1_attn_b_Wq, L1_attn_b_bq, L1_attn_b_Wk, L1_attn_b_Wv, L1_attn_b_bv, L1_attn_b_Wo, L1_attn_b_bo)
    x = x + _L1_ffn_ref(_layernorm(x, axis=-1), L1_ffn_Wqkv, L1_ffn_bqkv, L1_ffn_Wo, L1_ffn_bo, L1_ffn_g1, L1_ffn_be1, L1_ffn_g2, L1_ffn_be2, L1_ffn_Wg, L1_ffn_W1, L1_ffn_b1, L1_ffn_W2, L1_ffn_b2)
    return x

_drawn_inputs = setup_inputs


def setup_inputs(seed=0):
    import zlib

    import numpy as np

    out = dict(_drawn_inputs(seed))
    spreads = {'L0_attn_a_conv_b': (0.0, 0.8),
     'L0_attn_a_b_dt': (0.0, 0.8),
     'L0_attn_a_D': (1.0, 0.6),
     'L0_attn_b_D': (0.0, 0.518),
     'L0_attn_b_gamma': (1.0, 0.6),
     'L0_attn_b_beta': (0.0, 0.8),
     'L0_ffn_gate_b': (0.0, 2.0),
     'L0_ffn_wi_b': (0.0, 0.676),
     'L0_ffn_wo_b': (0.0, 0.548),
     'L1_ffn_bqkv': (0.0, 0.314),
     'L1_ffn_bo': (0.0, 0.443),
     'L1_ffn_g1': (1.0, 0.2),
     'L1_ffn_be1': (0.0, 0.1),
     'L1_ffn_g2': (1.0, 0.6),
     'L1_ffn_be2': (0.0, 0.8),
     'L1_ffn_b1': (0.0, 0.8),
     'L1_ffn_b2': (0.0, 0.8)}
    factors = {'L0_attn_a_W_in': 8.0,
     'L0_attn_a_conv_w': 8.0,
     'L0_attn_a_W_x': 8.0,
     'L0_attn_a_W_dt': 8.0,
     'L0_attn_a_W_out': 8.0,
     'L0_attn_a_A_log': 8.0,
     'L1_attn_b_bq': 64.0,
     'L1_attn_b_bo': 39.544,
     'L0_attn_b_A_log': 2.87,
     'L0_attn_b_delta': 8.0,
     'L0_attn_b_reward': 8.0,
     'L0_ffn_gate_W': 8.0,
     'L0_ffn_lora_A': 8.0,
     'L0_ffn_lora_B': 8.0,
     'L1_attn_a_w_qkv': 3.747,
     'L1_attn_a_w_out': 3.79,
     'L1_attn_a_b_out': 21.54,
     'L1_attn_b_Wq': 5.903,
     'L1_attn_b_Wk': 5.837,
     'L1_attn_b_Wv': 3.949,
     'L1_attn_b_bv': 8.0,
     'L1_attn_b_Wo': 4.061}
    for name, (base, spread) in spreads.items():
        noise = np.random.default_rng([zlib.crc32(name.encode()), seed]).standard_normal(out[name].shape)
        drawn = base * np.exp(spread * noise) if base else spread * noise
        out[name] = jnp.asarray(drawn.astype(out[name].dtype))
    for name, factor in factors.items():
        out[name] = (out[name] * factor).astype(out[name].dtype)
    return out
```

```python
from contextlib import ExitStack

import concourse.bass as bass
import numpy as np
from concourse import mybir

ALU = mybir.AluOpType
ACT = mybir.ActivationFunctionType
AX = mybir.AxisListType
F32 = mybir.dt.float32
BF16 = mybir.dt.bfloat16

P = 128
BATCH, SEQ, DIM = 8, 256, 128
TOK = BATCH * SEQ
TILES = TOK // P
BANK = 512
GROUPS = TOK // BANK
GT = TILES // GROUPS
EPS = 1e-5

CONV = 4
PAD = CONV - 1
DIN, NST, DTR = 256, 16, 64
CH = DIN // P
HALVES = 2
HB = BATCH // HALVES
HT = TOK // HALVES
LNST = 64
TOEPLITZ_LOADS = 8
FF, FT = 512, 4
EXP, RANK = 8, 4
ER = EXP * RANK
HEADS, HD = 16, 8
CHUNK_FRAMES, LOOKAHEAD = 100, 50
NEG = -1e30
MH, MHD = 4, 32
PG = 16
NPG = SEQ // PG


class Net:
    pass


def open_memory(nc, ctx):
    m = Net()

    def sb(name, shape, dt=F32):
        return ctx.enter_context(nc.sbuf_tensor(name, shape, dt))

    m.x = sb("x_res", [P, TILES, DIM])
    m.xn = sb("x_norm", [P, TILES, DIM])
    m.xt = sb("x_norm_t", [P, BATCH, PAD + SEQ])
    m.ident = sb("ident", [P, P])
    m.identb = sb("identb", [P, P], BF16)
    m.stats = sb("ln_stats", [P, TILES, 6])
    m.mv = sb("ln_mean_var", [P, TILES, 2])
    m.ve = sb("ln_var_eps", [P, TILES])
    m.rstd = sb("ln_rstd", [P, TILES])
    m.mhalf = sb("minus_half", [P, TILES])
    m.ones = sb("ones_row", [P, P])
    m.ps = ctx.enter_context(nc.psum_tensor("psum", [P, 8, BANK], F32))
    return m


def sems(nc, ctx, names, prefix=""):
    held = {n: ctx.enter_context(nc.semaphore(prefix + n)) for n in names.split()}

    def clear():
        for h in held.values():
            nc.gpsimd.sem_clear(h)

    ctx.callback(clear)
    return held


def load_weights(nc, m, ctx, dram):
    def sb(name, shape, dt=F32):
        return ctx.enter_context(nc.sbuf_tensor(name, shape, dt))

    w = m.w = Net()
    w.in_w = sb("w_in", [P, 2 * DIN])
    w.conv_rows = sb("w_conv_rows", [P, CONV, DIN])
    w.conv_b = sb("w_conv_b", [P, CH])
    w.x_w = sb("w_x", [P, CH, DTR + 2 * NST])
    w.dt_w = sb("w_dt", [DTR, DIN])
    w.dt_b = sb("w_dt_b", [P, CH])
    w.a_log = sb("w_a_log", [P, CH, NST])
    w.d_skip = sb("w_d_skip", [P, CH])
    w.out_w = sb("w_out", [P, CH, DIM])
    w.lc_a = sb("lc_a_log", [LNST, 1])
    w.lc_ct = sb("lc_ct", [LNST, DIM])
    w.lc_delta = sb("lc_delta0", [P, 1])
    w.lc_rows = sb("lc_rows", [P, 5, DIM])
    w.lc_arow = sb("lc_a_row", [P, LNST])
    w.gate = sb("f_gate", [P, EXP + ER])
    w.gate_b = sb("f_gate_b", [P, EXP])
    w.wi = sb("f_wi", [P, FF])
    w.wi_b = sb("f_wi_b", [P, FT])
    w.wo = sb("f_wo", [P, FT, DIM])
    w.wo_b = sb("f_wo_b", [P, DIM])
    w.lora_b = sb("f_lora_b", [ER, FF])
    for name, rope in (("a1", True), ("a2", False)):
        a = Net()
        a.wq1, a.wk1, a.wv = (sb(f"{name}_{n}", [P, DIM]) for n in ("wq", "wk", "wv"))
        a.wo = sb(f"{name}_wo", [P, 4, DIM])
        a.bo = sb(f"{name}_bo", [P, DIM])
        if rope:
            a.wq2, a.wk2 = sb(f"{name}_wq2", [P, DIM]), sb(f"{name}_wk2", [P, DIM])
            a.cos, a.sin = sb(f"{name}_cos", [P, SEQ]), sb(f"{name}_sin", [P, SEQ])
            w.a1 = a
        else:
            a.bq = sb(f"{name}_bq", [P, 1])
            a.bv = sb(f"{name}_bv", [P, DIM])
            a.mask_q, a.mask_k = (sb(f"{name}_{n}", [P, 2, SEQ], BF16) for n in ("mask_q", "mask_k"))
            w.a2 = a
    w.head_mask = sb("head_mask", [P, 4])
    w.head_rows = sb("head_rows", [P, MH])
    w.pick = sb("pick_max", [P, 4, P], BF16)
    w.m_q, w.m_k, w.m_v, w.m_o = (sb(f"m_{n}", [P, DIM]) for n in "qkvo")
    w.m_bqkv = sb("m_bqkv", [P, 3])
    w.m_gb = sb("m_gb", [P, 2])
    w.m_rows = sb("m_rows", [P, 5, DIM])
    w.m_gate = sb("m_gate", [P, EXP])
    w.m_mask = sb("m_mask", [P, P], BF16)
    for a in (w.a1, w.a2):
        a.head_mask, a.pick = w.head_mask, w.pick
    copies = [(w.in_w, "in_w"), (w.conv_b, "conv_b"), (w.x_w, "x_w"), (w.dt_w, "dt_w"), (w.dt_b, "dt_b"),
              (w.a_log, "a_log"), (w.d_skip, "d_skip"), (w.out_w, "out_w"), (w.lc_a, "lc_a"),
              (w.lc_ct, "lc_ct"), (w.gate, "gate"), (w.wi, "wi"), (w.wi_b, "wi_b"), (w.wo, "wo"),
              (w.lora_b, "lora_b"), (w.a1.wq1, "a1_wq1"), (w.a1.wq2, "a1_wq2"), (w.a1.wk1, "a1_wk1"),
              (w.a1.wk2, "a1_wk2"), (w.a1.wv, "a1_wv"), (w.a1.wo, "a1_wo"), (w.a1.cos, "a1_cos"),
              (w.a1.sin, "a1_sin"), (w.a2.wq1, "a2_wq"), (w.a2.wk1, "a2_wk"), (w.a2.wv, "a2_wv"),
              (w.a2.wo, "a2_wo"), (w.a2.bq, "a2_bq"), (w.head_mask, "head_mask"), (w.head_rows, "head_rows"), (w.m_q, "m_q"), (w.m_k, "m_k"),
              (w.m_v, "m_v"), (w.m_o, "m_o"), (w.m_bqkv, "m_bqkv"), (w.m_gb, "m_gb"), (w.m_gate, "m_gate")]
    spread = [(w.conv_rows, "conv_rows"), (w.lc_delta, "lc_delta"), (w.lc_rows, "lc_rows"), (w.lc_arow, "lc_arow"),
              (w.gate_b, "gate_b"), (w.wo_b, "wo_b"), (w.a1.bo, "a1_bo"), (w.a2.bo, "a2_bo"), (w.a2.bv, "a2_bv"), (w.m_rows, "m_rows")]
    w.tables = [(w.a2.mask_q, "mask_q"), (w.a2.mask_k, "mask_k"), (w.pick, "pick_max"), (w.m_mask, "m_mask")]

    return copies, spread


def on_all_partitions(ap):
    return bass.AP(ap.tensor, ap.offset, [[0, P]] + [list(d) for d in ap.ap])


def setup(nc, m, ctx, dram):
    copies, spread = load_weights(nc, m, ctx, dram)
    w = m.w
    m.toeplitz_loaded = ctx.enter_context(nc.semaphore("toeplitz_loaded"))
    m.lc_pow = ctx.enter_context(nc.sbuf_tensor("lc_pow", [LNST, P + 1], F32))
    m.lc_powt = ctx.enter_context(nc.sbuf_tensor("lc_powt", [P, LNST], F32))
    m.kernel_dram = kernel_dram = nc.dram_tensor("kernel_scratch", (DIM, 2 * P), F32, kind="Internal").ap()
    with ExitStack() as own:
        def sb(name, shape, dt=F32):
            return own.enter_context(nc.sbuf_tensor(name, shape, dt))

        steps = sb("steps", [LNST, P + 1])
        back = sb("steps_back", [P, 1])
        da = sb("delta_a", [LNST, 1])
        dar = sb("delta_a_row", [P, LNST])
        kpad = sb("kernel_padded", [DIM, 2 * P])
        wide = [sb(f"table{i}", list(t.shape)) for i, (t, _) in enumerate(w.tables)]
        s = sems(nc, own, "su_loaded su_w su_consts su_zeros su_dve su_rates su_pow su_kpsum su_kernel su_kdram su_tables")
        with nc.Block() as block:
            @block.sync
            def _(sp):
                sp.dma_start(m.x[:], dram["x"].rearrange("b (h p) d -> p (b h) d", p=P)).then_inc(s["su_w"], 16)
                for dst, (_, name) in zip(wide, w.tables):
                    sp.dma_start(dst[:], dram[name]).then_inc(s["su_tables"], 16)
                for dst, name in copies:
                    sp.dma_start(dst[:], dram[name]).then_inc(s["su_w"], 16)
                sp.wait_ge(s["su_kernel"], 1)
                sp.dma_start(kernel_dram, kpad[:]).then_inc(s["su_kdram"], 16)
                sp.wait_ge(s["su_kdram"], 16)
                sp.wait_ge(s["su_w"], 16 * (1 + len(copies)))

            @block.scalar
            def _(act):
                for dst, name in spread:
                    act.dma_start(dst[:], on_all_partitions(dram[name])).then_inc(s["su_loaded"], 16)
                act.wait_ge(s["su_w"], 16 * (1 + len(copies)))
                act.wait_ge(s["su_loaded"], 16 * len(spread))
                nc.scalar.activation(da[:], w.lc_a[:], ACT.Exp).then_inc(s["su_rates"], 1)
                nc.scalar.activation(dar[:], w.lc_arow[:], ACT.Exp).then_inc(s["su_rates"], 1)
                nc.scalar.activation(w.a_log[:], w.a_log[:], ACT.Exp).then_inc(s["su_rates"], 1)
                act.wait_ge(s["su_dve"], 3)
                act.wait_ge(s["su_consts"], 1)
                nc.scalar.activation(m.lc_pow[:], steps[:], ACT.Exp, scale=da[:]).then_inc(s["su_pow"], 1)
                nc.scalar.activation(m.lc_powt[:], dar[:], ACT.Exp, scale=back[:]).then_inc(s["su_pow"], 1)

            @block.vector
            def _(dve):
                nc.vector.memset(kpad[:], 0.0).then_inc(s["su_zeros"], 1)
                nc.vector.memset(m.xt[:], 0.0)
                nc.vector.memset(m.mhalf[:], -0.5)
                nc.vector.memset(m.ones[:], 1.0)
                dve.wait_ge(s["su_tables"], 16 * len(wide))
                for src, (dst, _) in zip(wide, w.tables):
                    nc.vector.tensor_copy(dst[:], src[:])
                dve.wait_ge(s["su_rates"], 3)
                nc.vector.tensor_scalar(da[:], da[:], w.lc_delta[0:LNST], -1.0, ALU.mult, ALU.mult).then_inc(s["su_dve"], 1)
                nc.vector.tensor_scalar(dar[:], dar[:], w.lc_delta[:], -1.0, ALU.mult, ALU.mult).then_inc(s["su_dve"], 1)
                nc.vector.tensor_scalar(w.a_log[:], w.a_log[:], -1.0, None, ALU.mult).then_inc(s["su_dve"], 1)
                dve.wait_ge(s["su_kpsum"], 1)
                dve.wait_ge(s["su_zeros"], 1)
                nc.vector.tensor_copy(kpad[:, P - 1:2 * P - 1], m.ps[:, 0, 0:P]).then_inc(s["su_kernel"], 1)

            @block.gpsimd
            def _(pool):
                nc.gpsimd.iota(steps[:], [[1, P + 1]], base=0, channel_multiplier=0,
                               allow_small_or_imprecise_dtypes=True)
                nc.gpsimd.iota(back[:], [[0, 1]], base=P - 1, channel_multiplier=-1,
                               allow_small_or_imprecise_dtypes=True).then_inc(s["su_consts"], 1)
                nc.gpsimd.memset(m.ident[:], 0.0)
                nc.gpsimd.memset(m.identb[:], 0.0).then_inc(s["su_consts"], 1)
                pool.wait_ge(s["su_consts"], 2)
                for t in (m.ident, m.identb):
                    nc.gpsimd.affine_select(out=t[:], in_=t[:], compare_op=ALU.not_equal, fill=1.0, base=0,
                                            pattern=[[-1, P]], channel_multiplier=1)

            @block.tensor
            def _(pe):
                pe.wait_ge(s["su_pow"], 1)
                nc.tensor.matmul(m.ps[:, 0, 0:P], w.lc_ct[:], m.lc_pow[:, 0:P], start=True,
                                 stop=True).then_inc(s["su_kpsum"], 1)
    return


def layernorm(nc, m, name, transposed=True, padded=True):
    with ExitStack() as own:
        k = sems(nc, own, "stats mv ve rstd xn xtp xt", f"{name}_")
        with nc.Block() as block:
            @block.vector
            def _(dve):
                for t in range(TILES):
                    ins = nc.vector.bn_stats(m.stats[:, t, :], m.x[:, t, :])
                ins.then_inc(k["stats"], 1)
                dve.wait_ge(k["stats"], 1)
                for t in range(TILES):
                    ins = nc.vector.bn_aggr(m.mv[:, t, :], m.stats[:, t, :])
                ins.then_inc(k["mv"], 1)
                dve.wait_ge(k["mv"], 1)
                nc.vector.tensor_scalar(m.ve[:], m.mv[:, :, 1], EPS, None, ALU.add).then_inc(k["ve"], 1)
                dve.wait_ge(k["rstd"], 1)
                for g in range(GROUPS):
                    for t in range(g * GT, (g + 1) * GT):
                        ins = nc.vector.tensor_scalar(m.xn[:, t, :], m.x[:, t, :], m.mv[:, t, 0:1],
                                                      m.rstd[:, t:t + 1], ALU.subtract, ALU.mult)
                    ins.then_inc(k["xn"], 1)

            @block.gpsimd
            def _(pool):
                pool.wait_ge(k["ve"], 1)
                nc.gpsimd.tensor_tensor(m.rstd[:], m.ve[:], m.mhalf[:], ALU.pow).then_inc(k["rstd"], 1)

            if transposed:
                @block.tensor
                def _(pe):
                    for g in range(GROUPS):
                        pe.wait_ge(k["xn"], g + 1)
                        for t in range(GT):
                            ins = nc.tensor.transpose(m.ps[:, g, t * P:(t + 1) * P], m.xn[:, g * GT + t, :],
                                                      m.ident[:])
                        ins.then_inc(k["xtp"], 1)

                @block.scalar
                def _(act):
                    for g in range(GROUPS):
                        act.wait_ge(k["xtp"], g + 1)
                        nc.scalar.activation(m.xt[:, 2 * g:2 * g + 2, PAD:],
                                             m.ps[:, g, :].rearrange("p (b t) -> p b t", b=2), ACT.Copy)


def state_space(nc, m):
    w = m.w
    with ExitStack() as own:
        def sb(name, shape, dt=F32):
            return own.enter_context(nc.sbuf_tensor(name, shape, dt))

        tap_w = w.conv_rows
        d_diag = sb("d_diag", [P, CH, P])
        pick = sb("pick", [96, 2 * NST, P], BF16)
        u = sb("u", [P, CH, HT])
        gate = sb("res_gate", [P, CH, HT])
        bc3 = sb("bc_split", [96, HT], BF16)
        bcm = sb("bc_mid", [96, HT], BF16)
        w_bc = sb("w_bc3", [P, CH, 96])
        delta = sb("delta", [P, CH, HT])
        t_abs = sb("t_abs", [P, CH, HT])
        du = m.xn[:].rearrange("p (c a) d -> p c (a d)", c=CH)
        bs = sb("b_rows", [P, 2, HT])
        cs = sb("c_rows", [P, 2, HT])
        da = sb("decay", [P, 2, CH, HB, SEQ])
        hs = sb("h_state", [P, 2, CH, HT])
        bcr, bcr2 = hs[0:96, 0, 0, :], hs[0:96, 0, 1, :]
        dt_in = hs[0:DTR, 1, 0, :]
        y = t_abs
        s = sems(nc, own, "ss_set ss_pool ss_xs ss_u ss_res ss_gate ss_xd ss_dtin ss_split ss_bc ss_z ss_expn ss_abs ss_sp ss_relu ss_delta ss_du "
                          "ss_pick ss_rows ss_free ss_da ss_dbu ss_h ss_hc ss_y0 ss_acc ss_y ss_o ss_x")
        ps = m.ps
        BC_BANKS, Y_BANKS = (0, 1, 2, 3), (4, 5, 6, 7)
        with nc.Block() as block:
            @block.gpsimd
            def _(pool):
                nc.gpsimd.memset(pick[:], 0.0)
                nc.gpsimd.memset(da[:, :, :, :, 0:1], 0.0).then_inc(s["ss_pool"], 1)
                pool.wait_ge(s["ss_pool"], 1)
                for part in range(3):
                    nc.gpsimd.affine_select(out=pick[:], in_=pick[:], compare_op=ALU.not_equal, fill=1.0,
                                            base=-32 * part, pattern=[[-1, 2 * NST], [0, P]],
                                            channel_multiplier=1).then_inc(s["ss_pool"], 1)
                    pool.wait_ge(s["ss_pool"], 2 + part)
                for half in range(HALVES):
                    base = half * NST
                    with pool.Fori(0, NST // 2) as pair:
                        n = pair * 2
                        for j in range(2):
                            pool.wait_ge(s["ss_rows"], n + (base + j + 1))
                            for c in range(CH):
                                unit = n * CH + ((base + j) * CH + c + 1)
                                pool.wait_ge(s["ss_h"], unit)
                                nc.gpsimd.tensor_tensor(hs[:, j, c, :], hs[:, j, c, :], cs[:, j, :],
                                                        ALU.mult).then_inc(s["ss_hc"], 1)
                            pool.wait_ge(s["ss_hc"], n * CH + (base + j + 1) * CH)
                            pool.sem_inc(s["ss_free"], 1)

            @block.vector
            def _(dve):
                for k in range(CONV):
                    nc.vector.tensor_tensor(tap_w[:, k, :], w.in_w[:, 0:DIN], w.conv_rows[:, k, :], ALU.mult)
                for c in range(CH):
                    for part in range(3):
                        nc.vector.tensor_copy(w_bc[:, c, part * 32:part * 32 + 32], w.x_w[:, c, DTR:])
                    ins = nc.vector.tensor_scalar(d_diag[:, c, :], m.ident[:], w.d_skip[:, c:c + 1], None, ALU.mult)
                ins.then_inc(s["ss_set"], 1)
                for half in range(HALVES):
                    split = 5 * half
                    dve.wait_ge(s["ss_xd"], half + 1)
                    src = ps[0:96, 2:4, :].rearrange("p a b -> p (a b)")
                    nc.vector.tensor_copy(bc3[:], src).then_inc(s["ss_split"], 1)
                    dve.wait_ge(s["ss_split"], split + 1)
                    nc.vector.tensor_tensor(bcr, src, bc3[:], ALU.subtract).then_inc(s["ss_split"], 1)
                    dve.wait_ge(s["ss_split"], split + 2)
                    nc.vector.tensor_copy(bcm[:], bcr).then_inc(s["ss_split"], 1)
                    dve.wait_ge(s["ss_split"], split + 3)
                    nc.vector.tensor_copy(bc3[32:64, :], bcm[32:64, :])
                    nc.vector.tensor_tensor(bcr2, bcr, bcm[:], ALU.subtract).then_inc(s["ss_split"], 1)
                    dve.wait_ge(s["ss_split"], split + 4)
                    nc.vector.tensor_copy(bc3[64:96, :], bcr2[64:96, :]).then_inc(s["ss_split"], 1)
                    dve.wait_ge(s["ss_abs"], CH * (half + 1))
                    for c in range(CH):
                        zc = ps[:, 4 + 2 * c:6 + 2 * c, :].rearrange("p a b -> p (a b)")
                        ins = nc.vector.tensor_scalar(delta[:, c, :], zc, w.dt_b[:, c:c + 1], 0.0, ALU.add, ALU.max)
                    ins.then_inc(s["ss_relu"], 1)
                    dve.wait_ge(s["ss_relu"], half + 1)
                    dve.wait_ge(s["ss_sp"], half + 1)
                    nc.vector.tensor_tensor(delta[:], delta[:], t_abs[:], ALU.add).then_inc(s["ss_delta"], 1)
                    dve.wait_ge(s["ss_delta"], half + 1)
                    nc.vector.tensor_tensor(du[:], delta[:], u[:], ALU.mult).then_inc(s["ss_du"], 1)
                    dve.wait_ge(s["ss_du"], half + 1)
                    base = half * NST
                    with dve.Fori(0, NST // 2) as pair:
                        n = pair * 2
                        for j in range(2):
                            dve.wait_ge(s["ss_rows"], n + (base + j + 1))
                            for c in range(CH):
                                unit = n * CH + ((base + j) * CH + c + 1)
                                dve.wait_ge(s["ss_acc"], unit)
                                nc.vector.tensor_tensor(hs[:, j, c, :], du[:, c, :], bs[:, j, :],
                                                        ALU.mult).then_inc(s["ss_dbu"], 1)
                                dve.wait_ge(s["ss_da"], unit)
                                dve.wait_ge(s["ss_dbu"], unit)
                                nc.vector.tensor_tensor_scan(
                                    hs[:, j, c, :], da[:, j, c, :, :].rearrange("p b t -> p (b t)"), hs[:, j, c, :],
                                    0.0, ALU.mult, ALU.add).then_inc(s["ss_h"], 1)
                    dve.wait_ge(s["ss_acc"], CH * NST * (half + 1) + 2 * CH)
                    for c in range(CH):
                        nc.vector.tensor_tensor(y[:, c, :], ps[:, 4 + 2 * c:6 + 2 * c, :].rearrange("p a b -> p (a b)"),
                                                gate[:, c, :], ALU.mult).then_inc(s["ss_y"], 1)
                    dve.wait_ge(s["ss_o"], half + 1)
                    xh = m.x[:, half * 8:half * 8 + 8, :].rearrange("p t d -> p (t d)")
                    nc.vector.tensor_tensor(xh, xh, ps[:, 0:2, :].rearrange("p a b -> p (a b)"),
                                            ALU.add).then_inc(s["ss_x"], 1)

            @block.tensor
            def _(pe):
                pe.sem_inc(s["ss_acc"], 2 * CH)
                pe.wait_ge(s["ss_set"], 1)
                pe.wait_ge(s["ss_pool"], 4)
                for half in range(HALVES):
                    if half:
                        pe.wait_ge(s["ss_x"], half)
                    for c in range(CH):
                        for q in range(2):
                            b0 = half * HB + 2 * q
                            for k in range(CONV):
                                ins = nc.tensor.matmul(ps[:, 2 * c + q, :], tap_w[:, k, c * P:(c + 1) * P],
                                                       m.xt[:, b0:b0 + 2, k:k + SEQ], start=(k == 0),
                                                       stop=(k == CONV - 1))
                        ins.then_inc(s["ss_xs"], 1)
                    for c in range(CH):
                        for q in range(2):
                            b0 = half * HB + 2 * q
                            ins = nc.tensor.matmul(ps[:, 4 + 2 * c + q, :], w.in_w[:, DIN + c * P:DIN + (c + 1) * P],
                                                   m.xt[:, b0:b0 + 2, PAD:], start=True, stop=True)
                        ins.then_inc(s["ss_res"], 1)
                    pe.wait_ge(s["ss_u"], CH * (half + 1))
                    for q in range(2):
                        for c in range(CH):
                            nc.tensor.matmul(ps[0:DTR, q, :], w.x_w[:, c, 0:DTR], u[:, c, q * BANK:(q + 1) * BANK],
                                             start=(c == 0), stop=(c == CH - 1))
                        for c in range(CH):
                            ins = nc.tensor.matmul(ps[0:96, 2 + q, :], w_bc[:, c, :], u[:, c, q * BANK:(q + 1) * BANK],
                                                   start=(c == 0), stop=(c == CH - 1))
                    ins.then_inc(s["ss_xd"], 1)
                    pe.wait_ge(s["ss_dtin"], half + 1)
                    pe.wait_ge(s["ss_gate"], CH * (half + 1))
                    for c in range(CH):
                        for q in range(2):
                            ins = nc.tensor.matmul(ps[:, 4 + 2 * c + q, :], w.dt_w[:, c * P:(c + 1) * P],
                                                   dt_in[:, q * BANK:(q + 1) * BANK], start=True, stop=True)
                    ins.then_inc(s["ss_z"], 1)
                    pe.wait_ge(s["ss_split"], 5 * (half + 1))
                    pe.wait_ge(s["ss_relu"], half + 1)
                    pe.wait_ge(s["ss_abs"], CH * (half + 1))
                    for c in range(CH):
                        for q in range(2):
                            nc.tensor.matmul(ps[:, 4 + 2 * c + q, :], d_diag[:, c, :], u[:, c, q * BANK:(q + 1) * BANK],
                                             start=True, stop=False, skip_group_check=True)
                    base = half * NST

                    def rows(n, j):
                        if base or j:
                            pe.wait_ge(s["ss_rows"], n + (base + j))
                        for k in range(2):
                            r = pick[:, bass.ds(n + (j + k * NST), 1), :].rearrange("k a p -> k (a p)")
                            for q in range(2):
                                ins = nc.tensor.matmul(ps[:, 2 * k + q, :], r, bc3[:, q * BANK:(q + 1) * BANK],
                                                       start=True, stop=True)
                        ins.then_inc(s["ss_pick"], 1)

                    def add_state(n, j):
                        for c in range(CH):
                            pe.wait_ge(s["ss_hc"], n * CH + ((base + j) * CH + c + 1))
                            for q in range(2):
                                ins = nc.tensor.matmul(ps[:, 4 + 2 * c + q, :], m.ident[:],
                                                       hs[:, j % 2, c, q * BANK:(q + 1) * BANK], start=False,
                                                       stop=False, skip_group_check=True)
                            ins.then_inc(s["ss_acc"], 1)

                    rows(0, 0)
                    with pe.Fori(0, NST // 2 - 1) as pair:
                        n = pair * 2
                        for j in range(2):
                            rows(n, j + 1)
                            add_state(n, j)
                    rows(0, NST - 1)
                    add_state(0, NST - 2)
                    add_state(0, NST - 1)
                    for q in range(2):
                        for t in range(4):
                            for c in range(CH):
                                pe.wait_ge(s["ss_y"], CH * (half + 1))
                                ins = nc.tensor.matmul(ps[:, q, t * P:(t + 1) * P],
                                                       y[:, c, (4 * q + t) * P:(4 * q + t + 1) * P], w.out_w[:, c, :],
                                                       start=(t == 0 and c == 0), stop=(c == CH - 1),
                                                       skip_group_check=True)
                    ins.then_inc(s["ss_o"], 1)

            @block.scalar
            def _(act):
                for half in range(HALVES):
                    for c in range(CH):
                        act.wait_ge(s["ss_xs"], CH * half + c + 1)
                        nc.scalar.activation(u[:, c, :], ps[:, 2 * c:2 * c + 2, :].rearrange("p a b -> p (a b)"),
                                             ACT.Silu, bias=w.conv_b[:, c:c + 1]).then_inc(s["ss_u"], 1)
                    for c in range(CH):
                        act.wait_ge(s["ss_res"], CH * half + c + 1)
                        nc.scalar.activation(gate[:, c, :], ps[:, 4 + 2 * c:6 + 2 * c, :].rearrange("p a b -> p (a b)"),
                                             ACT.Silu).then_inc(s["ss_gate"], 1)
                    act.wait_ge(s["ss_xd"], half + 1)
                    nc.scalar.activation(dt_in, ps[0:DTR, 0:2, :].rearrange("p a b -> p (a b)"),
                                         ACT.Copy).then_inc(s["ss_dtin"], 1)
                    act.wait_ge(s["ss_z"], half + 1)
                    for c in range(CH):
                        nc.scalar.activation(t_abs[:, c, :], ps[:, 4 + 2 * c:6 + 2 * c, :].rearrange("p a b -> p (a b)"),
                                             ACT.Abs, bias=w.dt_b[:, c:c + 1]).then_inc(s["ss_abs"], 1)
                    act.wait_ge(s["ss_abs"], CH * (half + 1))
                    nc.scalar.activation(t_abs[:], t_abs[:], ACT.Exp, scale=-1.0).then_inc(s["ss_expn"], 1)
                    act.wait_ge(s["ss_expn"], half + 1)
                    nc.scalar.activation(t_abs[:], t_abs[:], ACT.Ln, bias=1.0).then_inc(s["ss_sp"], 1)
                    base = half * NST
                    act.wait_ge(s["ss_delta"], half + 1)
                    if half == 0:
                        act.wait_ge(s["ss_pool"], 1)
                        act.sem_inc(s["ss_free"], 2)
                    with act.Fori(0, NST // 2) as pair:
                        n = pair * 2
                        for j in range(2):
                            act.wait_ge(s["ss_free"], n + (base + j + 1))
                            for c in range(CH):
                                nc.scalar.activation(
                                    da[:, j, c, :, 1:], delta[:, c, :].rearrange("p (b t) -> p b t", b=HB)[:, :, 1:],
                                    ACT.Exp, scale=w.a_log[:, c, bass.ds(n + j, 1)]).then_inc(s["ss_da"], 1)
                            act.wait_ge(s["ss_pick"], n + (base + j + 1))
                            nc.scalar.activation(bs[:, j, :], ps[:, 0:2, :].rearrange("p a b -> p (a b)"), ACT.Copy)
                            nc.scalar.activation(cs[:, j, :], ps[:, 2:4, :].rearrange("p a b -> p (a b)"),
                                                 ACT.Copy).then_inc(s["ss_rows"], 1)
                    act.wait_ge(s["ss_y"], CH * (half + 1))


def lora_ffn(nc, m, name, prefetch=None):
    w = m.w
    with ExitStack() as own:
        def sb(n, shape, dt=F32):
            return own.enter_context(nc.sbuf_tensor(f"{name}_{n}", shape, dt))

        logits = sb("logits", [P, TILES, EXP])
        down = sb("lora_down", [P, TILES, ER])
        best = sb("best", [P, TILES])
        hot = sb("hot", [P, TILES, EXP])
        order = sb("order", [P, EXP])
        downt = sb("lora_down_t", [ER, TOK])
        h = sb("h", [P, 2, FT, BANK])
        k = sems(nc, own, "order g ev st hot dt dtc hp h o x", f"{name}_")
        ps = m.ps

        def xt(c0, n):
            return m.xt[:, c0 // SEQ, PAD + c0 % SEQ:PAD + c0 % SEQ + n]

        with nc.Block() as block:
            if prefetch:
                @block.sync
                def _(sp):
                    prefetch(sp)

            @block.gpsimd
            def _(pool):
                nc.gpsimd.iota(order[:], [[-1, EXP]], base=EXP, channel_multiplier=0,
                               allow_small_or_imprecise_dtypes=True).then_inc(k["order"], 1)
                nc.gpsimd.tensor_tensor(m.x[:], m.x[:], w.wo_b[:].rearrange("p (a d) -> p a d", a=1)
                                        .to_broadcast([P, TILES, DIM]), ALU.add).then_inc(k["order"], 1)

            def second(pe, g):
                pe.wait_ge(k["h"], FT * (g + 1))
                if g >= 2:
                    pe.wait_ge(k["x"], g - 1)
                for t in range(GT):
                    for f in range(FT):
                        ins = nc.tensor.matmul(ps[:, 6 + g % 2, t * P:(t + 1) * P], h[:, g % 2, f, t * P:(t + 1) * P],
                                               w.wo[:, f, :], start=(t == 0 and f == 0), stop=(f == FT - 1),
                                               skip_group_check=True)
                ins.then_inc(k["o"], 1)

            @block.tensor
            def _(pe):
                for t in range(TILES):
                    ins = nc.tensor.matmul(ps[:, t // 8, (t % 8) * 64:(t % 8) * 64 + EXP + ER], xt(t * P, P), w.gate[:],
                                           start=(t % 8 == 0), stop=True, skip_group_check=True)
                ins.then_inc(k["g"], 1)
                pe.wait_ge(k["hot"], 1)
                for t in range(TILES):
                    ins = nc.tensor.transpose(ps[0:ER, 2 + t // 4, (t % 4) * P:(t % 4 + 1) * P], down[:, t, :], m.ident[:])
                ins.then_inc(k["dt"], 1)
                pe.wait_ge(k["dtc"], 1)
                for g in range(GROUPS):
                    for f in range(FT):
                        n = g * FT + f
                        if n >= 3:
                            pe.wait_ge(k["h"], n - 2)
                        bank = 2 + n % 3
                        nc.tensor.matmul(ps[:, bank, :], w.wi[:, f * P:(f + 1) * P],
                                         m.xt[:, 2 * g:2 * g + 2, PAD:], start=True, stop=False)
                        nc.tensor.matmul(ps[:, bank, :], w.lora_b[:, f * P:(f + 1) * P],
                                         downt[:, g * BANK:(g + 1) * BANK], start=False,
                                         stop=True).then_inc(k["hp"], 1)
                    if g:
                        second(pe, g - 1)
                second(pe, GROUPS - 1)

            @block.scalar
            def _(act):
                act.wait_ge(k["dt"], 1)
                nc.scalar.activation(downt[:], ps[0:ER, 2:6, :].rearrange("p a b -> p (a b)"),
                                     ACT.Copy).then_inc(k["dtc"], 1)
                for g in range(GROUPS):
                    for f in range(FT):
                        n = g * FT + f
                        act.wait_ge(k["hp"], n + 1)
                        if g >= 2 and f == 0:
                            act.wait_ge(k["o"], g - 1)
                        nc.scalar.activation(h[:, g % 2, f, :], ps[:, 2 + n % 3, :], ACT.Relu,
                                             bias=w.wi_b[:, f:f + 1]).then_inc(k["h"], 1)

            def first_of_max(nc, dve, m, k, logits, best, hot, order, ps, bias):
                dve.wait_ge(k["g"], 1)
                both = ps[:, 0:2, :].rearrange("p a (t e) -> p (a t) e", e=64)
                nc.vector.tensor_copy(down[:], both[:, :, EXP:EXP + ER])
                nc.vector.tensor_tensor(logits[:], both[:, :, 0:EXP],
                                        bias[:].rearrange("p (a e) -> p a e", a=1).to_broadcast([P, TILES, EXP]),
                                        ALU.add).then_inc(k["st"], 1)
                pick_first(nc, dve, k["st"], 1, k["order"], logits, best, hot, order)

            @block.vector
            def _(dve):
                first_of_max(nc, dve, m, k, logits, best, hot, order, ps, w.gate_b)
                nc.vector.tensor_tensor(
                    down[:].rearrange("p t (e r) -> p t e r", e=EXP), down[:].rearrange("p t (e r) -> p t e r", e=EXP),
                    hot[:].rearrange("p t (e r) -> p t e r", r=1).to_broadcast([P, TILES, EXP, RANK]),
                    ALU.mult).then_inc(k["hot"], 1)
                dve.wait_ge(k["order"], 2)
                for g in range(GROUPS):
                    dve.wait_ge(k["o"], g + 1)
                    xg = m.x[:, g * GT:(g + 1) * GT, :].rearrange("p t d -> p (t d)")
                    nc.vector.tensor_tensor(xg, xg, ps[:, 6 + g % 2, :], ALU.add).then_inc(k["x"], 1)


def pick_first(nc, dve, step, n, order_ready, logits, best, hot, order):
    wide = [P, TILES, EXP]

    def over(t):
        return t[:].rearrange("p (t a) -> p t a", a=1).to_broadcast(wide)

    dve.wait_ge(step, n)
    nc.vector.tensor_reduce(best[:], logits[:], AX.X, ALU.max).then_inc(step, 1)
    dve.wait_ge(step, n + 1)
    nc.vector.tensor_tensor(hot[:], logits[:], over(best), ALU.is_equal).then_inc(step, 1)
    dve.wait_ge(step, n + 2)
    dve.wait_ge(order_ready, 1)
    nc.vector.tensor_tensor(hot[:], hot[:], order[:].rearrange("p (a e) -> p a e", a=1).to_broadcast(wide),
                            ALU.mult).then_inc(step, 1)
    dve.wait_ge(step, n + 3)
    nc.vector.tensor_reduce(best[:], hot[:], AX.X, ALU.max).then_inc(step, 1)
    dve.wait_ge(step, n + 4)
    nc.vector.tensor_tensor(hot[:], hot[:], over(best), ALU.is_equal).then_inc(step, 1)
    dve.wait_ge(step, n + 5)


def load_toeplitz(sp, m):
    n = DIM // TOEPLITZ_LOADS
    for c in range(TOEPLITZ_LOADS):
        src = bass.AP(m.kernel_dram.tensor, c * n * 2 * P, [[1, P], [2 * P, n], [1, P]])
        sp.dma_start(m.toeplitz[:, c * n:(c + 1) * n, :], src).then_inc(m.toeplitz_loaded, 16)


def long_conv(nc, m):
    w = m.w
    with ExitStack() as own:
        def sb(name, shape, dt=F32):
            return own.enter_context(nc.sbuf_tensor(name, shape, dt))

        ud = sb("lc_skip", [P, TILES, DIM])
        state = sb("lc_state", [LNST, DIM, BATCH])
        y = sb("lc_y", [P, TILES, DIM])
        back = sb("lc_reversed", [P, TILES, DIM])
        flip = sb("lc_flip", [P, P])
        k = sems(nc, own, "lc_fz lc_flip lc_bp lc_back lc_ud lc_hp lc_hc lc_yp lc_y lc_st lc_pow lc_z")
        ps = m.ps
        step = k["lc_st"]
        with nc.Block() as block:
            def row(w, i, tiles=TILES):
                return w.lc_rows[:, i:i + 1, :].to_broadcast([P, tiles, DIM])

            @block.gpsimd
            def _(pool):
                nc.gpsimd.memset(flip[:], 0.0).then_inc(k["lc_fz"], 1)
                pool.wait_ge(k["lc_fz"], 1)
                nc.gpsimd.affine_select(out=flip[:], in_=flip[:], compare_op=ALU.not_equal, fill=1.0, base=1 - P,
                                        pattern=[[1, P]], channel_multiplier=1).then_inc(k["lc_flip"], 1)
                nc.gpsimd.tensor_tensor(ud[:], m.xn[:], row(w, 0), ALU.mult).then_inc(k["lc_ud"], 1)
                pool.wait_ge(step, 7)
                nc.gpsimd.tensor_tensor(m.rstd[:], m.ve[:], m.mhalf[:], ALU.pow).then_inc(k["lc_pow"], 1)

            @block.tensor
            def _(pe):
                first = m.xn[:].rearrange("p (b h) d -> p h b d", h=2)[:, 0]
                for i in range(2):
                    ins = nc.tensor.matmul(ps[0:LNST, 4 + i, :], m.lc_powt[:], first[:, 4 * i:4 * i + 4, :], start=True, stop=True)
                ins.then_inc(k["lc_hp"], 1)
                pe.wait_ge(k["lc_flip"], 1)
                for g in range(GROUPS):
                    nc.tensor.matmul(ps[:, g, :], flip[:], m.xn[:, g * GT:(g + 1) * GT, :], start=True,
                                     stop=True).then_inc(k["lc_bp"], 1)
                pe.wait_ge(m.toeplitz_loaded, 16 * TOEPLITZ_LOADS)
                pe.wait_ge(k["lc_back"], GROUPS)
                for d in range(DIM):
                    ins = nc.tensor.matmul(ps[:, d // 32, (d % 32) * TILES:(d % 32 + 1) * TILES], m.toeplitz[:, d, :],
                                           back[:, :, d], start=(d % 32 == 0), stop=False, skip_group_check=True)
                pe.wait_ge(k["lc_hc"], 1)
                for q in range(4):
                    out = ps[:, q, :].rearrange("p (d b h) -> p d b h", b=BATCH, h=2)[:, :, :, 1]
                    ins = nc.tensor.matmul(out, m.lc_pow[:, 1:], state[:, 32 * q:32 * q + 32, :], start=False,
                                           stop=True, skip_group_check=True)
                ins.then_inc(k["lc_yp"], 1)

            @block.scalar
            def _(act):
                for g in range(GROUPS):
                    act.wait_ge(k["lc_bp"], g + 1)
                    nc.scalar.activation(back[:, g * GT:(g + 1) * GT, :].rearrange("p t d -> p (t d)"), ps[:, g, :],
                                         ACT.Copy).then_inc(k["lc_back"], 1)

            @block.vector
            def _(dve):
                dve.wait_ge(k["lc_hp"], 1)
                src = ps[0:LNST, 4:6, :].rearrange("n a (b d) -> n d (a b)", b=4)
                nc.vector.tensor_tensor(state[:], src, w.lc_ct[:].rearrange("n (d a) -> n d a", a=1)
                                        .to_broadcast([LNST, DIM, BATCH]), ALU.mult).then_inc(k["lc_hc"], 1)
                dve.wait_ge(k["lc_ud"], 1)
                dve.wait_ge(k["lc_yp"], 1)
                for q in range(4):
                    ins = nc.vector.tensor_tensor(
                        y[:, :, 32 * q:32 * q + 32], ps[:, q, :].rearrange("p (d t) -> p t d", t=TILES),
                        ud[:, :, 32 * q:32 * q + 32], ALU.add)
                ins.then_inc(step, 1)
                dve.wait_ge(step, 1)
                nc.vector.tensor_tensor(y[:], y[:], row(w, 1), ALU.mult).then_inc(step, 1)
                dve.wait_ge(step, 2)
                y0 = y[0:1].rearrange("p (b h) d -> p h b d", h=2)[:, 0]
                nc.vector.tensor_tensor(y0, y0, w.lc_rows[0:1, 2:3, :].to_broadcast([1, BATCH, DIM]),
                                        ALU.add).then_inc(step, 1)
                dve.wait_ge(step, 3)
                for t in range(TILES):
                    ins = nc.vector.bn_stats(m.stats[:, t, :], y[:, t, :])
                ins.then_inc(step, 1)
                dve.wait_ge(step, 4)
                for t in range(TILES):
                    ins = nc.vector.bn_aggr(m.mv[:, t, :], m.stats[:, t, :])
                ins.then_inc(step, 1)
                dve.wait_ge(step, 5)
                nc.vector.tensor_scalar(m.ve[:], m.mv[:, :, 1], EPS, None, ALU.add).then_inc(step, 2)
                dve.wait_ge(k["lc_pow"], 1)
                for t in range(TILES):
                    ins = nc.vector.tensor_scalar(y[:, t, :], y[:, t, :], m.mv[:, t, 0:1], m.rstd[:, t:t + 1],
                                                  ALU.subtract, ALU.mult)
                ins.then_inc(step, 1)
                dve.wait_ge(step, 8)
                nc.vector.tensor_tensor(y[:], y[:], row(w, 3), ALU.mult).then_inc(step, 1)
                dve.wait_ge(step, 9)
                nc.vector.tensor_tensor(y[:], y[:], row(w, 4), ALU.add).then_inc(step, 1)
                dve.wait_ge(step, 10)
                nc.vector.tensor_tensor(m.x[:], m.x[:], y[:], ALU.add)


def attention(nc, m, name, a, rope):
    JS, GS = 4, HEADS // 4
    KT = SEQ // P
    SCALE = float(HD) ** -0.5
    MASKED = not rope
    with ExitStack() as own:
        def sb(n, shape, dt=F32):
            return own.enter_context(nc.sbuf_tensor(f"{name}_{n}", shape, dt))

        xb = sb("xb", [P, 2, SEQ])
        qr = sb("q", [P, SEQ])
        qm = sb("q_masked", [P, 2, JS, SEQ])
        kt = sb("k", [P, 2, SEQ])
        t1 = sb("rot1", [P, 2, SEQ])
        t2 = sb("rot2", [P, 2, SEQ])
        v = sb("v", [P, 2, KT, HEADS, 32])
        mx = sb("max", [P, KT, GS])
        res = sb("max_rest", [P, KT, GS])
        split = sb("max_split", [P, KT, 3, GS], BF16)
        mt = sb("max_t", [P, SEQ], BF16)
        e = sb("e", [P, 2, KT, GS, SEQ])
        rs = sb("rsum", [P, SEQ])
        on = sb("o", [P, JS, SEQ])
        k = sems(nc, own, "part vz bias xb qp kp vp qd kd qr kt qm v sq mx ms mtp mtc st ex pv rs nm out xa", f"{name}_")
        ps = m.ps
        SQ, ST, OB, MISC = (0, 1), (2, 4), 6, 7
        misc = ps[:, MISC, :]
        mtp = ps[0:3 * GS, MISC, 0:SEQ // 2].bitcast(BF16)

        def pe_q(pe, b, r):
            pe.wait_ge(k["xb"], b + 1)
            if rope:
                nc.tensor.matmul(misc[:, 0:SEQ], a.wq1[:], xb[:, r, :], start=True, stop=True)
                nc.tensor.matmul(misc[:, SEQ:], a.wq2[:], xb[:, r, :], start=False, stop=True,
                                 skip_group_check=True).then_inc(k["qp"], 1)
            else:
                nc.tensor.matmul(misc[:, 0:SEQ], a.wq1[:], xb[:, r, :], start=True, stop=True).then_inc(k["qp"], 1)

        def pe_k(pe, b, r):
            if rope:
                nc.tensor.matmul(misc[:, 0:SEQ], a.wk1[:], xb[:, r, :], start=True, stop=True)
                nc.tensor.matmul(misc[:, SEQ:], a.wk2[:], xb[:, r, :], start=False, stop=True,
                                 skip_group_check=True).then_inc(k["kp"], 1)
            else:
                nc.tensor.matmul(misc[:, 0:SEQ], a.wk1[:], xb[:, r, :], start=True, stop=True).then_inc(k["kp"], 1)

        def pe_v(pe, b, r):
            for i in range(KT):
                ins = nc.tensor.matmul(misc[:, i * P:(i + 1) * P], xb[:, r, i * P:(i + 1) * P], a.wv[:],
                                       start=(i == 0), stop=True, skip_group_check=True)
            ins.then_inc(k["vp"], 1)

        def pe_sq(pe, s, j, r):
            for i in range(4):
                qt, pair = i // 2, i % 2
                if not (isinstance(s, int) and s == 0 and i < 2):
                    pe.wait_ge(k["mx"], s * 4 + i - 1)
                bank = SQ[i % 2]
                if MASKED:
                    nc.tensor.matmul(ps[:, bank, :], m.identb[:],
                                     a.mask_q[:, qt:qt + 1, :].to_broadcast([P, 2, SEQ]), start=True, stop=False,
                                     skip_group_check=True)
                rows = slice(32 * j, 32 * j + 32)
                for c in range(2):
                    g = 2 * pair + c
                    ins = nc.tensor.matmul(ps[:, bank, c * SEQ:(c + 1) * SEQ], qm[rows, r, g, qt * P:(qt + 1) * P],
                                           kt[rows, r, :], start=(c == 0 and not MASKED), stop=True,
                                           skip_group_check=True)
                ins.then_inc(k["sq"], 1)

        def pe_mt(pe, s):
            pe.wait_ge(k["ms"], s + 1)
            for i in range(KT):
                ins = nc.tensor.transpose(mtp[:, i * P:(i + 1) * P], split[:, i, :, :].rearrange("p c g -> p (c g)"),
                                          m.identb[:])
            ins.then_inc(k["mtp"], 1)

        def pe_st(pe, s, j, r):
            pe.wait_ge(k["mtc"], s + 1)
            for i in range(KT):
                if not (isinstance(s, int) and s == 0):
                    pe.wait_ge(k["ex"], s * KT + i - 1)
                banks = ps[:, ST[i]:ST[i] + 2, :]
                if MASKED:
                    for c in range(2):
                        nc.tensor.matmul(banks[:, c, :], m.identb[:],
                                         a.mask_k[:, i:i + 1, :].to_broadcast([P, 2, SEQ]), start=True, stop=False,
                                         skip_group_check=True)
                for g in range(GS):
                    nc.tensor.matmul(banks[:, g // 2, (g % 2) * SEQ:(g % 2 + 1) * SEQ], a.pick[:, g, :], mt[:],
                                     start=(g % 2 == 0 and not MASKED), stop=False, skip_group_check=True)
                rows = slice(32 * j, 32 * j + 32)
                for g in range(GS):
                    ins = nc.tensor.matmul(banks[:, g // 2, (g % 2) * SEQ:(g % 2 + 1) * SEQ],
                                           kt[rows, r, i * P:(i + 1) * P], qm[rows, r, g, :], start=False, stop=True,
                                           skip_group_check=True)
                ins.then_inc(k["st"], 1)

        def pe_pv(pe, s, j, r):
            if not (isinstance(s, int) and s == 0):
                pe.wait_ge(k["nm"], s)
            for i in range(KT):
                pe.wait_ge(k["ex"], s * KT + i + 1)
                for part in range(2):
                    for g in range(GS):
                        lhs = v[:, r, i, 4 * j + g, :] if part == 0 else m.ones[:, 0:32]
                        ins = nc.tensor.matmul(ps[32 * g:32 * g + 32, OB, part * SEQ:(part + 1) * SEQ], lhs,
                                               e[:, j % 2, i, g, :], start=(i == 0 and part == 0),
                                               stop=(i == KT - 1), skip_group_check=True)
            ins.then_inc(k["pv"], 1)

        def pe_out(pe, b):
            pe.wait_ge(k["nm"], b * JS + JS)
            for i in range(KT):
                for j in range(JS):
                    ins = nc.tensor.matmul(misc[:, i * P:(i + 1) * P], on[:, j, i * P:(i + 1) * P], a.wo[:, j, :],
                                           start=(i == 0 and j == 0), stop=(j == JS - 1), skip_group_check=True)
            ins.then_inc(k["out"], 1)

        def pe_batch(pe, b, r, first, last):
            for j in range(JS):
                s = b * JS + j
                if j == 1 and not first:
                    pe.wait_ge(k["mtc"], s + 1)
                    pe_out(pe, b - 1)
                if j == 3 and not last:
                    pe.wait_ge(k["kd"], b + 2)
                    pe_v(pe, b + 1, 1 - r)
                more = not (last and j == 3)
                if more:
                    if j == 3:
                        pe.wait_ge(k["qm"], b + 2)
                        pe.wait_ge(k["kt" if rope else "kd"], b + 2)
                        pe_sq(pe, s + 1, 0, 1 - r)
                    else:
                        pe_sq(pe, s + 1, j + 1, r)
                pe_st(pe, s, j, r)
                if not (first and j == 0):
                    if j == 0:
                        pe_pv(pe, s - 1, 3, 1 - r)
                    else:
                        if j == 1:
                            pe.wait_ge(k["v"], b + 1)
                        pe_pv(pe, s - 1, j - 1, r)
                if more:
                    if j == 0:
                        pe.wait_ge(k["mtc"], s + 1)
                    if j == 1 and not first:
                        pe.wait_ge(k["xa"], b)
                    if j == 1 and first:
                        pe.wait_ge(k["mtc"], s + 1)
                    if j == 2:
                        pe.wait_ge(k["qd"], b + 2) if not last else pe.wait_ge(k["mtc"], s + 1)
                    if j == 3:
                        pe.wait_ge(k["v"], b + 2)
                    pe_mt(pe, s + 1)
                if not last and j in (1, 2):
                    pe.wait_ge(k["mtc"], s + 2)
                    (pe_q if j == 1 else pe_k)(pe, b + 1, 1 - r)

        def dve_q(dve, b, r):
            pe_sem = k["qp"]
            dve.wait_ge(pe_sem, b + 1)
            if rope:
                if not (isinstance(b, int) and b == 0):
                    dve.wait_ge(k["qr"], b)
                nc.vector.tensor_tensor(t1[:, 0, :], misc[:, 0:SEQ], a.cos[:], ALU.mult)
                nc.vector.tensor_tensor(t2[:, 0, :], misc[:, SEQ:], a.sin[:], ALU.mult).then_inc(k["qd"], 1)
            else:
                if not (isinstance(b, int) and b == 0):
                    dve.wait_ge(k["qm"], b)
                nc.vector.tensor_scalar(qr[:], misc[:, 0:SEQ], a.bq[:, 0:1], None, ALU.add).then_inc(k["qd"], 1)

        def dve_k(dve, b, r):
            dve.wait_ge(k["kp"], b + 1)
            if rope:
                if not (isinstance(b, int) and b == 0):
                    dve.wait_ge(k["kt"], b)
                nc.vector.tensor_tensor(t1[:, 1, :], misc[:, 0:SEQ], a.cos[:], ALU.mult)
                nc.vector.tensor_tensor(t2[:, 1, :], misc[:, SEQ:], a.sin[:], ALU.mult).then_inc(k["kd"], 1)
            else:
                if not (isinstance(b, int) and b <= 1):
                    dve.wait_ge(k["st"], (b - 1) * JS * KT)
                nc.vector.tensor_copy(kt[:, r, :], misc[:, 0:SEQ]).then_inc(k["kd"], 1)

        def dve_max(dve, s):
            for i in range(4):
                qt, pair = i // 2, i % 2
                dve.wait_ge(k["sq"], s * 4 + i + 1)
                if i == 0 and not (isinstance(s, int) and s == 0):
                    dve.wait_ge(k["ms"], s)
                nc.vector.tensor_reduce(mx[:, qt, 2 * pair:2 * pair + 2],
                                        ps[:, SQ[i % 2], :].rearrange("p (c t) -> p c t", c=2), AX.X,
                                        ALU.max).then_inc(k["mx"], 1)
            if not (isinstance(s, int) and s == 0):
                dve.wait_ge(k["mtp"], s)
            dve.wait_ge(k["mx"], s * 4 + 4)
            nc.vector.tensor_scalar(split[:, :, 0, :], mx[:], -1.0, None, ALU.mult).then_inc(k["part"], 1)
            dve.wait_ge(k["part"], s * 3 + 1)
            nc.vector.scalar_tensor_tensor(out=res[:], in0=mx[:], scalar=-1.0, in1=split[:, :, 0, :], op0=ALU.mult,
                                           op1=ALU.subtract).then_inc(k["part"], 1)
            dve.wait_ge(k["part"], s * 3 + 2)
            nc.vector.tensor_copy(split[:, :, 1, :], res[:]).then_inc(k["part"], 1)
            dve.wait_ge(k["part"], s * 3 + 3)
            nc.vector.tensor_tensor(split[:, :, 2, :], res[:], split[:, :, 1, :], ALU.subtract)\
                .then_inc(k["ms"], 1)

        def dve_norm(dve, s, j):
            dve.wait_ge(k["pv"], s + 1)
            nc.vector.reciprocal(rs[:], ps[:, OB, SEQ:]).then_inc(k["rs"], 1)
            dve.wait_ge(k["rs"], s + 1)
            nc.vector.tensor_tensor(on[:, j, :], ps[:, OB, 0:SEQ], rs[:], ALU.mult).then_inc(k["nm"], 1)

        def dve_add(dve, b):
            dve.wait_ge(k["out"], b + 1)
            dve.wait_ge(k["bias"], 1)
            xs = m.x[:, bass.ds(b * 2, 2), :] if not isinstance(b, int) else m.x[:, 2 * b:2 * b + 2, :]
            nc.vector.tensor_tensor(xs, xs, misc[:, 0:SEQ].rearrange("p (t d) -> p t d", t=2),
                                    ALU.add).then_inc(k["xa"], 1)

        def dve_batch(dve, b, first, last, r):
            for j in range(JS):
                s = b * JS + j
                if j == 1 and not first:
                    dve_add(dve, b - 1)
                if j == 3 and not last:
                    dve_v(dve, b + 1, 1 - r)
                if not (last and j == 3):
                    dve_max(dve, s + 1)
                if not (first and j == 0):
                    dve_norm(dve, s - 1, (j - 1) % JS)
                if not last and j == 1:
                    dve_q(dve, b + 1, 1 - r)
                if not last and j == 2:
                    dve_k(dve, b + 1, 1 - r)

        def act_mt(act, s):
            act.wait_ge(k["mtp"], s + 1)
            nc.scalar.activation(mt[0:3 * GS, :], mtp, ACT.Copy).then_inc(k["mtc"], 1)

        def act_qm(act, b, r):
            act.wait_ge(k["qr"] if rope else k["qd"], b + 1)
            if not (isinstance(b, int) and b <= 1):
                act.wait_ge(k["st"], (b - 1) * JS * KT)
            for j in range(JS):
                ins = nc.scalar.activation(qm[:, r, j, :], qr[:], ACT.Copy, scale=a.head_mask[:, j:j + 1])
            ins.then_inc(k["qm"], 1)

        def dve_v(dve, b, r):
            if rope:
                return
            dve.wait_ge(k["vp"], b + 1)
            if not (isinstance(b, int) and b <= 1):
                dve.wait_ge(k["pv"], (b - 1) * JS)
            for i in range(KT):
                ins = nc.vector.tensor_tensor(
                    v[:, r, i, :, 0:HD], misc[:, i * P:(i + 1) * P].rearrange("p (h e) -> p h e", e=HD),
                    a.bv[:].rearrange("p (h e) -> p h e", e=HD), ALU.add)
            ins.then_inc(k["v"], 1)

        def act_v(act, b, r):
            if not rope:
                return
            act.wait_ge(k["vp"], b + 1)
            if not (isinstance(b, int) and b <= 1):
                act.wait_ge(k["pv"], (b - 1) * JS)
            nc.scalar.activation(v[:, r, :, :, 0:HD], misc[:, 0:SEQ].rearrange("p (i h e) -> p i h e", i=KT, e=HD),
                                 ACT.Copy).then_inc(k["v"], 1)

        def act_exp(act, s, j):
            for i in range(KT):
                act.wait_ge(k["st"], s * KT + i + 1)
                if i == 0 and not (isinstance(s, int) and s <= 1):
                    act.wait_ge(k["pv"], s - 1)
                nc.scalar.activation(e[:, j % 2, i, :, :].rearrange("p g t -> p (g t)"),
                                     ps[:, ST[i]:ST[i] + 2, :].rearrange("p a b -> p (a b)"), ACT.Exp,
                                     scale=SCALE).then_inc(k["ex"], 1)

        def act_batch(act, b, last, r):
            for j in range(JS):
                s = b * JS + j
                if j == 3 and not last:
                    act_v(act, b + 1, 1 - r)
                act_exp(act, s, j)
                if not (last and j == 3):
                    act_mt(act, s + 1)
                if j == 2 and not last:
                    act_qm(act, b + 1, 1 - r)

        def pool_xb(pool, b, r):
            if not (isinstance(b, int) and b <= 1):
                pool.wait_ge(k["vp"], b - 1)
            src = m.xt[:, b, PAD:] if isinstance(b, int) else \
                m.xt[:, bass.ds(b, 1), PAD:].rearrange("p a t -> p (a t)")
            nc.gpsimd.tensor_copy(xb[:, r, :], src).then_inc(k["xb"], 1)

        def pool_rot(pool, b, r):
            if not rope:
                return
            pool.wait_ge(k["qd"], b + 1)
            if not (isinstance(b, int) and b == 0):
                pool.wait_ge(k["qm"], b)
            nc.gpsimd.tensor_tensor(qr[:], t1[:, 0, :], t2[:, 0, :], ALU.add).then_inc(k["qr"], 1)
            pool.wait_ge(k["kd"], b + 1)
            if not (isinstance(b, int) and b <= 1):
                pool.wait_ge(k["st"], (b - 1) * JS * KT)
            nc.gpsimd.tensor_tensor(kt[:, r, :], t1[:, 1, :], t2[:, 1, :], ALU.add).then_inc(k["kt"], 1)

        PAIRS = (BATCH - 2) // 2
        with nc.Block() as block:
            @block.tensor
            def _(pe):
                pe_q(pe, 0, 0)
                pe.wait_ge(k["qd"], 1)
                pe_k(pe, 0, 0)
                pe.wait_ge(k["kd"], 1)
                pe_v(pe, 0, 0)
                pe.wait_ge(k["qm"], 1)
                pe.wait_ge(k["kt" if rope else "kd"], 1)
                pe_sq(pe, 0, 0, 0)
                pe.wait_ge(k["v"], 1)
                pe_mt(pe, 0)
                pe_batch(pe, 0, 0, True, False)
                with pe.Fori(0, PAIRS) as pair:
                    pe_batch(pe, pair * 2 + 1, 1, False, False)
                    pe_batch(pe, pair * 2 + 2, 0, False, False)
                pe_batch(pe, BATCH - 1, 1, False, True)
                pe_pv(pe, BATCH * JS - 1, JS - 1, 1)
                pe_out(pe, BATCH - 1)

            @block.vector
            def _(dve):
                nc.vector.memset(mt[:], 0.0)
                nc.vector.memset(v[:], 0.0).then_inc(k["vz"], 1)
                dve_q(dve, 0, 0)
                dve_k(dve, 0, 0)
                dve.wait_ge(k["vz"], 1)
                dve_v(dve, 0, 0)
                dve_max(dve, 0)
                dve_batch(dve, 0, True, False, 0)
                with dve.Fori(0, PAIRS) as pair:
                    dve_batch(dve, pair * 2 + 1, False, False, 1)
                    dve_batch(dve, pair * 2 + 2, False, False, 0)
                dve_batch(dve, BATCH - 1, False, True, 1)
                dve_norm(dve, BATCH * JS - 1, JS - 1)
                dve_add(dve, BATCH - 1)

            @block.scalar
            def _(act):
                act_qm(act, 0, 0)
                act.wait_ge(k["vz"], 1)
                act_v(act, 0, 0)
                act_mt(act, 0)
                act_batch(act, 0, False, 0)
                with act.Fori(0, PAIRS) as pair:
                    act_batch(act, pair * 2 + 1, False, 1)
                    act_batch(act, pair * 2 + 2, False, 0)
                act_batch(act, BATCH - 1, True, 1)

            @block.gpsimd
            def _(pool):
                pool_xb(pool, 0, 0)
                pool_rot(pool, 0, 0)
                nc.gpsimd.tensor_tensor(m.x[:], m.x[:], a.bo[:].rearrange("p (a d) -> p a d", a=1)
                                        .to_broadcast([P, TILES, DIM]), ALU.add).then_inc(k["bias"], 1)
                pool_xb(pool, 1, 1)
                pool_rot(pool, 1, 1)
                with pool.Fori(0, PAIRS) as pair:
                    pool_xb(pool, pair * 2 + 2, 0)
                    pool_rot(pool, pair * 2 + 2, 0)
                    pool_xb(pool, pair * 2 + 3, 1)
                    pool_rot(pool, pair * 2 + 3, 1)


def batch_attention(nc, m, name):
    w = m.w
    SCALE = float(MHD) ** -0.5
    with ExitStack() as own:
        def sb(n, shape, dt=F32):
            return own.enter_context(nc.sbuf_tensor(f"{name}_{n}", shape, dt))

        qt = sb("q_t", [P, BATCH, SEQ])
        km = sb("k_t", [P, MH, BATCH, SEQ])
        kb = sb("k_bias", [P, MH])
        ot = sb("o_t", [P, BATCH, SEQ])
        xg = sb("x_group", [P, 2, P])
        qg = sb("q_group", [P, 2, P])
        v = sb("v", [P, 2, P])
        nb = sb("neg_max", [P, 2, MH])
        sums = sb("sums", [P, 2, MH])
        rec = sb("rec", [P, 2, MH])
        pr = sb("probs", [P, 2, MH, P])
        pt = sb("probs_t", [P, 2, MH, P])
        y = m.xn
        k = sems(nc, own, "qp qe kb cp sc vp ve mx nb ex rc nr tp tc pv oe pr r1 st pw nn yt rs gb", f"{name}_")
        ps = m.ps
        SC, VB, PT, OT = 0, 2, 4, 6

        def cols(t, g):
            if isinstance(g, int):
                return t[:, :, g * PG:(g + 1) * PG]
            return t[:, :, bass.ds(g * PG, PG)]

        def pool_copy(pool, g, r):
            if not (isinstance(g, int) and g <= 1):
                pool.wait_ge(k["sc"], g - 1)
            for dst, src in ((xg, m.xt[:, :, PAD:]), (qg, qt)):
                ins = nc.gpsimd.tensor_copy(dst[:, r, :].rearrange("p (b t) -> p b t", b=BATCH), cols(src, g))
            ins.then_inc(k["cp"], 1)

        def pe_scores(pe, g, r):
            pe.wait_ge(k["cp"], g + 1)
            if not (isinstance(g, int) and g <= 1):
                pe.wait_ge(k["ve"], g - 1)
                pe.wait_ge(k["ex"], g - 1)
            nc.tensor.matmul(ps[:, VB + r, 0:P], xg[:, r, :], w.m_v[:], start=True, stop=True).then_inc(k["vp"], 1)
            nc.tensor.matmul(ps[:, SC + r, :], m.identb[:], w.m_mask[:].rearrange("p (a c) -> p a c", a=1)
                             .to_broadcast([P, MH, P]), start=True, stop=False, skip_group_check=True)
            keys = km[:, :, :, g * PG:(g + 1) * PG] if isinstance(g, int) else km[:, :, :, bass.ds(g * PG, PG)]
            nc.tensor.matmul(ps[:, SC + r, :], qg[:, r, :], keys, start=False, stop=True,
                             skip_group_check=True).then_inc(k["sc"], 1)

        def pe_turn(pe, g, r):
            pe.wait_ge(k["nr"], g + 1)
            if not (isinstance(g, int) and g <= 1):
                pe.wait_ge(k["tc"], g - 1)
            for h in range(MH):
                ins = nc.tensor.transpose(ps[:, PT + r, h * P:(h + 1) * P], pr[:, r, h, :], m.ident[:])
            ins.then_inc(k["tp"], 1)

        def pe_pv(pe, g, r):
            pe.wait_ge(k["tc"], g + 1)
            pe.wait_ge(k["ve"], g + 1)
            pe.wait_ge(k["oe"], g + 1)
            for h in range(MH):
                ins = nc.tensor.matmul(ps[MHD * h:MHD * (h + 1), OT + r, 0:P], v[:, r, MHD * h:MHD * (h + 1)],
                                       pt[:, r, h, :], start=True, stop=True)
            ins.then_inc(k["pv"], 1)

        def pe_step(pe, g, r, first, last):
            if not last:
                pe_scores(pe, g + 1, 1 - r)
            if not first:
                pe_pv(pe, g - 1, 1 - r)
            pe_turn(pe, g, r)

        def dve_max(dve, g, r):
            dve.wait_ge(k["sc"], g + 1)
            if not (isinstance(g, int) and g <= 1):
                dve.wait_ge(k["ex"], g - 1)
            nc.vector.tensor_reduce(nb[:, r, :], ps[:, SC + r, :].rearrange("p (h t) -> p h t", h=MH), AX.X,
                                    ALU.max).then_inc(k["mx"], 1)
            dve.wait_ge(k["mx"], g + 1)
            nc.vector.tensor_scalar(nb[:, r, :], nb[:, r, :], -SCALE, None, ALU.mult).then_inc(k["nb"], 1)

        def dve_norm(dve, g, r):
            dve.wait_ge(k["ex"], g + 1)
            nc.vector.reciprocal(rec[:, r, :], sums[:, r, :]).then_inc(k["rc"], 1)
            dve.wait_ge(k["rc"], g + 1)
            nc.vector.tensor_tensor(pr[:, r], pr[:, r], rec[:, r, :].rearrange("p (h a) -> p h a", a=1)
                                    .to_broadcast([P, MH, P]), ALU.mult).then_inc(k["nr"], 1)

        def dve_step(dve, g, r, last):
            if not last:
                dve_max(dve, g + 1, 1 - r)
            dve_norm(dve, g, r)

        def act_exp(act, g, r):
            act.wait_ge(k["nb"], g + 1)
            if not (isinstance(g, int) and g <= 1):
                act.wait_ge(k["tp"], g - 1)
            for h in range(MH):
                ins = nc.scalar.activation(pr[:, r, h, :], ps[:, SC + r, h * P:(h + 1) * P], ACT.Exp,
                                           bias=nb[:, r, h:h + 1], scale=SCALE, accum_out=sums[:, r, h:h + 1])
            ins.then_inc(k["ex"], 1)

        def act_v(act, g, r):
            act.wait_ge(k["vp"], g + 1)
            if not (isinstance(g, int) and g <= 1):
                act.wait_ge(k["pv"], g - 1)
            nc.scalar.activation(v[:, r, :], ps[:, VB + r, 0:P], ACT.Copy).then_inc(k["ve"], 1)

        def act_turn(act, g, r):
            act.wait_ge(k["tp"], g + 1)
            if not (isinstance(g, int) and g <= 1):
                act.wait_ge(k["pv"], g - 1)
            nc.scalar.activation(pt[:, r].rearrange("p h t -> p (h t)"), ps[:, PT + r, :], ACT.Copy)\
                .then_inc(k["tc"], 1)

        def act_out(act, g, r):
            act.wait_ge(k["pv"], g + 1)
            act.wait_ge(k["qe"], 2 * GROUPS)
            nc.scalar.activation(cols(ot, g), ps[:, OT + r, 0:P].rearrange("p (b t) -> p b t", b=BATCH), ACT.Identity,
                                 bias=w.m_bqkv[:, 2:3]).then_inc(k["oe"], 1)

        def act_step(act, g, r, first, last):
            if not last:
                act_v(act, g + 1, 1 - r)
                act_exp(act, g + 1, 1 - r)
            if not first:
                act_out(act, g - 1, 1 - r)
            act_turn(act, g, r)

        LOOPS = (NPG - 2) // 2
        
        with nc.Block() as block:
            @block.tensor
            def _(pe):
                for i, wt in enumerate((w.m_q, w.m_k)):
                    for g in range(GROUPS):
                        nc.tensor.matmul(ps[:, 4 * i + g, :], wt[:], m.xt[:, 2 * g:2 * g + 2, PAD:], start=True,
                                         stop=True).then_inc(k["qp"], 1)
                pe.wait_ge(k["qe"], 2 * GROUPS)
                pe_scores(pe, 0, 0)
                pe_step(pe, 0, 0, True, False)
                with pe.Fori(0, LOOPS) as i:
                    pe_step(pe, i * 2 + 1, 1, False, False)
                    pe_step(pe, i * 2 + 2, 0, False, False)
                pe_step(pe, NPG - 1, 1, False, True)
                pe_pv(pe, NPG - 1, 1)
                pe.wait_ge(k["oe"], NPG + 2)
                for t in range(TILES):
                    ins = nc.tensor.matmul(ps[:, t // GT, (t % GT) * P:(t % GT + 1) * P],
                                           ot[:, t // 2, (t % 2) * P:(t % 2 + 1) * P], w.m_o[:], start=(t % GT == 0),
                                           stop=True, skip_group_check=True)
                    if t % GT == GT - 1:
                        ins.then_inc(k["pr"], 1)
                for g in range(GROUPS):
                    pe.wait_ge(k["nn"], g + 1)
                    for t in range(GT):
                        ins = nc.tensor.transpose(ps[:, 4 + g, t * P:(t + 1) * P], y[:, g * GT + t, :], m.ident[:])
                    ins.then_inc(k["yt"], 1)

            @block.vector
            def _(dve):
                nc.vector.tensor_tensor(kb[:], w.head_rows[:], w.m_bqkv[:, 1:2].to_broadcast([P, MH]),
                                        ALU.mult).then_inc(k["kb"], 1)
                dve_max(dve, 0, 0)
                dve_step(dve, 0, 0, False)
                with dve.Fori(0, LOOPS) as i:
                    dve_step(dve, i * 2 + 1, 1, False)
                    dve_step(dve, i * 2 + 2, 0, False)
                dve_step(dve, NPG - 1, 1, True)
                dve.wait_ge(k["rs"], 1)
                for g in range(GROUPS):
                    dve.wait_ge(k["pr"], g + 1)
                    yg = y[:, g * GT:(g + 1) * GT, :].rearrange("p t d -> p (t d)")
                    nc.vector.tensor_tensor(yg, yg, ps[:, g, :], ALU.add).then_inc(k["r1"], 1)
                normalise(nc, dve, m, y, k["st"], k["pw"], [(k["r1"], GROUPS)])
                for g in range(GROUPS):
                    for t in range(g * GT, (g + 1) * GT):
                        ins = nc.vector.tensor_scalar(y[:, t, :], y[:, t, :], m.mv[:, t, 0:1], m.rstd[:, t:t + 1],
                                                      ALU.subtract, ALU.mult)
                    ins.then_inc(k["nn"], 1)

            @block.scalar
            def _(act):
                for g in range(GROUPS):
                    act.wait_ge(k["qp"], g + 1)
                    nc.scalar.activation(qt[:, 2 * g:2 * g + 2, :], ps[:, g, :].rearrange("p (b t) -> p b t", b=2),
                                         ACT.Identity, bias=w.m_bqkv[:, 0:1]).then_inc(k["qe"], 1)
                act.wait_ge(k["kb"], 1)
                for g in range(GROUPS):
                    act.wait_ge(k["qp"], GROUPS + g + 1)
                    for h in range(MH):
                        ins = nc.scalar.activation(km[:, h, 2 * g:2 * g + 2, :],
                                                   ps[:, 4 + g, :].rearrange("p (b t) -> p b t", b=2), ACT.Identity,
                                                   bias=kb[:, h:h + 1], scale=w.head_rows[:, h:h + 1])
                    ins.then_inc(k["qe"], 1)
                act.sem_inc(k["oe"], 2)
                act_v(act, 0, 0)
                act_exp(act, 0, 0)
                act_step(act, 0, 0, True, False)
                with act.Fori(0, LOOPS) as i:
                    act_step(act, i * 2 + 1, 1, False, False)
                    act_step(act, i * 2 + 2, 0, False, False)
                act_step(act, NPG - 1, 1, False, True)
                act_out(act, NPG - 1, 1)
                for g in range(GROUPS):
                    act.wait_ge(k["yt"], g + 1)
                    nc.scalar.activation(m.xt[:, 2 * g:2 * g + 2, PAD:],
                                         ps[:, 4 + g, :].rearrange("p (b t) -> p b t", b=2), ACT.Identity,
                                         scale=w.m_gb[:, 0:1], bias=w.m_gb[:, 1:2])

            @block.gpsimd
            def _(pool):
                pool.wait_ge(k["qe"], 2 * GROUPS)
                pool_copy(pool, 0, 0)
                pool_copy(pool, 1, 1)
                with pool.Fori(0, LOOPS) as i:
                    pool_copy(pool, i * 2 + 2, 0)
                    pool_copy(pool, i * 2 + 3, 1)
                nc.gpsimd.tensor_tensor(y[:], y[:], w.m_rows[:, 0:1, :].to_broadcast([P, TILES, DIM]),
                                        ALU.add).then_inc(k["rs"], 1)
                pool.wait_ge(k["st"], 3)
                nc.gpsimd.tensor_tensor(m.rstd[:], m.ve[:], m.mhalf[:], ALU.pow).then_inc(k["pw"], 1)
                pool.wait_ge(k["yt"], GROUPS)
                nc.gpsimd.tensor_tensor(y[:], y[:], w.m_rows[:, 1:2, :].to_broadcast([P, TILES, DIM]),
                                        ALU.mult).then_inc(k["gb"], 1)
                pool.wait_ge(k["gb"], 1)
                nc.gpsimd.tensor_tensor(y[:], y[:], w.m_rows[:, 2:3, :].to_broadcast([P, TILES, DIM]), ALU.add)


def normalise(nc, dve, m, src, step, power, ready):
    for s, n in ready:
        dve.wait_ge(s, n)
    for t in range(TILES):
        ins = nc.vector.bn_stats(m.stats[:, t, :], src[:, t, :])
    ins.then_inc(step, 1)
    dve.wait_ge(step, 1)
    for t in range(TILES):
        ins = nc.vector.bn_aggr(m.mv[:, t, :], m.stats[:, t, :])
    ins.then_inc(step, 1)
    dve.wait_ge(step, 2)
    nc.vector.tensor_scalar(m.ve[:], m.mv[:, :, 1], EPS, None, ALU.add).then_inc(step, 1)
    dve.wait_ge(power, 1)


def experts(nc, m, name, dram):
    w = m.w
    with ExitStack() as own:
        def sb(n, shape, dt=F32):
            return own.enter_context(nc.sbuf_tensor(f"{name}_{n}", shape, dt))

        w1 = sb("w1", [P, 2, FF])
        w2 = sb("w2", [P, 2, FT, DIM])
        b1 = sb("b1", [P, 2, FT])
        b2 = sb("b2", [EXP, DIM])
        logits = sb("logits", [P, TILES, EXP])
        best = sb("best", [P, TILES])
        hot = sb("hot", [P, TILES, EXP])
        hott = sb("hot_t", [EXP, TOK])
        order = sb("order", [P, EXP])
        h = sb("h", [P, 2, FT, BANK])
        y = m.xn
        k = sems(nc, own, "w_even w_odd b order lg st hp ht hc bp bd hid h o acc pw nn g2", f"{name}_")
        loaded = (k["w_even"], k["w_odd"])
        ps = m.ps
        NH = GROUPS * FT

        def pe_hidden(pe, e, r, g):
            for f in range(FT):
                n = g * FT + f
                pe.wait_ge(k["h"], e * NH + (n + 1))
                nc.tensor.matmul(ps[:, n % 4, :], w1[:, r, f * P:(f + 1) * P], m.xt[:, 2 * g:2 * g + 2, PAD:],
                                 start=True, stop=True).then_inc(k["hid"], 1)

        def pe_second(pe, e, r, g):
            pe.wait_ge(k["h"], e * NH + (g * FT + 4 + FT))
            pe.wait_ge(k["acc"], e * GROUPS + (g + 1))
            for t in range(GT):
                for f in range(FT):
                    ins = nc.tensor.matmul(ps[:, 4 + g % 2, t * P:(t + 1) * P], h[:, g % 2, f, t * P:(t + 1) * P],
                                           w2[:, r, f, :], start=(t == 0 and f == 0), stop=(f == FT - 1),
                                           skip_group_check=True)
            ins.then_inc(k["o"], 1)

        def pe_expert(pe, i, r):
            e = i * 2 + r
            pe.wait_ge(loaded[r], i * 48 + 48)
            for g in range(GROUPS):
                pe_hidden(pe, e, r, g)
                if g:
                    pe_second(pe, e, r, g - 1)
            pe_second(pe, e, r, GROUPS - 1)

        def act_expert(act, i, r):
            e = i * 2 + r
            act.wait_ge(loaded[r], i * 48 + 48)
            for g in range(GROUPS):
                for f in range(FT):
                    n = g * FT + f
                    act.wait_ge(k["hid"], e * NH + (n + 1))
                    if f == 0:
                        act.wait_ge(k["o"], e * GROUPS + (g + 1))
                    nc.scalar.activation(h[:, g % 2, f, :], ps[:, n % 4, :], ACT.Relu,
                                         bias=b1[:, r, f:f + 1]).then_inc(k["h"], 1)

        def dve_expert(dve, e):
            for g in range(GROUPS):
                dve.wait_ge(k["o"], e * GROUPS + (g + 3))
                for t in range(GT):
                    yt = y[:, g * GT + t, :]
                    pick = hot[:, g * GT + t, bass.ds(e, 1)]
                    ins = nc.vector.scalar_tensor_tensor(out=yt, in0=ps[:, 4 + g % 2, t * P:(t + 1) * P], scalar=pick,
                                                         in1=yt, op0=ALU.mult, op1=ALU.add)
                ins.then_inc(k["acc"], 1)

        with nc.Block() as block:
            @block.sync
            def _(sp):
                sp.dma_start(b2[:], dram["m_b2"]).then_inc(k["b"], 16)

                def load(e, r):
                    pick = bass.ds(e, 1) if not isinstance(e, int) else slice(e, e + 1)
                    sp.dma_start(w1[:, r, :], dram["m_w1"][pick].rearrange("a p n -> p (a n)")).then_inc(loaded[r], 16)
                    sp.dma_start(b1[:, r, :], dram["m_b1"][pick].rearrange("a p f -> p (a f)"))\
                        .then_inc(loaded[r], 16)
                    sp.dma_start(w2[:, r], dram["m_w2"][pick].rearrange("a p f n -> p (a f) n")).then_inc(loaded[r], 16)

                load(0, 0)
                load(1, 1)
                with sp.Fori(0, EXP // 2 - 1) as i:
                    for r in range(2):
                        sp.wait_ge(k["o"], i * 2 * GROUPS + ((r + 1) * GROUPS + 2))
                        load(i * 2 + (r + 2), r)

            @block.tensor
            def _(pe):
                pe.sem_inc(k["o"], 2)
                for t in range(TILES):
                    ins = nc.tensor.matmul(ps[:, 6, t * EXP:(t + 1) * EXP],
                                           m.xt[:, t // 2, PAD + (t % 2) * P:PAD + (t % 2) * P + P], w.m_gate[:],
                                           start=(t == 0), stop=True, skip_group_check=True)
                ins.then_inc(k["lg"], 1)
                pe.wait_ge(k["st"], 6)
                for t in range(TILES):
                    ins = nc.tensor.transpose(ps[0:EXP, t // 4, (t % 4) * P:(t % 4 + 1) * P], hot[:, t, :], m.ident[:])
                ins.then_inc(k["ht"], 1)
                pe.wait_ge(k["hc"], 1)
                pe.wait_ge(k["b"], 16)
                for t in range(TILES):
                    ins = nc.tensor.matmul(ps[:, 4 + t // 4, (t % 4) * P:(t % 4 + 1) * P], hott[:, t * P:(t + 1) * P],
                                           b2[:], start=(t % 4 == 0), stop=True, skip_group_check=True)
                ins.then_inc(k["bp"], 1)
                with pe.Fori(0, EXP // 2) as i:
                    pe_expert(pe, i, 0)
                    pe_expert(pe, i, 1)

            @block.scalar
            def _(act):
                act.wait_ge(k["ht"], 1)
                nc.scalar.activation(hott[:], ps[0:EXP, 0:4, :].rearrange("p a b -> p (a b)"),
                                     ACT.Copy).then_inc(k["hc"], 1)
                act.wait_ge(k["hc"], 1)
                act.sem_inc(k["h"], 4)
                with act.Fori(0, EXP // 2) as i:
                    act_expert(act, i, 0)
                    act_expert(act, i, 1)

            @block.vector
            def _(dve):
                dve.wait_ge(k["lg"], 1)
                nc.vector.tensor_copy(logits[:], ps[:, 6, 0:TILES * EXP].rearrange("p (t e) -> p t e", e=EXP))\
                    .then_inc(k["st"], 1)
                pick_first(nc, dve, k["st"], 1, k["order"], logits, best, hot, order)
                dve.wait_ge(k["bp"], 1)
                nc.vector.tensor_tensor(y[:].rearrange("p t d -> p (t d)"), y[:].rearrange("p t d -> p (t d)"),
                                        ps[:, 4:8, :].rearrange("p a b -> p (a b)"), ALU.add).then_inc(k["bd"], 1)
                dve.wait_ge(k["bd"], 1)
                dve.sem_inc(k["acc"], 2)
                with dve.Fori(0, EXP) as e:
                    dve_expert(dve, e)
                normalise(nc, dve, m, y, k["nn"], k["pw"], [(k["acc"], EXP * GROUPS + 2)])
                for t in range(TILES):
                    ins = nc.vector.tensor_scalar(y[:, t, :], y[:, t, :], m.mv[:, t, 0:1], m.rstd[:, t:t + 1],
                                                  ALU.subtract, ALU.mult)
                ins.then_inc(k["g2"], 1)
                dve.wait_ge(k["g2"], 1)
                nc.vector.tensor_tensor(y[:], y[:], w.m_rows[:, 3:4, :].to_broadcast([P, TILES, DIM]),
                                        ALU.mult).then_inc(k["g2"], 1)
                dve.wait_ge(k["g2"], 2)
                dve.wait_ge(k["order"], 2)
                nc.vector.tensor_tensor(m.x[:], m.x[:], y[:], ALU.add)

            @block.gpsimd
            def _(pool):
                nc.gpsimd.iota(order[:], [[-1, EXP]], base=EXP, channel_multiplier=0,
                               allow_small_or_imprecise_dtypes=True).then_inc(k["order"], 1)
                nc.gpsimd.tensor_tensor(m.x[:], m.x[:], w.m_rows[:, 4:5, :].to_broadcast([P, TILES, DIM]),
                                        ALU.add).then_inc(k["order"], 1)
                pool.wait_ge(k["nn"], 3)
                nc.gpsimd.tensor_tensor(m.rstd[:], m.ve[:], m.mhalf[:], ALU.pow).then_inc(k["pw"], 1)


def network(nc, dram, out, start=0, stop=99):
    with ExitStack() as ctx:
        m = open_memory(nc, ctx)
        conv = ExitStack()

        def first_ffn():
            m.toeplitz = conv.enter_context(nc.sbuf_tensor("toeplitz", [P, DIM, P], F32))
            layernorm(nc, m, "ln1")
            lora_ffn(nc, m, "f1", prefetch=lambda sp: load_toeplitz(sp, m))

        def convolution():
            layernorm(nc, m, "ln2", transposed=False)
            long_conv(nc, m)
            conv.close()

        layers = [lambda: setup(nc, m, ctx, dram),
                  lambda: (layernorm(nc, m, "ln0"), state_space(nc, m)),
                  first_ffn,
                  convolution,
                  lambda: (layernorm(nc, m, "ln3"), lora_ffn(nc, m, "f2")),
                  lambda: (layernorm(nc, m, "ln4"), attention(nc, m, "at1", m.w.a1, True)),
                  lambda: (layernorm(nc, m, "ln5"), batch_attention(nc, m, "ba1"), experts(nc, m, "ex1", dram)),
                  lambda: (layernorm(nc, m, "ln6"), attention(nc, m, "at2", m.w.a2, False)),
                  lambda: (layernorm(nc, m, "ln7"), batch_attention(nc, m, "ba2"), experts(nc, m, "ex2", dram))]
        for layer in [layers[0]] + layers[start + 1:stop + 1]:
            layer()
        stored = ctx.enter_context(nc.semaphore("stored"))
        with nc.Block() as block:
            @block.sync
            def _(sp):
                sp.dma_start(out.rearrange("b (h p) d -> p (b h) d", p=P), m.x[:]).then_inc(stored, 16)
                sp.wait_ge(stored, 16)


def lay_out(inputs):
    g = {k: np.asarray(v) for k, v in inputs.items()}

    def cols(a):
        return a.reshape(-1, P).T

    def rows(a):
        return a.reshape(-1, P, a.shape[-1]).transpose(1, 0, 2)

    d = {
        "x": g["L0_attn_a_x"],
        "in_w": g["L0_attn_a_W_in"],
        "conv_rows": g["L0_attn_a_conv_w"][:, 0, :].T,
        "conv_b": cols(g["L0_attn_a_conv_b"]),
        "x_w": rows(g["L0_attn_a_W_x"]),
        "dt_w": g["L0_attn_a_W_dt"],
        "dt_b": cols(g["L0_attn_a_b_dt"]),
        "a_log": rows(g["L0_attn_a_A_log"]),
        "d_skip": cols(g["L0_attn_a_D"]),
        "out_w": rows(g["L0_attn_a_W_out"]),
        "lc_a": g["L0_attn_b_A_log"].reshape(-1, 1),
        "lc_arow": g["L0_attn_b_A_log"],
        "lc_ct": g["L0_attn_b_C"].T,
        "lc_delta": g["L0_attn_b_delta"][0:1],
        "lc_rows": np.stack([g[f"L0_attn_b_{n}"] for n in ("D", "freq_align", "reward", "gamma", "beta")]),
        "gate": np.concatenate([g["L0_ffn_gate_W"].T, g["L0_ffn_lora_A"].reshape(ER, DIM).T], axis=1),
        "gate_b": g["L0_ffn_gate_b"],
        "wi": g["L0_ffn_wi_W"].T,
        "wi_b": cols(g["L0_ffn_wi_b"]),
        "wo": rows(np.ascontiguousarray(g["L0_ffn_wo_W"].T)),
        "wo_b": g["L0_ffn_wo_b"],
        "lora_b": g["L0_ffn_lora_B"].transpose(0, 2, 1).reshape(ER, FF),
    }
    straight = np.concatenate([h * HD + np.r_[0:HD:2, 1:HD:2] for h in range(HEADS)])
    crossed = np.concatenate([h * HD + np.r_[1:HD:2, 0:HD:2] for h in range(HEADS)])
    wq, wk, wv = np.split(g["L1_attn_a_w_qkv"], 3, axis=0)

    def spread_heads(wo):
        t = np.zeros((4, 32, 4, DIM), np.float32)
        t[:, :HD] = wo.reshape(4, 4, HD, DIM).transpose(1, 2, 0, 3)
        return t.reshape(P, 4, DIM)

    half = (np.arange(0, HD, 2, dtype=np.float32) / np.float32(HD)).astype(np.float32)
    inv = (np.float32(1) / np.power(np.float32(10000), half)).astype(np.float32)
    angle = np.outer(inv, np.arange(SEQ, dtype=np.float32)).astype(np.float32)
    cos, sin = np.cos(angle), np.sin(angle)
    pos = np.arange(SEQ)
    chunk = pos // CHUNK_FRAMES
    allowed = (chunk[None, :] <= chunk[:, None]) | (pos[None, :] <= pos[:, None] + LOOKAHEAD)
    mask = np.where(allowed, 0, NEG).astype(np.float32)
    same = np.arange(P) % PG
    d.update({
        "a1_wq1": wq[straight].T, "a1_wq2": wq[crossed].T, "a1_wk1": wk[straight].T, "a1_wk2": wk[crossed].T,
        "a1_wv": wv.T, "a1_wo": spread_heads(g["L1_attn_a_w_out"].T), "a1_bo": g["L1_attn_a_b_out"],
        "a1_cos": np.tile(np.concatenate([cos, cos]), (HEADS, 1)),
        "a1_sin": np.tile(np.concatenate([-sin, sin]), (HEADS, 1)),
        "a2_wq": g["L1_attn_b_Wq"], "a2_wk": g["L1_attn_b_Wk"], "a2_wv": g["L1_attn_b_Wv"],
        "a2_wo": spread_heads(g["L1_attn_b_Wo"]),
        "a2_bq": g["L1_attn_b_bq"].reshape(P, 1),
        "a2_bo": g["L1_attn_b_bo"],
        "a2_bv": g["L1_attn_b_bv"],
        "head_mask": (np.arange(P)[:, None] // HD % 4 == np.arange(4)[None, :]).astype(np.float32),
        "head_rows": (np.arange(P)[:, None] // MHD == np.arange(MH)[None, :]).astype(np.float32),
        "pick_max": np.repeat(((np.arange(P)[:, None] % 4 == np.arange(4)[None, :])
                               & (np.arange(P)[:, None] < 12)).astype(np.float32)[:, :, None], P, axis=2),
        "mask_q": mask.reshape(2, P, SEQ).transpose(1, 0, 2),
        "mask_k": mask.T.reshape(2, P, SEQ).transpose(1, 0, 2),
        "m_q": g["L1_ffn_Wqkv"][0:DIM].T, "m_k": g["L1_ffn_Wqkv"][DIM:2 * DIM].T, "m_v": g["L1_ffn_Wqkv"][2 * DIM:].T,
        "m_o": g["L1_ffn_Wo"].T, "m_bqkv": cols(g["L1_ffn_bqkv"]),
        "m_gb": np.stack([g["L1_ffn_g1"], g["L1_ffn_be1"]], axis=1),
        "m_rows": np.stack([g[f"L1_ffn_{n}"] for n in ("bo", "g1", "be1", "g2", "be2")]),
        "m_gate": g["L1_ffn_Wg"].T,
        "m_mask": np.where(same[:, None] == same[None, :], 0, NEG).astype(np.float32),
        "m_w1": g["L1_ffn_W1"],
        "m_w2": g["L1_ffn_W2"].reshape(EXP, FT, P, DIM).transpose(0, 2, 1, 3),
        "m_b1": g["L1_ffn_b1"].reshape(EXP, FT, P).transpose(0, 2, 1),
        "m_b2": g["L1_ffn_b2"],
    })
    return {k: np.ascontiguousarray(v) for k, v in d.items()}


def kernel(**inputs):
    import concourse.bacc as bacc
    from concourse.bass_utils import run_bass_kernel_spmd as run

    nc = bacc.Bacc("TRN2", target_bir_lowering=False, num_devices=1)
    arrays, dram = {}, {}
    for name, a in lay_out(inputs).items():
        arrays[f"in_{name}_dram"] = a
        dram[name] = nc.dram_tensor(f"in_{name}_dram", a.shape, mybir.dt.from_np(a.dtype), kind="ExternalInput").ap()
    out = nc.dram_tensor("out_0_dram", (BATCH, SEQ, DIM), F32, kind="ExternalOutput").ap()
    network(nc, dram, out)
    return run(nc, [arrays], core_ids=[0]).results[0]["out_0_dram"]
```

```python
from contextlib import ExitStack

import concourse.bass as bass
import numpy as np
from concourse import mybir

ALU = mybir.AluOpType
ACT = mybir.ActivationFunctionType
AX = mybir.AxisListType
F32 = mybir.dt.float32
BF16 = mybir.dt.bfloat16

P = 128
BATCH, SEQ, DIM = 8, 256, 128
TOK = BATCH * SEQ
TILES = TOK // P
BANK = 512
GROUPS = TOK // BANK
GT = TILES // GROUPS
EPS = 1e-5

CONV = 4
PAD = CONV - 1
DIN, NST, DTR = 256, 16, 64
CH = DIN // P
HALVES = 2
HB = BATCH // HALVES
HT = TOK // HALVES
LNST = 64
TOEPLITZ_LOADS = 8
FF, FT = 512, 4
EXP, RANK = 8, 4
ER = EXP * RANK
HEADS, HD = 16, 8
CHUNK_FRAMES, LOOKAHEAD = 100, 50
NEG = -1e30
MH, MHD = 4, 32
PG = 16
NPG = SEQ // PG


class Net:
    pass


def open_memory(nc, ctx):
    m = Net()

    def sb(name, shape, dt=F32):
        return ctx.enter_context(nc.sbuf_tensor(name, shape, dt))

    m.x = sb("x_res", [P, TILES, DIM])
    m.xn = sb("x_norm", [P, TILES, DIM])
    m.xt = sb("x_norm_t", [P, BATCH, PAD + SEQ])
    m.ident = sb("ident", [P, P])
    m.identb = sb("identb", [P, P], BF16)
    m.stats = sb("ln_stats", [P, TILES, 6])
    m.mv = sb("ln_mean_var", [P, TILES, 2])
    m.ve = sb("ln_var_eps", [P, TILES])
    m.rstd = sb("ln_rstd", [P, TILES])
    m.mhalf = sb("minus_half", [P, TILES])
    m.ones = sb("ones_row", [P, P])
    m.ps = ctx.enter_context(nc.psum_tensor("psum", [P, 8, BANK], F32))
    return m


def sems(nc, ctx, names, prefix=""):
    held = {n: ctx.enter_context(nc.semaphore(prefix + n)) for n in names.split()}

    def clear():
        for h in held.values():
            nc.gpsimd.sem_clear(h)

    ctx.callback(clear)
    return held


def load_weights(nc, m, ctx, dram):
    def sb(name, shape, dt=F32):
        return ctx.enter_context(nc.sbuf_tensor(name, shape, dt))

    w = m.w = Net()
    w.in_w = sb("w_in", [P, 2 * DIN])
    w.conv_rows = sb("w_conv_rows", [P, CONV, DIN])
    w.conv_b = sb("w_conv_b", [P, CH])
    w.x_w = sb("w_x", [P, CH, DTR + 2 * NST])
    w.dt_w = sb("w_dt", [DTR, DIN])
    w.dt_b = sb("w_dt_b", [P, CH])
    w.a_log = sb("w_a_log", [P, CH, NST])
    w.d_skip = sb("w_d_skip", [P, CH])
    w.out_w = sb("w_out", [P, CH, DIM])
    w.lc_a = sb("lc_a_log", [LNST, 1])
    w.lc_ct = sb("lc_ct", [LNST, DIM])
    w.lc_delta = sb("lc_delta0", [P, 1])
    w.lc_rows = sb("lc_rows", [P, 5, DIM])
    w.lc_arow = sb("lc_a_row", [P, LNST])
    w.gate = sb("f_gate", [P, EXP + ER])
    w.gate_b = sb("f_gate_b", [P, EXP])
    w.wi = sb("f_wi", [P, FF])
    w.wi_b = sb("f_wi_b", [P, FT])
    w.wo = sb("f_wo", [P, FT, DIM])
    w.wo_b = sb("f_wo_b", [P, DIM])
    w.lora_b = sb("f_lora_b", [ER, FF])
    for name, rope in (("a1", True), ("a2", False)):
        a = Net()
        a.wq1, a.wk1, a.wv = (sb(f"{name}_{n}", [P, DIM]) for n in ("wq", "wk", "wv"))
        a.wo = sb(f"{name}_wo", [P, DIM])
        a.bo = sb(f"{name}_bo", [P, DIM])
        if rope:
            a.wq2, a.wk2 = sb(f"{name}_wq2", [P, DIM]), sb(f"{name}_wk2", [P, DIM])
            a.cos, a.sin = sb(f"{name}_cos", [P, SEQ]), sb(f"{name}_sin", [P, SEQ])
            w.a1 = a
        else:
            a.bq = sb(f"{name}_bq", [P, 1])
            a.bv = sb(f"{name}_bv", [P, DIM])
            a.mask_q, a.mask_k = (sb(f"{name}_{n}", [P, 2, SEQ], BF16) for n in ("mask_q", "mask_k"))
            w.a2 = a
    w.head_rows = sb("head_rows", [P, MH])
    w.pick = sb("pick_max", [P, 4, P], BF16)
    w.m_q, w.m_k, w.m_v, w.m_o = (sb(f"m_{n}", [P, DIM]) for n in "qkvo")
    w.m_bqkv = sb("m_bqkv", [P, 3])
    w.m_gb = sb("m_gb", [P, 2])
    w.m_rows = sb("m_rows", [P, 5, DIM])
    w.m_gate = sb("m_gate", [P, EXP])
    w.m_mask = sb("m_mask", [P, P], BF16)
    for a in (w.a1, w.a2):
        a.pick = w.pick
    copies = [(w.in_w, "in_w"), (w.conv_b, "conv_b"), (w.x_w, "x_w"), (w.dt_w, "dt_w"), (w.dt_b, "dt_b"),
              (w.a_log, "a_log"), (w.d_skip, "d_skip"), (w.out_w, "out_w"), (w.lc_a, "lc_a"),
              (w.lc_ct, "lc_ct"), (w.gate, "gate"), (w.wi, "wi"), (w.wi_b, "wi_b"), (w.wo, "wo"),
              (w.lora_b, "lora_b"), (w.a1.wq1, "a1_wq1"), (w.a1.wq2, "a1_wq2"), (w.a1.wk1, "a1_wk1"),
              (w.a1.wk2, "a1_wk2"), (w.a1.wv, "a1_wv"), (w.a1.wo, "a1_wo"), (w.a1.cos, "a1_cos"),
              (w.a1.sin, "a1_sin"), (w.a2.wq1, "a2_wq"), (w.a2.wk1, "a2_wk"), (w.a2.wv, "a2_wv"),
              (w.a2.wo, "a2_wo"), (w.a2.bq, "a2_bq"), (w.head_rows, "head_rows"), (w.m_q, "m_q"), (w.m_k, "m_k"),
              (w.m_v, "m_v"), (w.m_o, "m_o"), (w.m_bqkv, "m_bqkv"), (w.m_gb, "m_gb"), (w.m_gate, "m_gate")]
    spread = [(w.conv_rows, "conv_rows"), (w.lc_delta, "lc_delta"), (w.lc_rows, "lc_rows"), (w.lc_arow, "lc_arow"),
              (w.gate_b, "gate_b"), (w.wo_b, "wo_b"), (w.a1.bo, "a1_bo"), (w.a2.bo, "a2_bo"), (w.a2.bv, "a2_bv"), (w.m_rows, "m_rows")]
    w.tables = [(w.a2.mask_q, "mask_q"), (w.a2.mask_k, "mask_k"), (w.pick, "pick_max"), (w.m_mask, "m_mask")]

    return copies, spread


def on_all_partitions(ap):
    return bass.AP(ap.tensor, ap.offset, [[0, P]] + [list(d) for d in ap.ap])


def setup(nc, m, ctx, dram):
    copies, spread = load_weights(nc, m, ctx, dram)
    w = m.w
    m.toeplitz_loaded = ctx.enter_context(nc.semaphore("toeplitz_loaded"))
    m.lc_pow = ctx.enter_context(nc.sbuf_tensor("lc_pow", [LNST, P + 1], F32))
    m.lc_powt = ctx.enter_context(nc.sbuf_tensor("lc_powt", [P, LNST], F32))
    m.kernel_dram = kernel_dram = nc.dram_tensor("kernel_scratch", (DIM, 2 * P), F32, kind="Internal").ap()
    with ExitStack() as own:
        def sb(name, shape, dt=F32):
            return own.enter_context(nc.sbuf_tensor(name, shape, dt))

        steps = sb("steps", [LNST, P + 1])
        back = sb("steps_back", [P, 1])
        da = sb("delta_a", [LNST, 1])
        dar = sb("delta_a_row", [P, LNST])
        kpad = sb("kernel_padded", [DIM, 2 * P])
        wide = [sb(f"table{i}", list(t.shape)) for i, (t, _) in enumerate(w.tables)]
        s = sems(nc, own, "su_loaded su_w su_consts su_zeros su_dve su_rates su_pow su_kpsum su_kernel su_kdram su_tables")
        with nc.Block() as block:
            @block.sync
            def _(sp):
                sp.dma_start(m.x[:], dram["x"].rearrange("b (h p) d -> p (b h) d", p=P)).then_inc(s["su_w"], 16)
                for dst, (_, name) in zip(wide, w.tables):
                    sp.dma_start(dst[:], dram[name]).then_inc(s["su_tables"], 16)
                for dst, name in copies:
                    sp.dma_start(dst[:], dram[name]).then_inc(s["su_w"], 16)
                sp.wait_ge(s["su_kernel"], 1)
                sp.dma_start(kernel_dram, kpad[:]).then_inc(s["su_kdram"], 16)
                sp.wait_ge(s["su_kdram"], 16)
                sp.wait_ge(s["su_w"], 16 * (1 + len(copies)))

            @block.scalar
            def _(act):
                for dst, name in spread:
                    act.dma_start(dst[:], on_all_partitions(dram[name])).then_inc(s["su_loaded"], 16)
                act.wait_ge(s["su_w"], 16 * (1 + len(copies)))
                act.wait_ge(s["su_loaded"], 16 * len(spread))
                nc.scalar.activation(da[:], w.lc_a[:], ACT.Exp).then_inc(s["su_rates"], 1)
                nc.scalar.activation(dar[:], w.lc_arow[:], ACT.Exp).then_inc(s["su_rates"], 1)
                nc.scalar.activation(w.a_log[:], w.a_log[:], ACT.Exp).then_inc(s["su_rates"], 1)
                act.wait_ge(s["su_dve"], 3)
                act.wait_ge(s["su_consts"], 1)
                nc.scalar.activation(m.lc_pow[:], steps[:], ACT.Exp, scale=da[:]).then_inc(s["su_pow"], 1)
                nc.scalar.activation(m.lc_powt[:], dar[:], ACT.Exp, scale=back[:]).then_inc(s["su_pow"], 1)

            @block.vector
            def _(dve):
                nc.vector.memset(kpad[:], 0.0).then_inc(s["su_zeros"], 1)
                nc.vector.memset(m.xt[:], 0.0)
                nc.vector.memset(m.mhalf[:], -0.5)
                nc.vector.memset(m.ones[:], 1.0)
                dve.wait_ge(s["su_tables"], 16 * len(wide))
                for src, (dst, _) in zip(wide, w.tables):
                    nc.vector.tensor_copy(dst[:], src[:])
                dve.wait_ge(s["su_rates"], 3)
                nc.vector.tensor_scalar(da[:], da[:], w.lc_delta[0:LNST], -1.0, ALU.mult, ALU.mult).then_inc(s["su_dve"], 1)
                nc.vector.tensor_scalar(dar[:], dar[:], w.lc_delta[:], -1.0, ALU.mult, ALU.mult).then_inc(s["su_dve"], 1)
                nc.vector.tensor_scalar(w.a_log[:], w.a_log[:], -1.0, None, ALU.mult).then_inc(s["su_dve"], 1)
                dve.wait_ge(s["su_kpsum"], 1)
                dve.wait_ge(s["su_zeros"], 1)
                nc.vector.tensor_copy(kpad[:, P - 1:2 * P - 1], m.ps[:, 0, 0:P]).then_inc(s["su_kernel"], 1)

            @block.gpsimd
            def _(pool):
                nc.gpsimd.iota(steps[:], [[1, P + 1]], base=0, channel_multiplier=0,
                               allow_small_or_imprecise_dtypes=True)
                nc.gpsimd.iota(back[:], [[0, 1]], base=P - 1, channel_multiplier=-1,
                               allow_small_or_imprecise_dtypes=True).then_inc(s["su_consts"], 1)
                nc.gpsimd.memset(m.ident[:], 0.0)
                nc.gpsimd.memset(m.identb[:], 0.0).then_inc(s["su_consts"], 1)
                pool.wait_ge(s["su_consts"], 2)
                for t in (m.ident, m.identb):
                    nc.gpsimd.affine_select(out=t[:], in_=t[:], compare_op=ALU.not_equal, fill=1.0, base=0,
                                            pattern=[[-1, P]], channel_multiplier=1)

            @block.tensor
            def _(pe):
                pe.wait_ge(s["su_pow"], 1)
                nc.tensor.matmul(m.ps[:, 0, 0:P], w.lc_ct[:], m.lc_pow[:, 0:P], start=True,
                                 stop=True).then_inc(s["su_kpsum"], 1)
    return


def layernorm(nc, m, name, transposed=True, padded=True):
    with ExitStack() as own:
        k = sems(nc, own, "stats mv ve rstd xn xtp xt", f"{name}_")
        with nc.Block() as block:
            @block.vector
            def _(dve):
                for t in range(TILES):
                    ins = nc.vector.bn_stats(m.stats[:, t, :], m.x[:, t, :])
                ins.then_inc(k["stats"], 1)
                dve.wait_ge(k["stats"], 1)
                for t in range(TILES):
                    ins = nc.vector.bn_aggr(m.mv[:, t, :], m.stats[:, t, :])
                ins.then_inc(k["mv"], 1)
                dve.wait_ge(k["mv"], 1)
                nc.vector.tensor_scalar(m.ve[:], m.mv[:, :, 1], EPS, None, ALU.add).then_inc(k["ve"], 1)
                dve.wait_ge(k["rstd"], 1)
                for g in range(GROUPS):
                    for t in range(g * GT, (g + 1) * GT):
                        ins = nc.vector.tensor_scalar(m.xn[:, t, :], m.x[:, t, :], m.mv[:, t, 0:1],
                                                      m.rstd[:, t:t + 1], ALU.subtract, ALU.mult)
                    ins.then_inc(k["xn"], 1)

            @block.gpsimd
            def _(pool):
                pool.wait_ge(k["ve"], 1)
                nc.gpsimd.tensor_tensor(m.rstd[:], m.ve[:], m.mhalf[:], ALU.pow).then_inc(k["rstd"], 1)

            if transposed:
                @block.tensor
                def _(pe):
                    for g in range(GROUPS):
                        pe.wait_ge(k["xn"], g + 1)
                        for t in range(GT):
                            ins = nc.tensor.transpose(m.ps[:, g, t * P:(t + 1) * P], m.xn[:, g * GT + t, :],
                                                      m.ident[:])
                        ins.then_inc(k["xtp"], 1)

                @block.scalar
                def _(act):
                    for g in range(GROUPS):
                        act.wait_ge(k["xtp"], g + 1)
                        nc.scalar.activation(m.xt[:, 2 * g:2 * g + 2, PAD:],
                                             m.ps[:, g, :].rearrange("p (b t) -> p b t", b=2), ACT.Copy)


def state_space(nc, m):
    w = m.w
    with ExitStack() as own:
        def sb(name, shape, dt=F32):
            return own.enter_context(nc.sbuf_tensor(name, shape, dt))

        tap_w = w.conv_rows
        d_diag = sb("d_diag", [P, CH, P])
        pick = sb("pick", [96, 2 * NST, P], BF16)
        u = sb("u", [P, CH, HT])
        gate = sb("res_gate", [P, CH, HT])
        bc3 = sb("bc_split", [96, HT], BF16)
        bcm = sb("bc_mid", [96, HT], BF16)
        w_bc = sb("w_bc3", [P, CH, 96])
        delta = sb("delta", [P, CH, HT])
        t_abs = sb("t_abs", [P, CH, HT])
        du = m.xn[:].rearrange("p (c a) d -> p c (a d)", c=CH)
        bs = sb("b_rows", [P, 2, HT])
        cs = sb("c_rows", [P, 2, HT])
        da = sb("decay", [P, 2, CH, HB, SEQ])
        hs = sb("h_state", [P, 2, CH, HT])
        bcr, bcr2 = hs[0:96, 0, 0, :], hs[0:96, 0, 1, :]
        dt_in = hs[0:DTR, 1, 0, :]
        y = t_abs
        s = sems(nc, own, "ss_set ss_pool ss_xs ss_u ss_res ss_gate ss_xd ss_dtin ss_split ss_bc ss_z ss_expn ss_abs ss_sp ss_relu ss_delta ss_du "
                          "ss_pick ss_rows ss_free ss_da ss_dbu ss_h ss_hc ss_y0 ss_acc ss_y ss_o ss_x")
        ps = m.ps
        BC_BANKS, Y_BANKS = (0, 1, 2, 3), (4, 5, 6, 7)
        with nc.Block() as block:
            @block.gpsimd
            def _(pool):
                nc.gpsimd.memset(pick[:], 0.0)
                nc.gpsimd.memset(da[:, :, :, :, 0:1], 0.0).then_inc(s["ss_pool"], 1)
                pool.wait_ge(s["ss_pool"], 1)
                for part in range(3):
                    nc.gpsimd.affine_select(out=pick[:], in_=pick[:], compare_op=ALU.not_equal, fill=1.0,
                                            base=-32 * part, pattern=[[-1, 2 * NST], [0, P]],
                                            channel_multiplier=1).then_inc(s["ss_pool"], 1)
                    pool.wait_ge(s["ss_pool"], 2 + part)
                for half in range(HALVES):
                    base = half * NST
                    with pool.Fori(0, NST // 2) as pair:
                        n = pair * 2
                        for j in range(2):
                            pool.wait_ge(s["ss_rows"], n + (base + j + 1))
                            for c in range(CH):
                                unit = n * CH + ((base + j) * CH + c + 1)
                                pool.wait_ge(s["ss_h"], unit)
                                nc.gpsimd.tensor_tensor(hs[:, j, c, :], hs[:, j, c, :], cs[:, j, :],
                                                        ALU.mult).then_inc(s["ss_hc"], 1)
                            pool.wait_ge(s["ss_hc"], n * CH + (base + j + 1) * CH)
                            pool.sem_inc(s["ss_free"], 1)

            @block.vector
            def _(dve):
                for k in range(CONV):
                    nc.vector.tensor_tensor(tap_w[:, k, :], w.in_w[:, 0:DIN], w.conv_rows[:, k, :], ALU.mult)
                for c in range(CH):
                    for part in range(3):
                        nc.vector.tensor_copy(w_bc[:, c, part * 32:part * 32 + 32], w.x_w[:, c, DTR:])
                    ins = nc.vector.tensor_scalar(d_diag[:, c, :], m.ident[:], w.d_skip[:, c:c + 1], None, ALU.mult)
                ins.then_inc(s["ss_set"], 1)
                for half in range(HALVES):
                    split = 5 * half
                    dve.wait_ge(s["ss_xd"], half + 1)
                    src = ps[0:96, 2:4, :].rearrange("p a b -> p (a b)")
                    nc.vector.tensor_copy(bc3[:], src).then_inc(s["ss_split"], 1)
                    dve.wait_ge(s["ss_split"], split + 1)
                    nc.vector.tensor_tensor(bcr, src, bc3[:], ALU.subtract).then_inc(s["ss_split"], 1)
                    dve.wait_ge(s["ss_split"], split + 2)
                    nc.vector.tensor_copy(bcm[:], bcr).then_inc(s["ss_split"], 1)
                    dve.wait_ge(s["ss_split"], split + 3)
                    nc.vector.tensor_copy(bc3[32:64, :], bcm[32:64, :])
                    nc.vector.tensor_tensor(bcr2, bcr, bcm[:], ALU.subtract).then_inc(s["ss_split"], 1)
                    dve.wait_ge(s["ss_split"], split + 4)
                    nc.vector.tensor_copy(bc3[64:96, :], bcr2[64:96, :]).then_inc(s["ss_split"], 1)
                    dve.wait_ge(s["ss_abs"], CH * (half + 1))
                    for c in range(CH):
                        zc = ps[:, 4 + 2 * c:6 + 2 * c, :].rearrange("p a b -> p (a b)")
                        ins = nc.vector.tensor_scalar(delta[:, c, :], zc, w.dt_b[:, c:c + 1], 0.0, ALU.add, ALU.max)
                    ins.then_inc(s["ss_relu"], 1)
                    dve.wait_ge(s["ss_relu"], half + 1)
                    dve.wait_ge(s["ss_sp"], half + 1)
                    nc.vector.tensor_tensor(delta[:], delta[:], t_abs[:], ALU.add).then_inc(s["ss_delta"], 1)
                    dve.wait_ge(s["ss_delta"], half + 1)
                    nc.vector.tensor_tensor(du[:], delta[:], u[:], ALU.mult).then_inc(s["ss_du"], 1)
                    dve.wait_ge(s["ss_du"], half + 1)
                    base = half * NST
                    with dve.Fori(0, NST // 2) as pair:
                        n = pair * 2
                        for j in range(2):
                            dve.wait_ge(s["ss_rows"], n + (base + j + 1))
                            for c in range(CH):
                                unit = n * CH + ((base + j) * CH + c + 1)
                                dve.wait_ge(s["ss_acc"], unit)
                                nc.vector.tensor_tensor(hs[:, j, c, :], du[:, c, :], bs[:, j, :],
                                                        ALU.mult).then_inc(s["ss_dbu"], 1)
                                dve.wait_ge(s["ss_da"], unit)
                                dve.wait_ge(s["ss_dbu"], unit)
                                nc.vector.tensor_tensor_scan(
                                    hs[:, j, c, :], da[:, j, c, :, :].rearrange("p b t -> p (b t)"), hs[:, j, c, :],
                                    0.0, ALU.mult, ALU.add).then_inc(s["ss_h"], 1)
                    dve.wait_ge(s["ss_acc"], CH * NST * (half + 1) + 2 * CH)
                    for c in range(CH):
                        nc.vector.tensor_tensor(y[:, c, :], ps[:, 4 + 2 * c:6 + 2 * c, :].rearrange("p a b -> p (a b)"),
                                                gate[:, c, :], ALU.mult).then_inc(s["ss_y"], 1)
                    dve.wait_ge(s["ss_o"], half + 1)
                    xh = m.x[:, half * 8:half * 8 + 8, :].rearrange("p t d -> p (t d)")
                    nc.vector.tensor_tensor(xh, xh, ps[:, 0:2, :].rearrange("p a b -> p (a b)"),
                                            ALU.add).then_inc(s["ss_x"], 1)

            @block.tensor
            def _(pe):
                pe.sem_inc(s["ss_acc"], 2 * CH)
                pe.wait_ge(s["ss_set"], 1)
                pe.wait_ge(s["ss_pool"], 4)
                for half in range(HALVES):
                    if half:
                        pe.wait_ge(s["ss_x"], half)
                    for c in range(CH):
                        for q in range(2):
                            b0 = half * HB + 2 * q
                            for k in range(CONV):
                                ins = nc.tensor.matmul(ps[:, 2 * c + q, :], tap_w[:, k, c * P:(c + 1) * P],
                                                       m.xt[:, b0:b0 + 2, k:k + SEQ], start=(k == 0),
                                                       stop=(k == CONV - 1))
                        ins.then_inc(s["ss_xs"], 1)
                    for c in range(CH):
                        for q in range(2):
                            b0 = half * HB + 2 * q
                            ins = nc.tensor.matmul(ps[:, 4 + 2 * c + q, :], w.in_w[:, DIN + c * P:DIN + (c + 1) * P],
                                                   m.xt[:, b0:b0 + 2, PAD:], start=True, stop=True)
                        ins.then_inc(s["ss_res"], 1)
                    pe.wait_ge(s["ss_u"], CH * (half + 1))
                    for q in range(2):
                        for c in range(CH):
                            nc.tensor.matmul(ps[0:DTR, q, :], w.x_w[:, c, 0:DTR], u[:, c, q * BANK:(q + 1) * BANK],
                                             start=(c == 0), stop=(c == CH - 1))
                        for c in range(CH):
                            ins = nc.tensor.matmul(ps[0:96, 2 + q, :], w_bc[:, c, :], u[:, c, q * BANK:(q + 1) * BANK],
                                                   start=(c == 0), stop=(c == CH - 1))
                    ins.then_inc(s["ss_xd"], 1)
                    pe.wait_ge(s["ss_dtin"], half + 1)
                    pe.wait_ge(s["ss_gate"], CH * (half + 1))
                    for c in range(CH):
                        for q in range(2):
                            ins = nc.tensor.matmul(ps[:, 4 + 2 * c + q, :], w.dt_w[:, c * P:(c + 1) * P],
                                                   dt_in[:, q * BANK:(q + 1) * BANK], start=True, stop=True)
                    ins.then_inc(s["ss_z"], 1)
                    pe.wait_ge(s["ss_split"], 5 * (half + 1))
                    pe.wait_ge(s["ss_relu"], half + 1)
                    pe.wait_ge(s["ss_abs"], CH * (half + 1))
                    for c in range(CH):
                        for q in range(2):
                            nc.tensor.matmul(ps[:, 4 + 2 * c + q, :], d_diag[:, c, :], u[:, c, q * BANK:(q + 1) * BANK],
                                             start=True, stop=False, skip_group_check=True)
                    base = half * NST

                    def rows(n, j):
                        if base or j:
                            pe.wait_ge(s["ss_rows"], n + (base + j))
                        for k in range(2):
                            r = pick[:, bass.ds(n + (j + k * NST), 1), :].rearrange("k a p -> k (a p)")
                            for q in range(2):
                                ins = nc.tensor.matmul(ps[:, 2 * k + q, :], r, bc3[:, q * BANK:(q + 1) * BANK],
                                                       start=True, stop=True)
                        ins.then_inc(s["ss_pick"], 1)

                    def add_state(n, j):
                        for c in range(CH):
                            pe.wait_ge(s["ss_hc"], n * CH + ((base + j) * CH + c + 1))
                            for q in range(2):
                                ins = nc.tensor.matmul(ps[:, 4 + 2 * c + q, :], m.ident[:],
                                                       hs[:, j % 2, c, q * BANK:(q + 1) * BANK], start=False,
                                                       stop=False, skip_group_check=True)
                            ins.then_inc(s["ss_acc"], 1)

                    rows(0, 0)
                    with pe.Fori(0, NST // 2 - 1) as pair:
                        n = pair * 2
                        for j in range(2):
                            rows(n, j + 1)
                            add_state(n, j)
                    rows(0, NST - 1)
                    add_state(0, NST - 2)
                    add_state(0, NST - 1)
                    for q in range(2):
                        for t in range(4):
                            for c in range(CH):
                                pe.wait_ge(s["ss_y"], CH * (half + 1))
                                ins = nc.tensor.matmul(ps[:, q, t * P:(t + 1) * P],
                                                       y[:, c, (4 * q + t) * P:(4 * q + t + 1) * P], w.out_w[:, c, :],
                                                       start=(t == 0 and c == 0), stop=(c == CH - 1),
                                                       skip_group_check=True)
                    ins.then_inc(s["ss_o"], 1)

            @block.scalar
            def _(act):
                for half in range(HALVES):
                    for c in range(CH):
                        act.wait_ge(s["ss_xs"], CH * half + c + 1)
                        nc.scalar.activation(u[:, c, :], ps[:, 2 * c:2 * c + 2, :].rearrange("p a b -> p (a b)"),
                                             ACT.Silu, bias=w.conv_b[:, c:c + 1]).then_inc(s["ss_u"], 1)
                    for c in range(CH):
                        act.wait_ge(s["ss_res"], CH * half + c + 1)
                        nc.scalar.activation(gate[:, c, :], ps[:, 4 + 2 * c:6 + 2 * c, :].rearrange("p a b -> p (a b)"),
                                             ACT.Silu).then_inc(s["ss_gate"], 1)
                    act.wait_ge(s["ss_xd"], half + 1)
                    nc.scalar.activation(dt_in, ps[0:DTR, 0:2, :].rearrange("p a b -> p (a b)"),
                                         ACT.Copy).then_inc(s["ss_dtin"], 1)
                    act.wait_ge(s["ss_z"], half + 1)
                    for c in range(CH):
                        nc.scalar.activation(t_abs[:, c, :], ps[:, 4 + 2 * c:6 + 2 * c, :].rearrange("p a b -> p (a b)"),
                                             ACT.Abs, bias=w.dt_b[:, c:c + 1]).then_inc(s["ss_abs"], 1)
                    act.wait_ge(s["ss_abs"], CH * (half + 1))
                    nc.scalar.activation(t_abs[:], t_abs[:], ACT.Exp, scale=-1.0).then_inc(s["ss_expn"], 1)
                    act.wait_ge(s["ss_expn"], half + 1)
                    nc.scalar.activation(t_abs[:], t_abs[:], ACT.Ln, bias=1.0).then_inc(s["ss_sp"], 1)
                    base = half * NST
                    act.wait_ge(s["ss_delta"], half + 1)
                    if half == 0:
                        act.wait_ge(s["ss_pool"], 1)
                        act.sem_inc(s["ss_free"], 2)
                    with act.Fori(0, NST // 2) as pair:
                        n = pair * 2
                        for j in range(2):
                            act.wait_ge(s["ss_free"], n + (base + j + 1))
                            for c in range(CH):
                                nc.scalar.activation(
                                    da[:, j, c, :, 1:], delta[:, c, :].rearrange("p (b t) -> p b t", b=HB)[:, :, 1:],
                                    ACT.Exp, scale=w.a_log[:, c, bass.ds(n + j, 1)]).then_inc(s["ss_da"], 1)
                            act.wait_ge(s["ss_pick"], n + (base + j + 1))
                            nc.scalar.activation(bs[:, j, :], ps[:, 0:2, :].rearrange("p a b -> p (a b)"), ACT.Copy)
                            nc.scalar.activation(cs[:, j, :], ps[:, 2:4, :].rearrange("p a b -> p (a b)"),
                                                 ACT.Copy).then_inc(s["ss_rows"], 1)
                    act.wait_ge(s["ss_y"], CH * (half + 1))


def lora_ffn(nc, m, name, prefetch=None):
    w = m.w
    with ExitStack() as own:
        def sb(n, shape, dt=F32):
            return own.enter_context(nc.sbuf_tensor(f"{name}_{n}", shape, dt))

        logits = sb("logits", [P, TILES, EXP])
        down = sb("lora_down", [P, TILES, ER])
        best = sb("best", [P, TILES])
        hot = sb("hot", [P, TILES, EXP])
        order = sb("order", [P, EXP])
        downt = sb("lora_down_t", [ER, TOK])
        h = sb("h", [P, 2, FT, BANK])
        k = sems(nc, own, "order g ev st hot dt dtc hp h o x", f"{name}_")
        ps = m.ps

        def xt(c0, n):
            return m.xt[:, c0 // SEQ, PAD + c0 % SEQ:PAD + c0 % SEQ + n]

        with nc.Block() as block:
            if prefetch:
                @block.sync
                def _(sp):
                    prefetch(sp)

            @block.gpsimd
            def _(pool):
                nc.gpsimd.iota(order[:], [[-1, EXP]], base=EXP, channel_multiplier=0,
                               allow_small_or_imprecise_dtypes=True).then_inc(k["order"], 1)
                nc.gpsimd.tensor_tensor(m.x[:], m.x[:], w.wo_b[:].rearrange("p (a d) -> p a d", a=1)
                                        .to_broadcast([P, TILES, DIM]), ALU.add).then_inc(k["order"], 1)

            def second(pe, g):
                pe.wait_ge(k["h"], FT * (g + 1))
                if g >= 2:
                    pe.wait_ge(k["x"], g - 1)
                for t in range(GT):
                    for f in range(FT):
                        ins = nc.tensor.matmul(ps[:, 6 + g % 2, t * P:(t + 1) * P], h[:, g % 2, f, t * P:(t + 1) * P],
                                               w.wo[:, f, :], start=(t == 0 and f == 0), stop=(f == FT - 1),
                                               skip_group_check=True)
                ins.then_inc(k["o"], 1)

            @block.tensor
            def _(pe):
                for t in range(TILES):
                    ins = nc.tensor.matmul(ps[:, t // 8, (t % 8) * 64:(t % 8) * 64 + EXP + ER], xt(t * P, P), w.gate[:],
                                           start=(t % 8 == 0), stop=True, skip_group_check=True)
                ins.then_inc(k["g"], 1)
                pe.wait_ge(k["hot"], 1)
                for t in range(TILES):
                    ins = nc.tensor.transpose(ps[0:ER, 2 + t // 4, (t % 4) * P:(t % 4 + 1) * P], down[:, t, :], m.ident[:])
                ins.then_inc(k["dt"], 1)
                pe.wait_ge(k["dtc"], 1)
                for g in range(GROUPS):
                    for f in range(FT):
                        n = g * FT + f
                        if n >= 3:
                            pe.wait_ge(k["h"], n - 2)
                        bank = 2 + n % 3
                        nc.tensor.matmul(ps[:, bank, :], w.wi[:, f * P:(f + 1) * P],
                                         m.xt[:, 2 * g:2 * g + 2, PAD:], start=True, stop=False)
                        nc.tensor.matmul(ps[:, bank, :], w.lora_b[:, f * P:(f + 1) * P],
                                         downt[:, g * BANK:(g + 1) * BANK], start=False,
                                         stop=True).then_inc(k["hp"], 1)
                    if g:
                        second(pe, g - 1)
                second(pe, GROUPS - 1)

            @block.scalar
            def _(act):
                act.wait_ge(k["dt"], 1)
                nc.scalar.activation(downt[:], ps[0:ER, 2:6, :].rearrange("p a b -> p (a b)"),
                                     ACT.Copy).then_inc(k["dtc"], 1)
                for g in range(GROUPS):
                    for f in range(FT):
                        n = g * FT + f
                        act.wait_ge(k["hp"], n + 1)
                        if g >= 2 and f == 0:
                            act.wait_ge(k["o"], g - 1)
                        nc.scalar.activation(h[:, g % 2, f, :], ps[:, 2 + n % 3, :], ACT.Relu,
                                             bias=w.wi_b[:, f:f + 1]).then_inc(k["h"], 1)

            def first_of_max(nc, dve, m, k, logits, best, hot, order, ps, bias):
                dve.wait_ge(k["g"], 1)
                both = ps[:, 0:2, :].rearrange("p a (t e) -> p (a t) e", e=64)
                nc.vector.tensor_copy(down[:], both[:, :, EXP:EXP + ER])
                nc.vector.tensor_tensor(logits[:], both[:, :, 0:EXP],
                                        bias[:].rearrange("p (a e) -> p a e", a=1).to_broadcast([P, TILES, EXP]),
                                        ALU.add).then_inc(k["st"], 1)
                pick_first(nc, dve, k["st"], 1, k["order"], logits, best, hot, order)

            @block.vector
            def _(dve):
                first_of_max(nc, dve, m, k, logits, best, hot, order, ps, w.gate_b)
                nc.vector.tensor_tensor(
                    down[:].rearrange("p t (e r) -> p t e r", e=EXP), down[:].rearrange("p t (e r) -> p t e r", e=EXP),
                    hot[:].rearrange("p t (e r) -> p t e r", r=1).to_broadcast([P, TILES, EXP, RANK]),
                    ALU.mult).then_inc(k["hot"], 1)
                dve.wait_ge(k["order"], 2)
                for g in range(GROUPS):
                    dve.wait_ge(k["o"], g + 1)
                    xg = m.x[:, g * GT:(g + 1) * GT, :].rearrange("p t d -> p (t d)")
                    nc.vector.tensor_tensor(xg, xg, ps[:, 6 + g % 2, :], ALU.add).then_inc(k["x"], 1)


def pick_first(nc, dve, step, n, order_ready, logits, best, hot, order):
    wide = [P, TILES, EXP]

    def over(t):
        return t[:].rearrange("p (t a) -> p t a", a=1).to_broadcast(wide)

    dve.wait_ge(step, n)
    nc.vector.tensor_reduce(best[:], logits[:], AX.X, ALU.max).then_inc(step, 1)
    dve.wait_ge(step, n + 1)
    nc.vector.tensor_tensor(hot[:], logits[:], over(best), ALU.is_equal).then_inc(step, 1)
    dve.wait_ge(step, n + 2)
    dve.wait_ge(order_ready, 1)
    nc.vector.tensor_tensor(hot[:], hot[:], order[:].rearrange("p (a e) -> p a e", a=1).to_broadcast(wide),
                            ALU.mult).then_inc(step, 1)
    dve.wait_ge(step, n + 3)
    nc.vector.tensor_reduce(best[:], hot[:], AX.X, ALU.max).then_inc(step, 1)
    dve.wait_ge(step, n + 4)
    nc.vector.tensor_tensor(hot[:], hot[:], over(best), ALU.is_equal).then_inc(step, 1)
    dve.wait_ge(step, n + 5)


def load_toeplitz(sp, m):
    n = DIM // TOEPLITZ_LOADS
    for c in range(TOEPLITZ_LOADS):
        src = bass.AP(m.kernel_dram.tensor, c * n * 2 * P, [[1, P], [2 * P, n], [1, P]])
        sp.dma_start(m.toeplitz[:, c * n:(c + 1) * n, :], src).then_inc(m.toeplitz_loaded, 16)


def long_conv(nc, m):
    w = m.w
    with ExitStack() as own:
        def sb(name, shape, dt=F32):
            return own.enter_context(nc.sbuf_tensor(name, shape, dt))

        ud = sb("lc_skip", [P, TILES, DIM])
        state = sb("lc_state", [LNST, DIM, BATCH])
        y = sb("lc_y", [P, TILES, DIM])
        back = sb("lc_reversed", [P, TILES, DIM])
        flip = sb("lc_flip", [P, P])
        k = sems(nc, own, "lc_fz lc_flip lc_bp lc_back lc_ud lc_hp lc_hc lc_yp lc_y lc_st lc_pow lc_z")
        ps = m.ps
        step = k["lc_st"]
        with nc.Block() as block:
            def row(w, i, tiles=TILES):
                return w.lc_rows[:, i:i + 1, :].to_broadcast([P, tiles, DIM])

            @block.gpsimd
            def _(pool):
                nc.gpsimd.memset(flip[:], 0.0).then_inc(k["lc_fz"], 1)
                pool.wait_ge(k["lc_fz"], 1)
                nc.gpsimd.affine_select(out=flip[:], in_=flip[:], compare_op=ALU.not_equal, fill=1.0, base=1 - P,
                                        pattern=[[1, P]], channel_multiplier=1).then_inc(k["lc_flip"], 1)
                nc.gpsimd.tensor_tensor(ud[:], m.xn[:], row(w, 0), ALU.mult).then_inc(k["lc_ud"], 1)
                pool.wait_ge(step, 7)
                nc.gpsimd.tensor_tensor(m.rstd[:], m.ve[:], m.mhalf[:], ALU.pow).then_inc(k["lc_pow"], 1)

            @block.tensor
            def _(pe):
                first = m.xn[:].rearrange("p (b h) d -> p h b d", h=2)[:, 0]
                for i in range(2):
                    ins = nc.tensor.matmul(ps[0:LNST, 4 + i, :], m.lc_powt[:], first[:, 4 * i:4 * i + 4, :], start=True, stop=True)
                ins.then_inc(k["lc_hp"], 1)
                pe.wait_ge(k["lc_flip"], 1)
                for g in range(GROUPS):
                    nc.tensor.matmul(ps[:, g, :], flip[:], m.xn[:, g * GT:(g + 1) * GT, :], start=True,
                                     stop=True).then_inc(k["lc_bp"], 1)
                pe.wait_ge(m.toeplitz_loaded, 16 * TOEPLITZ_LOADS)
                pe.wait_ge(k["lc_back"], GROUPS)
                for d in range(DIM):
                    ins = nc.tensor.matmul(ps[:, d // 32, (d % 32) * TILES:(d % 32 + 1) * TILES], m.toeplitz[:, d, :],
                                           back[:, :, d], start=(d % 32 == 0), stop=False, skip_group_check=True)
                pe.wait_ge(k["lc_hc"], 1)
                for q in range(4):
                    out = ps[:, q, :].rearrange("p (d b h) -> p d b h", b=BATCH, h=2)[:, :, :, 1]
                    ins = nc.tensor.matmul(out, m.lc_pow[:, 1:], state[:, 32 * q:32 * q + 32, :], start=False,
                                           stop=True, skip_group_check=True)
                ins.then_inc(k["lc_yp"], 1)

            @block.scalar
            def _(act):
                for g in range(GROUPS):
                    act.wait_ge(k["lc_bp"], g + 1)
                    nc.scalar.activation(back[:, g * GT:(g + 1) * GT, :].rearrange("p t d -> p (t d)"), ps[:, g, :],
                                         ACT.Copy).then_inc(k["lc_back"], 1)

            @block.vector
            def _(dve):
                dve.wait_ge(k["lc_hp"], 1)
                src = ps[0:LNST, 4:6, :].rearrange("n a (b d) -> n d (a b)", b=4)
                nc.vector.tensor_tensor(state[:], src, w.lc_ct[:].rearrange("n (d a) -> n d a", a=1)
                                        .to_broadcast([LNST, DIM, BATCH]), ALU.mult).then_inc(k["lc_hc"], 1)
                dve.wait_ge(k["lc_ud"], 1)
                dve.wait_ge(k["lc_yp"], 1)
                for q in range(4):
                    ins = nc.vector.tensor_tensor(
                        y[:, :, 32 * q:32 * q + 32], ps[:, q, :].rearrange("p (d t) -> p t d", t=TILES),
                        ud[:, :, 32 * q:32 * q + 32], ALU.add)
                ins.then_inc(step, 1)
                dve.wait_ge(step, 1)
                nc.vector.tensor_tensor(y[:], y[:], row(w, 1), ALU.mult).then_inc(step, 1)
                dve.wait_ge(step, 2)
                y0 = y[0:1].rearrange("p (b h) d -> p h b d", h=2)[:, 0]
                nc.vector.tensor_tensor(y0, y0, w.lc_rows[0:1, 2:3, :].to_broadcast([1, BATCH, DIM]),
                                        ALU.add).then_inc(step, 1)
                dve.wait_ge(step, 3)
                for t in range(TILES):
                    ins = nc.vector.bn_stats(m.stats[:, t, :], y[:, t, :])
                ins.then_inc(step, 1)
                dve.wait_ge(step, 4)
                for t in range(TILES):
                    ins = nc.vector.bn_aggr(m.mv[:, t, :], m.stats[:, t, :])
                ins.then_inc(step, 1)
                dve.wait_ge(step, 5)
                nc.vector.tensor_scalar(m.ve[:], m.mv[:, :, 1], EPS, None, ALU.add).then_inc(step, 2)
                dve.wait_ge(k["lc_pow"], 1)
                for t in range(TILES):
                    ins = nc.vector.tensor_scalar(y[:, t, :], y[:, t, :], m.mv[:, t, 0:1], m.rstd[:, t:t + 1],
                                                  ALU.subtract, ALU.mult)
                ins.then_inc(step, 1)
                dve.wait_ge(step, 8)
                nc.vector.tensor_tensor(y[:], y[:], row(w, 3), ALU.mult).then_inc(step, 1)
                dve.wait_ge(step, 9)
                nc.vector.tensor_tensor(y[:], y[:], row(w, 4), ALU.add).then_inc(step, 1)
                dve.wait_ge(step, 10)
                nc.vector.tensor_tensor(m.x[:], m.x[:], y[:], ALU.add)


def allowed_pairs():
    pos = np.arange(SEQ)
    chunk = pos // CHUNK_FRAMES
    return (chunk[None, :] <= chunk[:, None]) | (pos[None, :] <= pos[:, None] + LOOKAHEAD)


def attention(nc, m, name, a, rope):
    JS, GS = 4, HEADS // 4
    KT = SEQ // P
    PARTS = 3
    STACK = PARTS * PARTS * HD
    PUT, GOT = 16 * 2 * PARTS, 16 * (PARTS + 1)
    SCALE = float(HD) ** -0.5
    MASKED = not rope
    hidden = ~allowed_pairs()
    first_key = [int(np.flatnonzero(hidden[i * P:(i + 1) * P].any(0))[0]) for i in range(KT)]
    end_query = [int(np.flatnonzero(hidden[:, i * P:(i + 1) * P].any(1))[-1]) + 1 for i in range(KT)]
    with ExitStack() as own:
        def sb(n, shape, dt=F32):
            return own.enter_context(nc.sbuf_tensor(f"{name}_{n}", shape, dt))

        xb = sb("xb", [P, 2, SEQ])
        t1 = sb("rot1", [P, 2, SEQ])
        t2 = sb("rot2", [P, 2, SEQ])
        qk = sb("qk", [P, 2, SEQ])
        qk_rest = sb("qk_rest", [P, 2, SEQ])
        parts = sb("qk_parts", [P, PARTS, 2, SEQ], BF16)
        q_stack = sb("q_stack", [STACK, 2, HEADS, SEQ], BF16)
        k_stack = sb("k_stack", [STACK, 2, HEADS, SEQ], BF16)
        v = sb("v", [P, 2, KT, HEADS, 32])
        mx = sb("max", [P, KT, GS])
        res = sb("max_rest", [P, KT, GS])
        split = sb("max_split", [P, KT, 3, GS], BF16)
        mt = sb("max_t", [P, SEQ], BF16)
        e = sb("e", [P, 2, KT, GS, SEQ])
        o_heads = sb("o_heads", [P, SEQ])
        rs = sb("rsum", [P, KT, GS])
        on = sb("o", [P, 2, KT, DIM])
        ont = sb("o_t", [P, SEQ])
        k = sems(nc, own, "part vz bias xb qp kp vp qd kd p1 p2 pt put got v sq mx ms mtp mtc st ex pv oc to rs nm tu tc out xa",
                 f"{name}_")
        scratch = nc.dram_tensor(f"{name}_parts", (2, PARTS, HD, HEADS, SEQ), BF16, kind="Internal").ap()
        ps = m.ps
        SQ, ST, OB, MISC = (0, 1), (2, 4), 6, 7
        misc = ps[:, MISC, :]
        mtp = ps[0:3 * GS, MISC, 0:SEQ // 2].bitcast(BF16)
        o_psum = ps[:, OB, 0:SEQ]
        turned = ps[:, OB, SEQ:].rearrange("p (i g c) -> p i g c", i=KT, g=GS)

        def pe_qk(pe, b, r, ws, done):
            for n, wt in enumerate(ws):
                ins = nc.tensor.matmul(misc[:, n * SEQ:(n + 1) * SEQ], wt[:], xb[:, r, :], start=(n == 0), stop=True,
                                       skip_group_check=True)
            ins.then_inc(done, 1)

        def pe_q(pe, b, r):
            pe.wait_ge(k["xb"], b + 1)
            pe_qk(pe, b, r, (a.wq1, a.wq2) if rope else (a.wq1,), k["qp"])

        def pe_k(pe, b, r):
            pe_qk(pe, b, r, (a.wk1, a.wk2) if rope else (a.wk1,), k["kp"])

        def pe_v(pe, b, r):
            for i in range(KT):
                ins = nc.tensor.matmul(misc[:, i * P:(i + 1) * P], xb[:, r, i * P:(i + 1) * P], a.wv[:],
                                       start=(i == 0), stop=True, skip_group_check=True)
            ins.then_inc(k["vp"], 1)

        def pe_sq(pe, s, j, r, i):
            qt, pair = i // 2, i % 2
            if not (isinstance(s, int) and s == 0 and i < 2):
                pe.wait_ge(k["mx"], s * 4 + i - 1)
            bank = ps[:, SQ[i % 2], :]
            if MASKED:
                lo = first_key[qt]
                nc.tensor.matmul(bank.rearrange("p (c t) -> p c t", c=2)[:, :, lo:], m.identb[:],
                                 a.mask_q[:, qt:qt + 1, lo:].to_broadcast([P, 2, SEQ - lo]), start=True, stop=False,
                                 skip_group_check=True)
            for c in range(2):
                h = 4 * j + 2 * pair + c
                ins = nc.tensor.matmul(bank[:, c * SEQ:(c + 1) * SEQ], q_stack[:, r, h, qt * P:(qt + 1) * P],
                                       k_stack[:, r, h, :], start=(c == 0 and not MASKED), stop=True,
                                       skip_group_check=True)
            ins.then_inc(k["sq"], 1)

        def pe_mt(pe, s):
            pe.wait_ge(k["ms"], s + 1)
            for i in range(KT):
                ins = nc.tensor.transpose(mtp[:, i * P:(i + 1) * P], split[:, i, :, :].rearrange("p c g -> p (c g)"),
                                          m.identb[:])
            ins.then_inc(k["mtp"], 1)

        def pe_st(pe, s, j, r, i):
            if not (isinstance(s, int) and s == 0):
                pe.wait_ge(k["ex"], s * KT + i - 1)
            banks = ps[:, ST[i]:ST[i] + 2, :]
            if MASKED:
                hi = end_query[i]
                for c in range(2):
                    nc.tensor.matmul(banks[:, c, :].rearrange("p (g t) -> p g t", g=2)[:, :, 0:hi], m.identb[:],
                                     a.mask_k[:, i:i + 1, 0:hi].to_broadcast([P, 2, hi]), start=True, stop=False,
                                     skip_group_check=True)
            for g in range(GS):
                nc.tensor.matmul(banks[:, g // 2, (g % 2) * SEQ:(g % 2 + 1) * SEQ], a.pick[:, g, :], mt[:],
                                 start=(g % 2 == 0 and not MASKED), stop=False, skip_group_check=True)
            for g in range(GS):
                h = 4 * j + g
                ins = nc.tensor.matmul(banks[:, g // 2, (g % 2) * SEQ:(g % 2 + 1) * SEQ],
                                       k_stack[:, r, h, i * P:(i + 1) * P], q_stack[:, r, h, :], start=False, stop=True,
                                       skip_group_check=True)
            ins.then_inc(k["st"], 1)

        def pe_pv(pe, s, j, r):
            if not (isinstance(s, int) and s == 0):
                pe.wait_ge(k["nm"], s)
            for i in range(KT):
                pe.wait_ge(k["ex"], s * KT + i + 1)
                for g in range(GS):
                    ins = nc.tensor.matmul(o_psum[32 * g:32 * g + 32, :], v[:, r, i, 4 * j + g, :],
                                           e[:, j % 2, i, g, :], start=(i == 0), stop=(i == KT - 1),
                                           skip_group_check=True)
            ins.then_inc(k["pv"], 1)

        def pe_to(pe, s):
            pe.wait_ge(k["oc"], s + 1)
            for i in range(KT):
                ins = nc.tensor.transpose(ps[:, OB, SEQ + i * P:SEQ + (i + 1) * P], o_heads[:, i * P:(i + 1) * P],
                                          m.ident[:])
            ins.then_inc(k["to"], 1)

        def pe_turn(pe, b, r):
            pe.wait_ge(k["nm"], b * JS + JS)
            for i in range(KT):
                ins = nc.tensor.transpose(misc[:, i * P:(i + 1) * P], on[:, r, i, :], m.ident[:])
            ins.then_inc(k["tu"], 1)

        def pe_out(pe, b):
            pe.wait_ge(k["tc"], b + 1)
            for i in range(KT):
                ins = nc.tensor.matmul(misc[:, i * P:(i + 1) * P], ont[:, i * P:(i + 1) * P], a.wo[:],
                                       start=(i == 0), stop=True, skip_group_check=True)
            ins.then_inc(k["out"], 1)

        def pe_step(pe, b, j, r, first, last, project=False):
            s = b * JS + j
            more = not (last and j == JS - 1)
            nj, nr = ((j + 1), r) if j < JS - 1 else (0, 1 - r)
            project_v, finish = j == 1 and not last, j == 2 and not first
            if more:
                if j == JS - 1:
                    pe.wait_ge(k["got"], b * GOT + 2 * GOT)
                pe_sq(pe, s + 1, nj, nr, 0)
                pe_sq(pe, s + 1, nj, nr, 1)
            pe.wait_ge(k["mtc"], s + 1)
            if project:
                pe_q(pe, b + 2, r)
            if project_v:
                pe_v(pe, b + 1, 1 - r)
            if finish:
                pe_turn(pe, b - 1, 1 - r)
            pe_st(pe, s, j, r, 0)
            if more:
                pe_sq(pe, s + 1, nj, nr, 2)
                pe_sq(pe, s + 1, nj, nr, 3)
            if not (first and j <= 1):
                pe_to(pe, s - 2)
            pe_st(pe, s, j, r, 1)
            if project:
                pe.wait_ge(k["qd"], b + 3)
                pe_k(pe, b + 2, r)
            if finish:
                pe_out(pe, b - 1)
            if not (first and j == 0):
                if j == 1:
                    pe.wait_ge(k["v"], b + 1)
                pe_pv(pe, s - 1, (j - 1) % JS, r if j > 0 else 1 - r)
            if more:
                if project:
                    pe.wait_ge(k["kd"], b + 3)
                if project_v:
                    pe.wait_ge(k["v"], b + 2)
                if finish:
                    pe.wait_ge(k["xa"], b)
                pe_mt(pe, s + 1)

        def window(step, eng, b, r, first, last):
            if not first:
                step(eng, b - 1, JS - 1, 1 - r, False, False, project=not last)
            for j in range(JS - 1):
                step(eng, b, j, r, first, last)

        def dve_qk(dve, b, n, read):
            if not (isinstance(b, int) and b == 0):
                dve.wait_ge(k["pt"], b)
            if rope:
                nc.vector.tensor_tensor(t1[:, n, :], misc[:, 0:SEQ], a.cos[:], ALU.mult)
                nc.vector.tensor_tensor(t2[:, n, :], misc[:, SEQ:], a.sin[:], ALU.mult).then_inc(read, 1)
            else:
                if not (isinstance(b, int) and b == 0):
                    dve.wait_ge(k["put"], b * PUT)
                for dst in (qk[:, n, :], parts[:, 0, n, :]):
                    if n == 0:
                        ins = nc.vector.tensor_scalar(dst, misc[:, 0:SEQ], a.bq[:, 0:1], None, ALU.add)
                    else:
                        ins = nc.vector.tensor_copy(dst, misc[:, 0:SEQ])
                ins.then_inc(read, 1)

        def dve_q(dve, b):
            dve.wait_ge(k["qp"], b + 1)
            dve_qk(dve, b, 0, k["qd"])

        def dve_k(dve, b):
            dve.wait_ge(k["kp"], b + 1)
            dve_qk(dve, b, 1, k["kd"])

        def dve_v(dve, b, r):
            dve.wait_ge(k["vp"], b + 1)
            if not (isinstance(b, int) and b <= 1):
                dve.wait_ge(k["pv"], (b - 1) * JS)
            for i in range(KT):
                ins = nc.vector.tensor_tensor(
                    v[:, r, i, :, 0:HD], misc[:, i * P:(i + 1) * P].rearrange("p (h e) -> p h e", e=HD),
                    a.bv[:].rearrange("p (h e) -> p h e", e=HD), ALU.add)
            ins.then_inc(k["v"], 1)

        def dve_max(dve, s, i):
            qt, pair = i // 2, i % 2
            dve.wait_ge(k["sq"], s * 4 + i + 1)
            if i == 0 and not (isinstance(s, int) and s == 0):
                dve.wait_ge(k["ms"], s)
            nc.vector.tensor_reduce(mx[:, qt, 2 * pair:2 * pair + 2],
                                    ps[:, SQ[i % 2], :].rearrange("p (c t) -> p c t", c=2), AX.X,
                                    ALU.max).then_inc(k["mx"], 1)

        def dve_split(dve, s):
            if not (isinstance(s, int) and s == 0):
                dve.wait_ge(k["mtp"], s)
            dve.wait_ge(k["mx"], s * 4 + 4)
            nc.vector.tensor_scalar(split[:, :, 0, :], mx[:], -1.0, None, ALU.mult).then_inc(k["part"], 1)
            dve.wait_ge(k["part"], s * 3 + 1)
            nc.vector.scalar_tensor_tensor(out=res[:], in0=mx[:], scalar=-1.0, in1=split[:, :, 0, :], op0=ALU.mult,
                                           op1=ALU.subtract).then_inc(k["part"], 1)
            dve.wait_ge(k["part"], s * 3 + 2)
            nc.vector.tensor_copy(split[:, :, 1, :], res[:]).then_inc(k["part"], 1)
            dve.wait_ge(k["part"], s * 3 + 3)
            nc.vector.tensor_tensor(split[:, :, 2, :], res[:], split[:, :, 1, :], ALU.subtract)\
                .then_inc(k["ms"], 1)

        def dve_norm(dve, s, j, r):
            dve.wait_ge(k["to"], s + 1)
            nc.vector.reciprocal(rs[:], turned[:, :, :, HD]).then_inc(k["rs"], 1)
            dve.wait_ge(k["rs"], s + 1)
            nc.vector.tensor_tensor(on[:, r, :, 32 * j:32 * j + 32].rearrange("p i (g e) -> p i g e", g=GS),
                                    turned[:, :, :, 0:HD],
                                    rs[:].rearrange("p i (g a) -> p i g a", a=1).to_broadcast([P, KT, GS, HD]),
                                    ALU.mult).then_inc(k["nm"], 1)

        def dve_add(dve, b):
            dve.wait_ge(k["out"], b + 1)
            dve.wait_ge(k["bias"], 1)
            xs = m.x[:, bass.ds(b * 2, 2), :] if not isinstance(b, int) else m.x[:, 2 * b:2 * b + 2, :]
            nc.vector.tensor_tensor(xs, xs, misc[:, 0:SEQ].rearrange("p (t d) -> p t d", t=2),
                                    ALU.add).then_inc(k["xa"], 1)

        def dve_step(dve, b, j, r, first, last, project=False):
            s = b * JS + j
            more = not (last and j == JS - 1)
            if more:
                dve_max(dve, s + 1, 0)
                dve_max(dve, s + 1, 1)
            if project:
                dve_q(dve, b + 2)
            if j == 1 and not last and not rope:
                dve_v(dve, b + 1, 1 - r)
            if more:
                dve_max(dve, s + 1, 2)
                dve_max(dve, s + 1, 3)
            if not (first and j <= 1):
                dve_norm(dve, s - 2, (j - 2) % JS, r if j >= 2 else 1 - r)
            if more:
                dve_split(dve, s + 1)
            if project:
                dve_k(dve, b + 2)
            if j == 2 and not first:
                dve_add(dve, b - 1)

        def act_mt(act, s):
            act.wait_ge(k["mtp"], s + 1)
            nc.scalar.activation(mt[0:3 * GS, :], mtp, ACT.Copy).then_inc(k["mtc"], 1)

        def act_v(act, b, r):
            act.wait_ge(k["vp"], b + 1)
            if not (isinstance(b, int) and b <= 1):
                act.wait_ge(k["pv"], (b - 1) * JS)
            nc.scalar.activation(v[:, r, :, :, 0:HD], misc[:, 0:SEQ].rearrange("p (i h e) -> p i h e", i=KT, e=HD),
                                 ACT.Copy).then_inc(k["v"], 1)

        def act_exp(act, s, j):
            for i in range(KT):
                act.wait_ge(k["st"], s * KT + i + 1)
                if i == 0 and not (isinstance(s, int) and s <= 1):
                    act.wait_ge(k["pv"], s - 1)
                nc.scalar.activation(e[:, j % 2, i, :, :].rearrange("p g t -> p (g t)"),
                                     ps[:, ST[i]:ST[i] + 2, :].rearrange("p a b -> p (a b)"), ACT.Exp,
                                     scale=SCALE).then_inc(k["ex"], 1)

        def act_oc(act, s):
            act.wait_ge(k["pv"], s + 1)
            if not (isinstance(s, int) and s == 0):
                act.wait_ge(k["to"], s)
            nc.scalar.activation(o_heads[:], o_psum, ACT.Copy).then_inc(k["oc"], 1)

        def act_turn(act, b):
            act.wait_ge(k["tu"], b + 1)
            nc.scalar.activation(ont[:], misc[:, 0:SEQ], ACT.Copy).then_inc(k["tc"], 1)

        def act_step(act, b, j, r, first, last, project=False):
            s = b * JS + j
            if j == 1 and not last and rope:
                act_v(act, b + 1, 1 - r)
            if j == 2 and not first:
                act_turn(act, b - 1)
            act_exp(act, s, j)
            if not (first and j == 0):
                act_oc(act, s - 1)
            if not (last and j == JS - 1):
                act_mt(act, s + 1)

        def pool_xb(pool, b, r):
            if not (isinstance(b, int) and b <= 1):
                pool.wait_ge(k["vp"], b - 1)
            src = m.xt[:, b, PAD:] if isinstance(b, int) else \
                m.xt[:, bass.ds(b, 1), PAD:].rearrange("p a t -> p (a t)")
            nc.gpsimd.tensor_copy(xb[:, r, :], src).then_inc(k["xb"], 1)

        def pool_parts(pool, b):
            pool.wait_ge(k["kd"], b + 1)
            if not (isinstance(b, int) and b == 0):
                pool.wait_ge(k["put"], b * PUT)
            if rope:
                nc.gpsimd.tensor_tensor(parts[:, 0, :, :], t1[:], t2[:], ALU.add)
                nc.gpsimd.tensor_tensor(qk[:], t1[:], t2[:], ALU.add).then_inc(k["p1"], 1)
                pool.wait_ge(k["p1"], b + 1)
            nc.gpsimd.tensor_tensor(parts[:, 1, :, :], qk[:], parts[:, 0, :, :], ALU.subtract)
            nc.gpsimd.tensor_tensor(qk_rest[:], qk[:], parts[:, 0, :, :], ALU.subtract).then_inc(k["p2"], 1)
            pool.wait_ge(k["p2"], b + 1)
            nc.gpsimd.tensor_tensor(parts[:, 2, :, :], qk_rest[:], parts[:, 1, :, :], ALU.subtract)\
                .then_inc(k["pt"], 1)

        def sp_stacks(sp, b, r):
            sp.wait_ge(k["pt"], b + 1)
            if isinstance(b, int) and b == 1:
                sp.wait_ge(k["got"], GOT)
            for n in range(2):
                for c in range(PARTS):
                    sp.dma_start(scratch[n, c].rearrange("d h t -> h d t"), parts[:, c, n, :]).then_inc(k["put"], 16)
            sp.wait_ge(k["put"], b * PUT + PUT)
            if not (isinstance(b, int) and b <= 1):
                sp.wait_ge(k["put"], PUT)
                sp.wait_ge(k["st"], (b - 1) * JS * KT)
            part, row = HD * HEADS * SEQ, HEADS * SEQ
            k_part = bass.AP(scratch.tensor, scratch[1].offset, [[0, PARTS], [row, PARTS * HD], [1, row]])
            for c in range(PARTS):
                q_part = bass.AP(scratch.tensor, scratch[0, c].offset, [[0, PARTS], [row, HD], [1, row]])
                rows = slice(c * PARTS * HD, (c + 1) * PARTS * HD)
                sp.dma_start(q_stack[rows, r, :, :].rearrange("p h t -> p (h t)"), q_part).then_inc(k["got"], 16)
            sp.dma_start(k_stack[:, r, :, :].rearrange("p h t -> p (h t)"), k_part).then_inc(k["got"], 16)

        PAIRS = (BATCH - 2) // 2
        with nc.Block() as block:
            @block.sync
            def _(sp):
                sp_stacks(sp, 0, 0)
                sp_stacks(sp, 1, 1)
                with sp.Fori(0, PAIRS) as pair:
                    sp_stacks(sp, pair * 2 + 2, 0)
                    sp_stacks(sp, pair * 2 + 3, 1)
                sp.wait_ge(k["got"], BATCH * GOT)

            @block.tensor
            def _(pe):
                pe_q(pe, 0, 0)
                pe.wait_ge(k["qd"], 1)
                pe_k(pe, 0, 0)
                pe.wait_ge(k["kd"], 1)
                pe_v(pe, 0, 0)
                pe.wait_ge(k["v"], 1)
                pe_q(pe, 1, 1)
                pe.wait_ge(k["qd"], 2)
                pe_k(pe, 1, 1)
                pe.wait_ge(k["got"], GOT)
                for i in range(4):
                    pe_sq(pe, 0, 0, 0, i)
                pe.wait_ge(k["kd"], 2)
                pe_mt(pe, 0)
                window(pe_step, pe, 0, 0, True, False)
                with pe.Fori(0, PAIRS) as pair:
                    window(pe_step, pe, pair * 2 + 1, 1, False, False)
                    window(pe_step, pe, pair * 2 + 2, 0, False, False)
                window(pe_step, pe, BATCH - 1, 1, False, True)
                pe_step(pe, BATCH - 1, JS - 1, 1, False, True)
                pe_to(pe, BATCH * JS - 2)
                pe_pv(pe, BATCH * JS - 1, JS - 1, 1)
                pe_to(pe, BATCH * JS - 1)
                pe_turn(pe, BATCH - 1, 1)
                pe_out(pe, BATCH - 1)

            @block.vector
            def _(dve):
                nc.vector.memset(mt[:], 0.0)
                nc.vector.memset(v[:], 0.0).then_inc(k["vz"], 1)
                dve.wait_ge(k["vz"], 1)
                nc.vector.memset(v[:, :, :, :, HD:HD + 1], 1.0).then_inc(k["vz"], 1)
                dve_q(dve, 0)
                dve_k(dve, 0)
                dve.wait_ge(k["vz"], 2)
                if not rope:
                    dve_v(dve, 0, 0)
                dve_q(dve, 1)
                dve_k(dve, 1)
                for i in range(4):
                    dve_max(dve, 0, i)
                dve_split(dve, 0)
                window(dve_step, dve, 0, 0, True, False)
                with dve.Fori(0, PAIRS) as pair:
                    window(dve_step, dve, pair * 2 + 1, 1, False, False)
                    window(dve_step, dve, pair * 2 + 2, 0, False, False)
                window(dve_step, dve, BATCH - 1, 1, False, True)
                dve_step(dve, BATCH - 1, JS - 1, 1, False, True)
                dve_norm(dve, BATCH * JS - 2, JS - 2, 1)
                dve_norm(dve, BATCH * JS - 1, JS - 1, 1)
                dve_add(dve, BATCH - 1)

            @block.scalar
            def _(act):
                act.wait_ge(k["vz"], 2)
                if rope:
                    act_v(act, 0, 0)
                act_mt(act, 0)
                window(act_step, act, 0, 0, True, False)
                with act.Fori(0, PAIRS) as pair:
                    window(act_step, act, pair * 2 + 1, 1, False, False)
                    window(act_step, act, pair * 2 + 2, 0, False, False)
                window(act_step, act, BATCH - 1, 1, False, True)
                act_step(act, BATCH - 1, JS - 1, 1, False, True)
                act_oc(act, BATCH * JS - 1)
                act_turn(act, BATCH - 1)

            @block.gpsimd
            def _(pool):
                pool_xb(pool, 0, 0)
                pool_xb(pool, 1, 1)
                pool_parts(pool, 0)
                nc.gpsimd.tensor_tensor(m.x[:], m.x[:], a.bo[:].rearrange("p (a d) -> p a d", a=1)
                                        .to_broadcast([P, TILES, DIM]), ALU.add).then_inc(k["bias"], 1)
                pool_parts(pool, 1)
                with pool.Fori(0, PAIRS) as pair:
                    pool_xb(pool, pair * 2 + 2, 0)
                    pool_parts(pool, pair * 2 + 2)
                    pool_xb(pool, pair * 2 + 3, 1)
                    pool_parts(pool, pair * 2 + 3)


def batch_attention(nc, m, name):
    w = m.w
    SCALE = float(MHD) ** -0.5
    with ExitStack() as own:
        def sb(n, shape, dt=F32):
            return own.enter_context(nc.sbuf_tensor(f"{name}_{n}", shape, dt))

        qt = sb("q_t", [P, BATCH, SEQ])
        km = sb("k_t", [P, MH, BATCH, SEQ])
        kb = sb("k_bias", [P, MH])
        ot = sb("o_t", [P, BATCH, SEQ])
        xg = sb("x_group", [P, 2, P])
        qg = sb("q_group", [P, 2, P])
        v = sb("v", [P, 2, P])
        nb = sb("neg_max", [P, 2, MH])
        sums = sb("sums", [P, 2, MH])
        rec = sb("rec", [P, 2, MH])
        pr = sb("probs", [P, 2, MH, P])
        pt = sb("probs_t", [P, 2, MH, P])
        y = m.xn
        k = sems(nc, own, "qp qe kb cp sc vp ve mx nb ex rc nr tp tc pv oe pr r1 st pw nn yt rs gb", f"{name}_")
        ps = m.ps
        SC, VB, PT, OT = 0, 2, 4, 6

        def cols(t, g):
            if isinstance(g, int):
                return t[:, :, g * PG:(g + 1) * PG]
            return t[:, :, bass.ds(g * PG, PG)]

        def pool_copy(pool, g, r):
            if not (isinstance(g, int) and g <= 1):
                pool.wait_ge(k["sc"], g - 1)
            for dst, src in ((xg, m.xt[:, :, PAD:]), (qg, qt)):
                ins = nc.gpsimd.tensor_copy(dst[:, r, :].rearrange("p (b t) -> p b t", b=BATCH), cols(src, g))
            ins.then_inc(k["cp"], 1)

        def pe_scores(pe, g, r):
            pe.wait_ge(k["cp"], g + 1)
            if not (isinstance(g, int) and g <= 1):
                pe.wait_ge(k["ve"], g - 1)
                pe.wait_ge(k["ex"], g - 1)
            nc.tensor.matmul(ps[:, VB + r, 0:P], xg[:, r, :], w.m_v[:], start=True, stop=True).then_inc(k["vp"], 1)
            nc.tensor.matmul(ps[:, SC + r, :], m.identb[:], w.m_mask[:].rearrange("p (a c) -> p a c", a=1)
                             .to_broadcast([P, MH, P]), start=True, stop=False, skip_group_check=True)
            keys = km[:, :, :, g * PG:(g + 1) * PG] if isinstance(g, int) else km[:, :, :, bass.ds(g * PG, PG)]
            nc.tensor.matmul(ps[:, SC + r, :], qg[:, r, :], keys, start=False, stop=True,
                             skip_group_check=True).then_inc(k["sc"], 1)

        def pe_turn(pe, g, r):
            pe.wait_ge(k["nr"], g + 1)
            if not (isinstance(g, int) and g <= 1):
                pe.wait_ge(k["tc"], g - 1)
            for h in range(MH):
                ins = nc.tensor.transpose(ps[:, PT + r, h * P:(h + 1) * P], pr[:, r, h, :], m.ident[:])
            ins.then_inc(k["tp"], 1)

        def pe_pv(pe, g, r):
            pe.wait_ge(k["tc"], g + 1)
            pe.wait_ge(k["ve"], g + 1)
            pe.wait_ge(k["oe"], g + 1)
            for h in range(MH):
                ins = nc.tensor.matmul(ps[MHD * h:MHD * (h + 1), OT + r, 0:P], v[:, r, MHD * h:MHD * (h + 1)],
                                       pt[:, r, h, :], start=True, stop=True)
            ins.then_inc(k["pv"], 1)

        def pe_step(pe, g, r, first, last):
            if not last:
                pe_scores(pe, g + 1, 1 - r)
            if not first:
                pe_pv(pe, g - 1, 1 - r)
            pe_turn(pe, g, r)

        def dve_max(dve, g, r):
            dve.wait_ge(k["sc"], g + 1)
            if not (isinstance(g, int) and g <= 1):
                dve.wait_ge(k["ex"], g - 1)
            nc.vector.tensor_reduce(nb[:, r, :], ps[:, SC + r, :].rearrange("p (h t) -> p h t", h=MH), AX.X,
                                    ALU.max).then_inc(k["mx"], 1)
            dve.wait_ge(k["mx"], g + 1)
            nc.vector.tensor_scalar(nb[:, r, :], nb[:, r, :], -SCALE, None, ALU.mult).then_inc(k["nb"], 1)

        def dve_norm(dve, g, r):
            dve.wait_ge(k["ex"], g + 1)
            nc.vector.reciprocal(rec[:, r, :], sums[:, r, :]).then_inc(k["rc"], 1)
            dve.wait_ge(k["rc"], g + 1)
            nc.vector.tensor_tensor(pr[:, r], pr[:, r], rec[:, r, :].rearrange("p (h a) -> p h a", a=1)
                                    .to_broadcast([P, MH, P]), ALU.mult).then_inc(k["nr"], 1)

        def dve_step(dve, g, r, last):
            if not last:
                dve_max(dve, g + 1, 1 - r)
            dve_norm(dve, g, r)

        def act_exp(act, g, r):
            act.wait_ge(k["nb"], g + 1)
            if not (isinstance(g, int) and g <= 1):
                act.wait_ge(k["tp"], g - 1)
            for h in range(MH):
                ins = nc.scalar.activation(pr[:, r, h, :], ps[:, SC + r, h * P:(h + 1) * P], ACT.Exp,
                                           bias=nb[:, r, h:h + 1], scale=SCALE, accum_out=sums[:, r, h:h + 1])
            ins.then_inc(k["ex"], 1)

        def act_v(act, g, r):
            act.wait_ge(k["vp"], g + 1)
            if not (isinstance(g, int) and g <= 1):
                act.wait_ge(k["pv"], g - 1)
            nc.scalar.activation(v[:, r, :], ps[:, VB + r, 0:P], ACT.Copy).then_inc(k["ve"], 1)

        def act_turn(act, g, r):
            act.wait_ge(k["tp"], g + 1)
            if not (isinstance(g, int) and g <= 1):
                act.wait_ge(k["pv"], g - 1)
            nc.scalar.activation(pt[:, r].rearrange("p h t -> p (h t)"), ps[:, PT + r, :], ACT.Copy)\
                .then_inc(k["tc"], 1)

        def act_out(act, g, r):
            act.wait_ge(k["pv"], g + 1)
            act.wait_ge(k["qe"], 2 * GROUPS)
            nc.scalar.activation(cols(ot, g), ps[:, OT + r, 0:P].rearrange("p (b t) -> p b t", b=BATCH), ACT.Identity,
                                 bias=w.m_bqkv[:, 2:3]).then_inc(k["oe"], 1)

        def act_step(act, g, r, first, last):
            if not last:
                act_v(act, g + 1, 1 - r)
                act_exp(act, g + 1, 1 - r)
            if not first:
                act_out(act, g - 1, 1 - r)
            act_turn(act, g, r)

        LOOPS = (NPG - 2) // 2
        
        with nc.Block() as block:
            @block.tensor
            def _(pe):
                for i, wt in enumerate((w.m_q, w.m_k)):
                    for g in range(GROUPS):
                        nc.tensor.matmul(ps[:, 4 * i + g, :], wt[:], m.xt[:, 2 * g:2 * g + 2, PAD:], start=True,
                                         stop=True).then_inc(k["qp"], 1)
                pe.wait_ge(k["qe"], 2 * GROUPS)
                pe_scores(pe, 0, 0)
                pe_step(pe, 0, 0, True, False)
                with pe.Fori(0, LOOPS) as i:
                    pe_step(pe, i * 2 + 1, 1, False, False)
                    pe_step(pe, i * 2 + 2, 0, False, False)
                pe_step(pe, NPG - 1, 1, False, True)
                pe_pv(pe, NPG - 1, 1)
                pe.wait_ge(k["oe"], NPG + 2)
                for t in range(TILES):
                    ins = nc.tensor.matmul(ps[:, t // GT, (t % GT) * P:(t % GT + 1) * P],
                                           ot[:, t // 2, (t % 2) * P:(t % 2 + 1) * P], w.m_o[:], start=(t % GT == 0),
                                           stop=True, skip_group_check=True)
                    if t % GT == GT - 1:
                        ins.then_inc(k["pr"], 1)
                for g in range(GROUPS):
                    pe.wait_ge(k["nn"], g + 1)
                    for t in range(GT):
                        ins = nc.tensor.transpose(ps[:, 4 + g, t * P:(t + 1) * P], y[:, g * GT + t, :], m.ident[:])
                    ins.then_inc(k["yt"], 1)

            @block.vector
            def _(dve):
                nc.vector.tensor_tensor(kb[:], w.head_rows[:], w.m_bqkv[:, 1:2].to_broadcast([P, MH]),
                                        ALU.mult).then_inc(k["kb"], 1)
                dve_max(dve, 0, 0)
                dve_step(dve, 0, 0, False)
                with dve.Fori(0, LOOPS) as i:
                    dve_step(dve, i * 2 + 1, 1, False)
                    dve_step(dve, i * 2 + 2, 0, False)
                dve_step(dve, NPG - 1, 1, True)
                dve.wait_ge(k["rs"], 1)
                for g in range(GROUPS):
                    dve.wait_ge(k["pr"], g + 1)
                    yg = y[:, g * GT:(g + 1) * GT, :].rearrange("p t d -> p (t d)")
                    nc.vector.tensor_tensor(yg, yg, ps[:, g, :], ALU.add).then_inc(k["r1"], 1)
                normalise(nc, dve, m, y, k["st"], k["pw"], [(k["r1"], GROUPS)])
                for g in range(GROUPS):
                    for t in range(g * GT, (g + 1) * GT):
                        ins = nc.vector.tensor_scalar(y[:, t, :], y[:, t, :], m.mv[:, t, 0:1], m.rstd[:, t:t + 1],
                                                      ALU.subtract, ALU.mult)
                    ins.then_inc(k["nn"], 1)

            @block.scalar
            def _(act):
                for g in range(GROUPS):
                    act.wait_ge(k["qp"], g + 1)
                    nc.scalar.activation(qt[:, 2 * g:2 * g + 2, :], ps[:, g, :].rearrange("p (b t) -> p b t", b=2),
                                         ACT.Identity, bias=w.m_bqkv[:, 0:1]).then_inc(k["qe"], 1)
                act.wait_ge(k["kb"], 1)
                for g in range(GROUPS):
                    act.wait_ge(k["qp"], GROUPS + g + 1)
                    for h in range(MH):
                        ins = nc.scalar.activation(km[:, h, 2 * g:2 * g + 2, :],
                                                   ps[:, 4 + g, :].rearrange("p (b t) -> p b t", b=2), ACT.Identity,
                                                   bias=kb[:, h:h + 1], scale=w.head_rows[:, h:h + 1])
                    ins.then_inc(k["qe"], 1)
                act.sem_inc(k["oe"], 2)
                act_v(act, 0, 0)
                act_exp(act, 0, 0)
                act_step(act, 0, 0, True, False)
                with act.Fori(0, LOOPS) as i:
                    act_step(act, i * 2 + 1, 1, False, False)
                    act_step(act, i * 2 + 2, 0, False, False)
                act_step(act, NPG - 1, 1, False, True)
                act_out(act, NPG - 1, 1)
                for g in range(GROUPS):
                    act.wait_ge(k["yt"], g + 1)
                    nc.scalar.activation(m.xt[:, 2 * g:2 * g + 2, PAD:],
                                         ps[:, 4 + g, :].rearrange("p (b t) -> p b t", b=2), ACT.Identity,
                                         scale=w.m_gb[:, 0:1], bias=w.m_gb[:, 1:2])

            @block.gpsimd
            def _(pool):
                pool.wait_ge(k["qe"], 2 * GROUPS)
                pool_copy(pool, 0, 0)
                pool_copy(pool, 1, 1)
                with pool.Fori(0, LOOPS) as i:
                    pool_copy(pool, i * 2 + 2, 0)
                    pool_copy(pool, i * 2 + 3, 1)
                nc.gpsimd.tensor_tensor(y[:], y[:], w.m_rows[:, 0:1, :].to_broadcast([P, TILES, DIM]),
                                        ALU.add).then_inc(k["rs"], 1)
                pool.wait_ge(k["st"], 3)
                nc.gpsimd.tensor_tensor(m.rstd[:], m.ve[:], m.mhalf[:], ALU.pow).then_inc(k["pw"], 1)
                pool.wait_ge(k["yt"], GROUPS)
                nc.gpsimd.tensor_tensor(y[:], y[:], w.m_rows[:, 1:2, :].to_broadcast([P, TILES, DIM]),
                                        ALU.mult).then_inc(k["gb"], 1)
                pool.wait_ge(k["gb"], 1)
                nc.gpsimd.tensor_tensor(y[:], y[:], w.m_rows[:, 2:3, :].to_broadcast([P, TILES, DIM]), ALU.add)


def normalise(nc, dve, m, src, step, power, ready):
    for s, n in ready:
        dve.wait_ge(s, n)
    for t in range(TILES):
        ins = nc.vector.bn_stats(m.stats[:, t, :], src[:, t, :])
    ins.then_inc(step, 1)
    dve.wait_ge(step, 1)
    for t in range(TILES):
        ins = nc.vector.bn_aggr(m.mv[:, t, :], m.stats[:, t, :])
    ins.then_inc(step, 1)
    dve.wait_ge(step, 2)
    nc.vector.tensor_scalar(m.ve[:], m.mv[:, :, 1], EPS, None, ALU.add).then_inc(step, 1)
    dve.wait_ge(power, 1)


def experts(nc, m, name, dram):
    w = m.w
    with ExitStack() as own:
        def sb(n, shape, dt=F32):
            return own.enter_context(nc.sbuf_tensor(f"{name}_{n}", shape, dt))

        w1 = sb("w1", [P, 2, FF])
        w2 = sb("w2", [P, 2, FT, DIM])
        b1 = sb("b1", [P, 2, FT])
        b2 = sb("b2", [EXP, DIM])
        logits = sb("logits", [P, TILES, EXP])
        best = sb("best", [P, TILES])
        hot = sb("hot", [P, TILES, EXP])
        hott = sb("hot_t", [EXP, TOK])
        order = sb("order", [P, EXP])
        h = sb("h", [P, 2, FT, BANK])
        y = m.xn
        k = sems(nc, own, "w_even w_odd b order lg st hp ht hc bp bd hid h o acc pw nn g2", f"{name}_")
        loaded = (k["w_even"], k["w_odd"])
        ps = m.ps
        NH = GROUPS * FT

        def pe_hidden(pe, e, r, g):
            for f in range(FT):
                n = g * FT + f
                pe.wait_ge(k["h"], e * NH + (n + 1))
                nc.tensor.matmul(ps[:, n % 4, :], w1[:, r, f * P:(f + 1) * P], m.xt[:, 2 * g:2 * g + 2, PAD:],
                                 start=True, stop=True).then_inc(k["hid"], 1)

        def pe_second(pe, e, r, g):
            pe.wait_ge(k["h"], e * NH + (g * FT + 4 + FT))
            pe.wait_ge(k["acc"], e * GROUPS + (g + 1))
            for t in range(GT):
                for f in range(FT):
                    ins = nc.tensor.matmul(ps[:, 4 + g % 2, t * P:(t + 1) * P], h[:, g % 2, f, t * P:(t + 1) * P],
                                           w2[:, r, f, :], start=(t == 0 and f == 0), stop=(f == FT - 1),
                                           skip_group_check=True)
            ins.then_inc(k["o"], 1)

        def pe_expert(pe, i, r):
            e = i * 2 + r
            pe.wait_ge(loaded[r], i * 48 + 48)
            for g in range(GROUPS):
                pe_hidden(pe, e, r, g)
                if g:
                    pe_second(pe, e, r, g - 1)
            pe_second(pe, e, r, GROUPS - 1)

        def act_expert(act, i, r):
            e = i * 2 + r
            act.wait_ge(loaded[r], i * 48 + 48)
            for g in range(GROUPS):
                for f in range(FT):
                    n = g * FT + f
                    act.wait_ge(k["hid"], e * NH + (n + 1))
                    if f == 0:
                        act.wait_ge(k["o"], e * GROUPS + (g + 1))
                    nc.scalar.activation(h[:, g % 2, f, :], ps[:, n % 4, :], ACT.Relu,
                                         bias=b1[:, r, f:f + 1]).then_inc(k["h"], 1)

        def dve_expert(dve, e):
            for g in range(GROUPS):
                dve.wait_ge(k["o"], e * GROUPS + (g + 3))
                for t in range(GT):
                    yt = y[:, g * GT + t, :]
                    pick = hot[:, g * GT + t, bass.ds(e, 1)]
                    ins = nc.vector.scalar_tensor_tensor(out=yt, in0=ps[:, 4 + g % 2, t * P:(t + 1) * P], scalar=pick,
                                                         in1=yt, op0=ALU.mult, op1=ALU.add)
                ins.then_inc(k["acc"], 1)

        with nc.Block() as block:
            @block.sync
            def _(sp):
                sp.dma_start(b2[:], dram["m_b2"]).then_inc(k["b"], 16)

                def load(e, r):
                    pick = bass.ds(e, 1) if not isinstance(e, int) else slice(e, e + 1)
                    sp.dma_start(w1[:, r, :], dram["m_w1"][pick].rearrange("a p n -> p (a n)")).then_inc(loaded[r], 16)
                    sp.dma_start(b1[:, r, :], dram["m_b1"][pick].rearrange("a p f -> p (a f)"))\
                        .then_inc(loaded[r], 16)
                    sp.dma_start(w2[:, r], dram["m_w2"][pick].rearrange("a p f n -> p (a f) n")).then_inc(loaded[r], 16)

                load(0, 0)
                load(1, 1)
                with sp.Fori(0, EXP // 2 - 1) as i:
                    for r in range(2):
                        sp.wait_ge(k["o"], i * 2 * GROUPS + ((r + 1) * GROUPS + 2))
                        load(i * 2 + (r + 2), r)

            @block.tensor
            def _(pe):
                pe.sem_inc(k["o"], 2)
                for t in range(TILES):
                    ins = nc.tensor.matmul(ps[:, 6, t * EXP:(t + 1) * EXP],
                                           m.xt[:, t // 2, PAD + (t % 2) * P:PAD + (t % 2) * P + P], w.m_gate[:],
                                           start=(t == 0), stop=True, skip_group_check=True)
                ins.then_inc(k["lg"], 1)
                pe.wait_ge(k["st"], 6)
                for t in range(TILES):
                    ins = nc.tensor.transpose(ps[0:EXP, t // 4, (t % 4) * P:(t % 4 + 1) * P], hot[:, t, :], m.ident[:])
                ins.then_inc(k["ht"], 1)
                pe.wait_ge(k["hc"], 1)
                pe.wait_ge(k["b"], 16)
                for t in range(TILES):
                    ins = nc.tensor.matmul(ps[:, 4 + t // 4, (t % 4) * P:(t % 4 + 1) * P], hott[:, t * P:(t + 1) * P],
                                           b2[:], start=(t % 4 == 0), stop=True, skip_group_check=True)
                ins.then_inc(k["bp"], 1)
                with pe.Fori(0, EXP // 2) as i:
                    pe_expert(pe, i, 0)
                    pe_expert(pe, i, 1)

            @block.scalar
            def _(act):
                act.wait_ge(k["ht"], 1)
                nc.scalar.activation(hott[:], ps[0:EXP, 0:4, :].rearrange("p a b -> p (a b)"),
                                     ACT.Copy).then_inc(k["hc"], 1)
                act.wait_ge(k["hc"], 1)
                act.sem_inc(k["h"], 4)
                with act.Fori(0, EXP // 2) as i:
                    act_expert(act, i, 0)
                    act_expert(act, i, 1)

            @block.vector
            def _(dve):
                dve.wait_ge(k["lg"], 1)
                nc.vector.tensor_copy(logits[:], ps[:, 6, 0:TILES * EXP].rearrange("p (t e) -> p t e", e=EXP))\
                    .then_inc(k["st"], 1)
                pick_first(nc, dve, k["st"], 1, k["order"], logits, best, hot, order)
                dve.wait_ge(k["bp"], 1)
                nc.vector.tensor_tensor(y[:].rearrange("p t d -> p (t d)"), y[:].rearrange("p t d -> p (t d)"),
                                        ps[:, 4:8, :].rearrange("p a b -> p (a b)"), ALU.add).then_inc(k["bd"], 1)
                dve.wait_ge(k["bd"], 1)
                dve.sem_inc(k["acc"], 2)
                with dve.Fori(0, EXP) as e:
                    dve_expert(dve, e)
                normalise(nc, dve, m, y, k["nn"], k["pw"], [(k["acc"], EXP * GROUPS + 2)])
                for t in range(TILES):
                    ins = nc.vector.tensor_scalar(y[:, t, :], y[:, t, :], m.mv[:, t, 0:1], m.rstd[:, t:t + 1],
                                                  ALU.subtract, ALU.mult)
                ins.then_inc(k["g2"], 1)
                dve.wait_ge(k["g2"], 1)
                nc.vector.tensor_tensor(y[:], y[:], w.m_rows[:, 3:4, :].to_broadcast([P, TILES, DIM]),
                                        ALU.mult).then_inc(k["g2"], 1)
                dve.wait_ge(k["g2"], 2)
                dve.wait_ge(k["order"], 2)
                nc.vector.tensor_tensor(m.x[:], m.x[:], y[:], ALU.add)

            @block.gpsimd
            def _(pool):
                nc.gpsimd.iota(order[:], [[-1, EXP]], base=EXP, channel_multiplier=0,
                               allow_small_or_imprecise_dtypes=True).then_inc(k["order"], 1)
                nc.gpsimd.tensor_tensor(m.x[:], m.x[:], w.m_rows[:, 4:5, :].to_broadcast([P, TILES, DIM]),
                                        ALU.add).then_inc(k["order"], 1)
                pool.wait_ge(k["nn"], 3)
                nc.gpsimd.tensor_tensor(m.rstd[:], m.ve[:], m.mhalf[:], ALU.pow).then_inc(k["pw"], 1)


def network(nc, dram, out, start=0, stop=99):
    with ExitStack() as ctx:
        m = open_memory(nc, ctx)
        conv = ExitStack()

        def first_ffn():
            m.toeplitz = conv.enter_context(nc.sbuf_tensor("toeplitz", [P, DIM, P], F32))
            layernorm(nc, m, "ln1")
            lora_ffn(nc, m, "f1", prefetch=lambda sp: load_toeplitz(sp, m))

        def convolution():
            layernorm(nc, m, "ln2", transposed=False)
            long_conv(nc, m)
            conv.close()

        layers = [lambda: setup(nc, m, ctx, dram),
                  lambda: (layernorm(nc, m, "ln0"), state_space(nc, m)),
                  first_ffn,
                  convolution,
                  lambda: (layernorm(nc, m, "ln3"), lora_ffn(nc, m, "f2")),
                  lambda: (layernorm(nc, m, "ln4"), attention(nc, m, "at1", m.w.a1, True)),
                  lambda: (layernorm(nc, m, "ln5"), batch_attention(nc, m, "ba1"), experts(nc, m, "ex1", dram)),
                  lambda: (layernorm(nc, m, "ln6"), attention(nc, m, "at2", m.w.a2, False)),
                  lambda: (layernorm(nc, m, "ln7"), batch_attention(nc, m, "ba2"), experts(nc, m, "ex2", dram))]
        for layer in [layers[0]] + layers[start + 1:stop + 1]:
            layer()
        stored = ctx.enter_context(nc.semaphore("stored"))
        with nc.Block() as block:
            @block.sync
            def _(sp):
                sp.dma_start(out.rearrange("b (h p) d -> p (b h) d", p=P), m.x[:]).then_inc(stored, 16)
                sp.wait_ge(stored, 16)


def lay_out(inputs):
    g = {k: np.asarray(v) for k, v in inputs.items()}

    def cols(a):
        return a.reshape(-1, P).T

    def rows(a):
        return a.reshape(-1, P, a.shape[-1]).transpose(1, 0, 2)

    d = {
        "x": g["L0_attn_a_x"],
        "in_w": g["L0_attn_a_W_in"],
        "conv_rows": g["L0_attn_a_conv_w"][:, 0, :].T,
        "conv_b": cols(g["L0_attn_a_conv_b"]),
        "x_w": rows(g["L0_attn_a_W_x"]),
        "dt_w": g["L0_attn_a_W_dt"],
        "dt_b": cols(g["L0_attn_a_b_dt"]),
        "a_log": rows(g["L0_attn_a_A_log"]),
        "d_skip": cols(g["L0_attn_a_D"]),
        "out_w": rows(g["L0_attn_a_W_out"]),
        "lc_a": g["L0_attn_b_A_log"].reshape(-1, 1),
        "lc_arow": g["L0_attn_b_A_log"],
        "lc_ct": g["L0_attn_b_C"].T,
        "lc_delta": g["L0_attn_b_delta"][0:1],
        "lc_rows": np.stack([g[f"L0_attn_b_{n}"] for n in ("D", "freq_align", "reward", "gamma", "beta")]),
        "gate": np.concatenate([g["L0_ffn_gate_W"].T, g["L0_ffn_lora_A"].reshape(ER, DIM).T], axis=1),
        "gate_b": g["L0_ffn_gate_b"],
        "wi": g["L0_ffn_wi_W"].T,
        "wi_b": cols(g["L0_ffn_wi_b"]),
        "wo": rows(np.ascontiguousarray(g["L0_ffn_wo_W"].T)),
        "wo_b": g["L0_ffn_wo_b"],
        "lora_b": g["L0_ffn_lora_B"].transpose(0, 2, 1).reshape(ER, FF),
    }
    straight = np.concatenate([h * HD + np.r_[0:HD:2, 1:HD:2] for h in range(HEADS)])
    crossed = np.concatenate([h * HD + np.r_[1:HD:2, 0:HD:2] for h in range(HEADS)])
    wq, wk, wv = np.split(g["L1_attn_a_w_qkv"], 3, axis=0)

    half = (np.arange(0, HD, 2, dtype=np.float32) / np.float32(HD)).astype(np.float32)
    inv = (np.float32(1) / np.power(np.float32(10000), half)).astype(np.float32)
    angle = np.outer(inv, np.arange(SEQ, dtype=np.float32)).astype(np.float32)
    cos, sin = np.cos(angle), np.sin(angle)
    mask = np.where(allowed_pairs(), 0, NEG).astype(np.float32)
    same = np.arange(P) % PG
    d.update({
        "a1_wq1": wq[straight].T, "a1_wq2": wq[crossed].T, "a1_wk1": wk[straight].T, "a1_wk2": wk[crossed].T,
        "a1_wv": wv.T, "a1_wo": g["L1_attn_a_w_out"].T, "a1_bo": g["L1_attn_a_b_out"],
        "a1_cos": np.tile(np.concatenate([cos, cos]), (HEADS, 1)),
        "a1_sin": np.tile(np.concatenate([-sin, sin]), (HEADS, 1)),
        "a2_wq": g["L1_attn_b_Wq"], "a2_wk": g["L1_attn_b_Wk"], "a2_wv": g["L1_attn_b_Wv"],
        "a2_wo": g["L1_attn_b_Wo"],
        "a2_bq": g["L1_attn_b_bq"].reshape(P, 1),
        "a2_bo": g["L1_attn_b_bo"],
        "a2_bv": g["L1_attn_b_bv"],
        "head_rows": (np.arange(P)[:, None] // MHD == np.arange(MH)[None, :]).astype(np.float32),
        "pick_max": np.repeat(((np.arange(P)[:, None] % 4 == np.arange(4)[None, :])
                               & (np.arange(P)[:, None] < 12)).astype(np.float32)[:, :, None], P, axis=2),
        "mask_q": mask.reshape(2, P, SEQ).transpose(1, 0, 2),
        "mask_k": mask.T.reshape(2, P, SEQ).transpose(1, 0, 2),
        "m_q": g["L1_ffn_Wqkv"][0:DIM].T, "m_k": g["L1_ffn_Wqkv"][DIM:2 * DIM].T, "m_v": g["L1_ffn_Wqkv"][2 * DIM:].T,
        "m_o": g["L1_ffn_Wo"].T, "m_bqkv": cols(g["L1_ffn_bqkv"]),
        "m_gb": np.stack([g["L1_ffn_g1"], g["L1_ffn_be1"]], axis=1),
        "m_rows": np.stack([g[f"L1_ffn_{n}"] for n in ("bo", "g1", "be1", "g2", "be2")]),
        "m_gate": g["L1_ffn_Wg"].T,
        "m_mask": np.where(same[:, None] == same[None, :], 0, NEG).astype(np.float32),
        "m_w1": g["L1_ffn_W1"],
        "m_w2": g["L1_ffn_W2"].reshape(EXP, FT, P, DIM).transpose(0, 2, 1, 3),
        "m_b1": g["L1_ffn_b1"].reshape(EXP, FT, P).transpose(0, 2, 1),
        "m_b2": g["L1_ffn_b2"],
    })
    return {k: np.ascontiguousarray(v) for k, v in d.items()}


def kernel(**inputs):
    import concourse.bacc as bacc
    from concourse.bass_utils import run_bass_kernel_spmd as run

    nc = bacc.Bacc("TRN2", target_bir_lowering=False, num_devices=1)
    arrays, dram = {}, {}
    for name, a in lay_out(inputs).items():
        arrays[f"in_{name}_dram"] = a
        dram[name] = nc.dram_tensor(f"in_{name}_dram", a.shape, mybir.dt.from_np(a.dtype), kind="ExternalInput").ap()
    out = nc.dram_tensor("out_0_dram", (BATCH, SEQ, DIM), F32, kind="ExternalOutput").ap()
    network(nc, dram, out)
    return run(nc, [arrays], core_ids=[0]).results[0]["out_0_dram"]
```

```python
from contextlib import ExitStack

import concourse.bass as bass
import numpy as np
from concourse import mybir

ALU = mybir.AluOpType
ACT = mybir.ActivationFunctionType
AX = mybir.AxisListType
F32 = mybir.dt.float32
BF16 = mybir.dt.bfloat16

P = 128
BATCH, SEQ, DIM = 8, 256, 128
TOK = BATCH * SEQ
TILES = TOK // P
BANK = 512
GROUPS = TOK // BANK
GT = TILES // GROUPS
EPS = 1e-5

CONV = 4
PAD = CONV - 1
DIN, NST, DTR = 256, 16, 64
CH = DIN // P
HALVES = 2
HB = BATCH // HALVES
HT = TOK // HALVES
LNST = 64
TOEPLITZ_LOADS = 8
FF, FT = 512, 4
EXP, RANK = 8, 4
ER = EXP * RANK
HEADS, HD = 16, 8
CHUNK_FRAMES, LOOKAHEAD = 100, 50
NEG = -1e30
MH, MHD = 4, 32
PG = 16
NPG = SEQ // PG
SORTED = (TOK + EXP * (P - 1)) // P


class Net:
    pass


def open_memory(nc, ctx):
    m = Net()

    def sb(name, shape, dt=F32):
        return ctx.enter_context(nc.sbuf_tensor(name, shape, dt))

    m.x = sb("x_res", [P, TILES, DIM])
    m.xn = sb("x_norm", [P, TILES, DIM])
    m.xt = sb("x_norm_t", [P, BATCH, PAD + SEQ])
    m.ident = sb("ident", [P, P])
    m.identb = sb("identb", [P, P], BF16)
    m.stats = sb("ln_stats", [P, TILES, 6])
    m.mv = sb("ln_mean_var", [P, TILES, 2])
    m.ve = sb("ln_var_eps", [P, TILES])
    m.rstd = sb("ln_rstd", [P, TILES])
    m.nmean = sb("ln_minus_mean", [P, TILES])
    m.shift = sb("ln_shift", [P, TILES])
    m.mhalf = sb("minus_half", [P, TILES])
    m.ones = sb("ones_row", [P, P])
    m.ps = ctx.enter_context(nc.psum_tensor("psum", [P, 8, BANK], F32))
    return m


def sems(nc, ctx, names, prefix=""):
    held = {n: ctx.enter_context(nc.semaphore(prefix + n)) for n in names.split()}

    def clear():
        for h in held.values():
            nc.gpsimd.sem_clear(h)

    ctx.callback(clear)
    return held


PACKS = {
    "early": "in_w conv_b x_w dt_b a_log d_skip out_w lc_align",
    "early64": "dt_w lc_a lc_ct",
    "rows_early": "conv_rows lc_delta lc_rows lc_arow",
    "tables": "mask_q mask_k pick_max m_mask",
    "late": "gate lora_b wi wi_b wo a1_wq1 a1_wq2 a1_wk1 a1_wk2 a1_wv a1_wo a1_cos a1_sin a2_wq a2_wk a2_wv a2_wo a2_bq "
            "head_rows m_q m_k m_v m_o m_bqkv m_gb m_gate sort_before",
    "rows_late": "gate_b wo_b a1_bo a2_bo a2_bv m_rows sort_not_first sort_multiples sort_tiles",
}


class Pack:

    def __init__(self, nc, ctx, dram, name):
        self.dram = dram[name]
        rows = P if name.startswith("rows_") else self.dram.shape[0]
        self.tile = ctx.enter_context(nc.sbuf_tensor(f"pack_{name}", [rows, self.dram.shape[-1]], F32))
        self.left, self.at = PACKS[name].split(), 0

    def take(self, name, *shape):
        assert name == self.left.pop(0), name
        n = int(np.prod(shape))
        ap = self.tile[:, self.at:self.at + n]
        self.at += n
        return ap if len(shape) == 1 else ap.rearrange("p (a b) -> p a b", a=shape[0])


def load_weights(nc, m, ctx, own, dram):
    def sb(name, shape, dt=F32):
        return ctx.enter_context(nc.sbuf_tensor(name, shape, dt))

    w = m.w = Net()
    packs = {name: Pack(nc, ctx, dram, name) for name in PACKS if name != "tables"}
    early, early64, rows_early = packs["early"].take, packs["early64"].take, packs["rows_early"].take
    w.in_w = early("in_w", 2 * DIN)
    w.conv_b = early("conv_b", CH)
    w.x_w = early("x_w", CH, DTR + 2 * NST)
    w.dt_b = early("dt_b", CH)
    w.a_log = early("a_log", CH, NST)
    w.d_skip = early("d_skip", CH)
    w.out_w = early("out_w", CH, DIM)
    w.lc_align = early("lc_align", 1)
    w.dt_w = early64("dt_w", DIN)
    w.lc_a = early64("lc_a", 1)
    w.lc_ct = early64("lc_ct", DIM)
    w.conv_rows = rows_early("conv_rows", CONV, DIN)
    w.lc_delta = rows_early("lc_delta", 1)
    w.lc_rows = rows_early("lc_rows", 5, DIM)
    w.lc_arow = rows_early("lc_arow", LNST)
    late, rows_late = packs["late"].take, packs["rows_late"].take
    w.gate = late("gate", 2 * 32)
    w.lora_b = late("lora_b", GROUPS, FF)
    w.wi = late("wi", FF)
    w.wi_b = late("wi_b", FT)
    w.wo = late("wo", FT, DIM)
    a1, a2 = w.a1, w.a2 = Net(), Net()
    a1.wq1, a1.wq2, a1.wk1, a1.wk2, a1.wv, a1.wo = (late(f"a1_{n}", DIM) for n in "wq1 wq2 wk1 wk2 wv wo".split())
    a1.cos, a1.sin = late("a1_cos", SEQ), late("a1_sin", SEQ)
    a2.wq1, a2.wk1, a2.wv, a2.wo = (late(f"a2_{n}", DIM) for n in "wq wk wv wo".split())
    a2.bq = late("a2_bq", 1)
    w.head_rows = late("head_rows", MH)
    w.m_q, w.m_k, w.m_v, w.m_o = (late(f"m_{n}", DIM) for n in "qkvo")
    w.m_bqkv = late("m_bqkv", 3)
    w.m_gb = late("m_gb", 2)
    w.m_gate = late("m_gate", 32)
    w.before = late("sort_before", P)
    w.gate_b = rows_late("gate_b", EXP)
    w.wo_b = rows_late("wo_b", DIM)
    a1.bo, a2.bo, a2.bv = rows_late("a1_bo", DIM), rows_late("a2_bo", DIM), rows_late("a2_bv", DIM)
    w.m_rows = rows_late("m_rows", 5, DIM)
    w.sort_not_first = rows_late("sort_not_first", EXP * TILES)
    w.sort_multiples = rows_late("sort_multiples", TILES)
    w.sort_tiles = rows_late("sort_tiles", SORTED)
    a2.mask_q, a2.mask_k = (sb(f"a2_{n}", [P, 2, SEQ], BF16) for n in ("mask_q", "mask_k"))
    a1.pick = a2.pick = sb("pick", [P, 4], BF16)
    w.m_mask = sb("m_mask", [P, P], BF16)
    packs["tables"] = Pack(nc, own, dram, "tables")
    tables = packs["tables"].take
    w.tables = [(a2.mask_q, tables("mask_q", 2, SEQ)), (a2.mask_k, tables("mask_k", 2, SEQ)),
                (a1.pick, tables("pick_max", 4)), (w.m_mask, tables("m_mask", P))]
    return packs


def on_all_partitions(ap, partitions=P):
    return bass.AP(ap.tensor, ap.offset, [[0, partitions]] + [list(d) for d in ap.ap])


def setup(nc, m, ctx, dram):
    m.toeplitz_loaded = ctx.enter_context(nc.semaphore("toeplitz_loaded"))
    m.kernels_stored = ctx.enter_context(nc.semaphore("kernels_stored"))
    kpad = ctx.enter_context(nc.sbuf_tensor("kernel_padded", [DIM, 2 * P], F32))
    m.late_loaded = ctx.enter_context(nc.semaphore("late_loaded"))
    m.lc_pow = ctx.enter_context(nc.sbuf_tensor("lc_pow", [LNST, P + 1], F32))
    m.lc_powt = ctx.enter_context(nc.sbuf_tensor("lc_powt", [P, LNST], F32))
    m.kernel_dram = kernel_dram = nc.dram_tensor("kernel_scratch", (DIM, 2 * P), F32, kind="Internal").ap()
    with ExitStack() as own:
        def sb(name, shape, dt=F32):
            return own.enter_context(nc.sbuf_tensor(name, shape, dt))

        packs = load_weights(nc, m, ctx, own, dram)
        w = m.w
        steps = sb("steps", [LNST, P + 1])
        back = sb("steps_back", [P, 1])
        da = sb("delta_a", [LNST, 1])
        dar = sb("delta_a_row", [P, LNST])
        s = sems(nc, own, "su_w su_consts su_zeros su_dve su_rates su_pow su_kpsum su_kernel su_tables")
        with nc.Block() as block:
            @block.sync
            def _(sp):
                def load(name, counter):
                    src = packs[name].dram
                    src = on_all_partitions(src) if name.startswith("rows_") else src
                    sp.dma_start(packs[name].tile[:], src).then_inc(counter, 16)

                for name in ("early64", "rows_early", "early"):
                    load(name, s["su_w"])
                sp.dma_start(m.x[:], dram["x"].rearrange("b (h p) d -> p (b h) d", p=P)).then_inc(s["su_w"], 16)
                load("tables", s["su_tables"])
                for name in ("late", "rows_late"):
                    load(name, m.late_loaded)
                sp.wait_ge(s["su_kernel"], 1)
                sp.dma_start(kernel_dram, kpad[:]).then_inc(m.kernels_stored, 16)

            @block.scalar
            def _(act):
                act.wait_ge(s["su_w"], 16 * 4)
                nc.scalar.activation(da[:], w.lc_a[:], ACT.Exp).then_inc(s["su_rates"], 1)
                nc.scalar.activation(dar[:], w.lc_arow[:], ACT.Exp).then_inc(s["su_rates"], 1)
                nc.scalar.activation(w.a_log[:], w.a_log[:], ACT.Exp).then_inc(s["su_rates"], 1)
                act.wait_ge(s["su_dve"], 3)
                act.wait_ge(s["su_consts"], 1)
                nc.scalar.activation(m.lc_pow[:], steps[:], ACT.Exp, scale=da[:]).then_inc(s["su_pow"], 1)
                nc.scalar.activation(m.lc_powt[:], dar[:], ACT.Exp, scale=back[:]).then_inc(s["su_pow"], 1)

            @block.vector
            def _(dve):
                nc.vector.memset(kpad[:], 0.0).then_inc(s["su_zeros"], 1)
                nc.vector.memset(m.xt[:], 0.0)
                nc.vector.memset(m.mhalf[:], -0.5)
                nc.vector.memset(m.ones[:], 1.0)
                dve.wait_ge(s["su_rates"], 3)
                nc.vector.tensor_scalar(da[:], da[:], w.lc_delta[0:LNST], -1.0, ALU.mult, ALU.mult).then_inc(s["su_dve"], 1)
                nc.vector.tensor_scalar(dar[:], dar[:], w.lc_delta[:], -1.0, ALU.mult, ALU.mult).then_inc(s["su_dve"], 1)
                nc.vector.tensor_scalar(w.a_log[:], w.a_log[:], -1.0, None, ALU.mult).then_inc(s["su_dve"], 1)
                dve.wait_ge(s["su_kpsum"], 1)
                dve.wait_ge(s["su_zeros"], 1)
                nc.vector.tensor_scalar(kpad[:, P - 1:2 * P - 1], m.ps[:, 0, 0:P], w.lc_align[:, 0:1], None,
                                        ALU.mult).then_inc(s["su_kernel"], 1)
                nc.vector.tensor_tensor(w.lc_ct[:], w.lc_ct[:], w.lc_rows[0:LNST, 1, :], ALU.mult)
                nc.vector.tensor_tensor(w.lc_rows[:, 0, :], w.lc_rows[:, 0, :], w.lc_rows[:, 1, :], ALU.mult)
                dve.wait_ge(s["su_tables"], 16)
                for dst, src in w.tables:
                    nc.vector.tensor_copy(dst[:], src)

            @block.gpsimd
            def _(pool):
                nc.gpsimd.iota(steps[:], [[1, P + 1]], base=0, channel_multiplier=0,
                               allow_small_or_imprecise_dtypes=True)
                nc.gpsimd.iota(back[:], [[0, 1]], base=P - 1, channel_multiplier=-1,
                               allow_small_or_imprecise_dtypes=True).then_inc(s["su_consts"], 1)
                nc.gpsimd.memset(m.ident[:], 0.0)
                nc.gpsimd.memset(m.identb[:], 0.0).then_inc(s["su_consts"], 1)
                pool.wait_ge(s["su_consts"], 2)
                for t in (m.ident, m.identb):
                    nc.gpsimd.affine_select(out=t[:], in_=t[:], compare_op=ALU.not_equal, fill=1.0, base=0,
                                            pattern=[[-1, P]], channel_multiplier=1)

            @block.tensor
            def _(pe):
                pe.wait_ge(s["su_pow"], 1)
                nc.tensor.matmul(m.ps[:, 0, 0:P], w.lc_ct[:], m.lc_pow[:, 0:P], start=True,
                                 stop=True).then_inc(s["su_kpsum"], 1)


def group_stats(nc, dve, m, src, g, step):
    tiles = slice(g * GT, (g + 1) * GT)
    for t in range(g * GT, (g + 1) * GT):
        ins = nc.vector.bn_stats(m.stats[:, t, :], src[:, t, :])
    ins.then_inc(step, 1)
    dve.wait_ge(step, 3 * g + 1)
    for t in range(g * GT, (g + 1) * GT):
        ins = nc.vector.bn_aggr(m.mv[:, t, :], m.stats[:, t, :])
    ins.then_inc(step, 1)
    dve.wait_ge(step, 3 * g + 2)
    nc.vector.tensor_scalar(m.nmean[:, tiles], m.mv[:, tiles, 0], -1.0, None, ALU.mult)
    nc.vector.tensor_scalar(m.ve[:, tiles], m.mv[:, tiles, 1], EPS, None, ALU.add).then_inc(step, 1)


def group_power(nc, pool, m, g, step, power):
    tiles = slice(g * GT, (g + 1) * GT)
    pool.wait_ge(step, 3 * g + 3)
    nc.gpsimd.tensor_tensor(m.rstd[:, tiles], m.ve[:, tiles], m.mhalf[:, tiles], ALU.pow).then_inc(power, 1)


def group_scale(nc, dve, m, y, g, power, done):
    dve.wait_ge(power, g + 1)
    for t in range(g * GT, (g + 1) * GT):
        ins = nc.vector.tensor_scalar(y[:, t, :], y[:, t, :], m.mv[:, t, 0:1], m.rstd[:, t:t + 1], ALU.subtract, ALU.mult)
    ins.then_inc(done, 1)


def group_shift(nc, pool, m, g, power, shift):
    tiles = slice(g * GT, (g + 1) * GT)
    pool.wait_ge(power, g + 1)
    nc.gpsimd.tensor_tensor(m.shift[:, tiles], m.nmean[:, tiles], m.rstd[:, tiles], ALU.mult).then_inc(shift, 1)


def group_scale_by_act(nc, act, m, dst, src, g, shift, done):
    act.wait_ge(shift, g + 1)
    for t in range(g * GT, (g + 1) * GT):
        ins = nc.scalar.activation(dst[:, t, :], src[:, t, :], ACT.Identity, scale=m.rstd[:, t:t + 1],
                                   bias=m.shift[:, t:t + 1])
    ins.then_inc(done, 1)


def layernorm(nc, m, name, transposed=True):
    with ExitStack() as own:
        k = sems(nc, own, "stats power shift xn xtp", f"{name}_")
        with nc.Block() as block:
            @block.vector
            def _(dve):
                for g in range(GROUPS):
                    group_stats(nc, dve, m, m.x, g, k["stats"])

            @block.gpsimd
            def _(pool):
                for g in range(GROUPS):
                    group_power(nc, pool, m, g, k["stats"], k["power"])
                    group_shift(nc, pool, m, g, k["power"], k["shift"])

            @block.scalar
            def _(act):
                def scale(g):
                    group_scale_by_act(nc, act, m, m.xn, m.x, g, k["shift"], k["xn"])

                def copy(g):
                    act.wait_ge(k["xtp"], g + 1)
                    nc.scalar.activation(m.xt[:, 2 * g:2 * g + 2, PAD:],
                                         m.ps[:, g, :].rearrange("p (b t) -> p b t", b=2), ACT.Copy)

                scale(0)
                for g in range(1, GROUPS):
                    scale(g)
                    if transposed:
                        copy(g - 1)
                if transposed:
                    copy(GROUPS - 1)

            if transposed:
                @block.tensor
                def _(pe):
                    for g in range(GROUPS):
                        pe.wait_ge(k["xn"], g + 1)
                        for t in range(GT):
                            ins = nc.tensor.transpose(m.ps[:, g, t * P:(t + 1) * P], m.xn[:, g * GT + t, :],
                                                      m.ident[:])
                        ins.then_inc(k["xtp"], 1)


def state_space(nc, m):
    w = m.w
    with ExitStack() as own:
        def sb(name, shape, dt=F32):
            return own.enter_context(nc.sbuf_tensor(name, shape, dt))

        tap_w = w.conv_rows
        d_diag = sb("d_diag", [P, CH, P])
        pick = sb("pick_rows", [96, 2 * NST, P], BF16)
        u = sb("u", [P, CH, HT])
        gate = sb("res_gate", [P, CH, HT])
        bc3 = sb("bc_split", [96, HT], BF16)
        bcm = sb("bc_mid", [96, HT], BF16)
        w_bc = sb("w_bc3", [P, CH, 96])
        delta = sb("delta", [P, CH, HT])
        t_abs = sb("t_abs", [P, CH, HT])
        du = m.xn[:].rearrange("p (c a) d -> p c (a d)", c=CH)
        AHEAD = 4
        bs = sb("b_rows", [P, AHEAD, HT])
        cs = sb("c_rows", [P, AHEAD, HT])
        da = sb("decay", [P, AHEAD, CH, HB, SEQ])
        hs = sb("h_state", [P, 2, CH, HT])
        bcr, bcr2 = hs[0:96, 0, 0, :], hs[0:96, 0, 1, :]
        dt_in = hs[0:DTR, 1, 0, :]
        y = t_abs
        s = sems(nc, own, "ss_set ss_pool ss_xs ss_u ss_res ss_gate ss_dt ss_xd ss_dtin ss_split ss_z ss_expn ss_abs "
                          "ss_sp ss_relu ss_delta ss_du ss_pick ss_rows ss_free ss_da ss_dbu ss_h ss_hc ss_acc ss_y "
                          "ss_o ss_x")
        ps = m.ps
        with nc.Block() as block:
            @block.sync
            def _(sp):
                sp.wait_ge(m.late_loaded, 16 * 2)

            @block.gpsimd
            def _(pool):
                nc.gpsimd.memset(da[:, :, :, :, 0:1], 0.0)
                nc.gpsimd.memset(pick[:], 0.0).then_inc(s["ss_pool"], 1)
                for part in range(3):
                    pool.wait_ge(s["ss_pool"], part + 1)
                    nc.gpsimd.affine_select(out=pick[:], in_=pick[:], compare_op=ALU.not_equal, fill=1.0,
                                            base=-32 * part, pattern=[[-1, 2 * NST], [0, P]],
                                            channel_multiplier=1).then_inc(s["ss_pool"], 1)
                for half in range(HALVES):
                    base = half * NST
                    with pool.Fori(0, NST // AHEAD) as turn:
                        n = turn * AHEAD
                        for j in range(AHEAD):
                            pool.wait_ge(s["ss_rows"], n + (base + j + 1))
                            for c in range(CH):
                                unit = n * CH + ((base + j) * CH + c + 1)
                                pool.wait_ge(s["ss_h"], unit)
                                nc.gpsimd.tensor_tensor(hs[:, j % 2, c, :], hs[:, j % 2, c, :], cs[:, j, :],
                                                        ALU.mult).then_inc(s["ss_hc"], 1)
                            pool.wait_ge(s["ss_hc"], n * CH + (base + j + 1) * CH)
                            pool.sem_inc(s["ss_free"], 1)

            @block.vector
            def _(dve):
                for k in range(CONV):
                    nc.vector.tensor_tensor(tap_w[:, k, :], w.in_w[:, 0:DIN], w.conv_rows[:, k, :], ALU.mult)
                for c in range(CH):
                    for part in range(3):
                        nc.vector.tensor_copy(w_bc[:, c, part * 32:part * 32 + 32], w.x_w[:, c, DTR:])
                    ins = nc.vector.tensor_scalar(d_diag[:, c, :], m.ident[:], w.d_skip[:, c:c + 1], None, ALU.mult)
                ins.then_inc(s["ss_set"], 1)
                for half in range(HALVES):
                    split = 5 * half
                    dve.wait_ge(s["ss_xd"], half + 1)
                    src = ps[0:96, 2:4, :].rearrange("p a b -> p (a b)")
                    nc.vector.tensor_copy(bc3[:], src).then_inc(s["ss_split"], 1)
                    dve.wait_ge(s["ss_split"], split + 1)
                    nc.vector.tensor_tensor(bcr, src, bc3[:], ALU.subtract).then_inc(s["ss_split"], 1)
                    dve.wait_ge(s["ss_split"], split + 2)
                    nc.vector.tensor_copy(bcm[:], bcr).then_inc(s["ss_split"], 1)
                    dve.wait_ge(s["ss_split"], split + 3)
                    nc.vector.tensor_copy(bc3[32:64, :], bcm[32:64, :])
                    nc.vector.tensor_tensor(bcr2, bcr, bcm[:], ALU.subtract).then_inc(s["ss_split"], 1)
                    dve.wait_ge(s["ss_split"], split + 4)
                    nc.vector.tensor_copy(bc3[64:96, :], bcr2[64:96, :]).then_inc(s["ss_split"], 1)
                    dve.wait_ge(s["ss_abs"], CH * (half + 1))
                    for c in range(CH):
                        zc = ps[:, 4 + 2 * c:6 + 2 * c, :].rearrange("p a b -> p (a b)")
                        ins = nc.vector.tensor_scalar(delta[:, c, :], zc, w.dt_b[:, c:c + 1], 0.0, ALU.add, ALU.max)
                    ins.then_inc(s["ss_relu"], 1)
                    dve.wait_ge(s["ss_relu"], half + 1)
                    for c in range(CH):
                        dve.wait_ge(s["ss_sp"], half * CH + c + 1)
                        nc.vector.tensor_tensor(delta[:, c, :], delta[:, c, :], t_abs[:, c, :],
                                                ALU.add).then_inc(s["ss_delta"], 1)
                    for c in range(CH):
                        dve.wait_ge(s["ss_delta"], half * CH + c + 1)
                        nc.vector.tensor_tensor(du[:, c, :], delta[:, c, :], u[:, c, :], ALU.mult).then_inc(s["ss_du"], 1)
                    dve.wait_ge(s["ss_du"], CH * (half + 1))
                    base = half * NST
                    with dve.Fori(0, NST // AHEAD) as turn:
                        n = turn * AHEAD
                        for j in range(AHEAD):
                            dve.wait_ge(s["ss_rows"], n + (base + j + 1))
                            for c in range(CH):
                                unit = n * CH + ((base + j) * CH + c + 1)
                                dve.wait_ge(s["ss_acc"], unit)
                                nc.vector.tensor_tensor(hs[:, j % 2, c, :], du[:, c, :], bs[:, j, :],
                                                        ALU.mult).then_inc(s["ss_dbu"], 1)
                                dve.wait_ge(s["ss_da"], unit)
                                dve.wait_ge(s["ss_dbu"], unit)
                                nc.vector.tensor_tensor_scan(
                                    hs[:, j % 2, c, :], da[:, j, c, :, :].rearrange("p b t -> p (b t)"), hs[:, j % 2, c, :],
                                    0.0, ALU.mult, ALU.add).then_inc(s["ss_h"], 1)
                    dve.wait_ge(s["ss_acc"], CH * NST * (half + 1) + 2 * CH)
                    for c in range(CH):
                        nc.vector.tensor_tensor(y[:, c, :], ps[:, 4 + 2 * c:6 + 2 * c, :].rearrange("p a b -> p (a b)"),
                                                gate[:, c, :], ALU.mult).then_inc(s["ss_y"], 1)
                    dve.wait_ge(s["ss_o"], half + 1)
                    xh = m.x[:, half * 8:half * 8 + 8, :].rearrange("p t d -> p (t d)")
                    nc.vector.tensor_tensor(xh, xh, ps[:, 4:6, :].rearrange("p a b -> p (a b)"),
                                            ALU.add).then_inc(s["ss_x"], 1)

            @block.tensor
            def _(pe):
                pe.sem_inc(s["ss_acc"], 2 * CH)
                pe.wait_ge(s["ss_set"], 1)

                def conv(half, c, q):
                    b0 = half * HB + 2 * q
                    for k in range(CONV):
                        ins = nc.tensor.matmul(ps[:, 2 * c + q, :], tap_w[:, k, c * P:(c + 1) * P],
                                               m.xt[:, b0:b0 + 2, k:k + SEQ], start=(k == 0), stop=(k == CONV - 1))
                    if q == 1:
                        ins.then_inc(s["ss_xs"], 1)

                def res_products(half):
                    for c in range(CH):
                        for q in range(2):
                            b0 = half * HB + 2 * q
                            ins = nc.tensor.matmul(ps[:, 4 + 2 * c + q, :], w.in_w[:, DIN + c * P:DIN + (c + 1) * P],
                                                   m.xt[:, b0:b0 + 2, PAD:], start=True, stop=True)
                        ins.then_inc(s["ss_res"], 1)

                def dt_products(half):
                    pe.wait_ge(s["ss_u"], CH * (half + 1))
                    for q in range(2):
                        for c in range(CH):
                            ins = nc.tensor.matmul(ps[0:DTR, q, :], w.x_w[:, c, 0:DTR],
                                                   u[:, c, q * BANK:(q + 1) * BANK], start=(c == 0),
                                                   stop=(c == CH - 1))
                    ins.then_inc(s["ss_dt"], 1)

                for c in range(CH):
                    for q in range(2):
                        conv(0, c, q)
                for half in range(HALVES):
                    if half:
                        dt_products(half)
                        pe.wait_ge(s["ss_x"], half)
                        res_products(half)
                    else:
                        res_products(half)
                        dt_products(half)
                    for q in range(2):
                        for c in range(CH):
                            ins = nc.tensor.matmul(ps[0:96, 2 + q, :], w_bc[:, c, :], u[:, c, q * BANK:(q + 1) * BANK],
                                                   start=(c == 0), stop=(c == CH - 1))
                    ins.then_inc(s["ss_xd"], 1)
                    pe.wait_ge(s["ss_dtin"], half + 1)
                    pe.wait_ge(s["ss_gate"], CH * (half + 1))
                    for c in range(CH):
                        for q in range(2):
                            ins = nc.tensor.matmul(ps[:, 4 + 2 * c + q, :], w.dt_w[:, c * P:(c + 1) * P],
                                                   dt_in[:, q * BANK:(q + 1) * BANK], start=True, stop=True)
                    ins.then_inc(s["ss_z"], 1)
                    pe.wait_ge(s["ss_split"], 5 * (half + 1))
                    pe.wait_ge(s["ss_relu"], half + 1)
                    pe.wait_ge(s["ss_abs"], CH * (half + 1))
                    for c in range(CH):
                        for q in range(2):
                            nc.tensor.matmul(ps[:, 4 + 2 * c + q, :], d_diag[:, c, :], u[:, c, q * BANK:(q + 1) * BANK],
                                             start=True, stop=False, skip_group_check=True)
                    base = half * NST

                    def rows(n, j):
                        if base or j:
                            pe.wait_ge(s["ss_rows"], n + (base + j))
                        for k in range(2):
                            r = pick[:, bass.ds(n + (j + k * NST), 1), :].rearrange("k a p -> k (a p)")
                            for q in range(2):
                                ins = nc.tensor.matmul(ps[:, 2 * k + q, :], r, bc3[:, q * BANK:(q + 1) * BANK],
                                                       start=True, stop=True)
                        ins.then_inc(s["ss_pick"], 1)

                    def add_state(n, j):
                        for c in range(CH):
                            pe.wait_ge(s["ss_hc"], n * CH + ((base + j) * CH + c + 1))
                            for q in range(2):
                                ins = nc.tensor.matmul(ps[:, 4 + 2 * c + q, :], m.ident[:],
                                                       hs[:, j % 2, c, q * BANK:(q + 1) * BANK], start=False,
                                                       stop=False, skip_group_check=True)
                            ins.then_inc(s["ss_acc"], 1)

                    pe.wait_ge(s["ss_pool"], 4)
                    lead = AHEAD - 1
                    for j in range(lead):
                        rows(0, j)
                    with pe.Fori(0, NST // 2 - 2) as pair:
                        n = pair * 2
                        for j in range(2):
                            rows(n, j + lead)
                            add_state(n, j)
                    for n in range(NST - 4, NST):
                        if n + lead < NST:
                            rows(0, n + lead)
                        add_state(0, n)
                        if half + 1 < HALVES:
                            if n == NST - 4:
                                pe.wait_ge(s["ss_rows"], NST * (half + 1))
                            conv(half + 1, (n - NST + 4) // 2, n % 2)
                    for q in range(2):
                        for t in range(4):
                            for c in range(CH):
                                pe.wait_ge(s["ss_y"], CH * (half + 1))
                                ins = nc.tensor.matmul(ps[:, 4 + q, t * P:(t + 1) * P],
                                                       y[:, c, (4 * q + t) * P:(4 * q + t + 1) * P], w.out_w[:, c, :],
                                                       start=(t == 0 and c == 0), stop=(c == CH - 1),
                                                       skip_group_check=True)
                    ins.then_inc(s["ss_o"], 1)

            @block.scalar
            def _(act):
                def gates(half):
                    for c in range(CH):
                        act.wait_ge(s["ss_res"], CH * half + c + 1)
                        nc.scalar.activation(gate[:, c, :], ps[:, 4 + 2 * c:6 + 2 * c, :].rearrange("p a b -> p (a b)"),
                                             ACT.Silu).then_inc(s["ss_gate"], 1)

                def copy_dt(half):
                    act.wait_ge(s["ss_dt"], half + 1)
                    nc.scalar.activation(dt_in, ps[0:DTR, 0:2, :].rearrange("p a b -> p (a b)"),
                                         ACT.Copy).then_inc(s["ss_dtin"], 1)

                for half in range(HALVES):
                    for c in range(CH):
                        act.wait_ge(s["ss_xs"], CH * half + c + 1)
                        nc.scalar.activation(u[:, c, :], ps[:, 2 * c:2 * c + 2, :].rearrange("p a b -> p (a b)"),
                                             ACT.Silu, bias=w.conv_b[:, c:c + 1]).then_inc(s["ss_u"], 1)
                    if half:
                        copy_dt(half)
                        act.wait_ge(s["ss_y"], CH * half)
                        gates(half)
                    else:
                        gates(half)
                        copy_dt(half)
                    act.wait_ge(s["ss_z"], half + 1)
                    for c in range(CH):
                        nc.scalar.activation(t_abs[:, c, :], ps[:, 4 + 2 * c:6 + 2 * c, :].rearrange("p a b -> p (a b)"),
                                             ACT.Abs, bias=w.dt_b[:, c:c + 1]).then_inc(s["ss_abs"], 1)
                    act.wait_ge(s["ss_abs"], CH * (half + 1))
                    nc.scalar.activation(t_abs[:], t_abs[:], ACT.Exp, scale=-1.0).then_inc(s["ss_expn"], 1)
                    act.wait_ge(s["ss_expn"], half + 1)
                    for c in range(CH):
                        nc.scalar.activation(t_abs[:, c, :], t_abs[:, c, :], ACT.Ln, bias=1.0).then_inc(s["ss_sp"], 1)
                    base = half * NST
                    act.wait_ge(s["ss_delta"], CH * (half + 1))
                    if half == 0:
                        act.wait_ge(s["ss_pool"], 1)
                        act.sem_inc(s["ss_free"], AHEAD)
                    with act.Fori(0, NST // AHEAD) as turn:
                        n = turn * AHEAD
                        for j in range(AHEAD):
                            act.wait_ge(s["ss_free"], n + (base + j + 1))
                            for c in range(CH):
                                nc.scalar.activation(
                                    da[:, j, c, :, 1:], delta[:, c, :].rearrange("p (b t) -> p b t", b=HB)[:, :, 1:],
                                    ACT.Exp, scale=w.a_log[:, c, bass.ds(n + j, 1)]).then_inc(s["ss_da"], 1)
                            act.wait_ge(s["ss_pick"], n + (base + j + 1))
                            nc.scalar.activation(bs[:, j, :], ps[:, 0:2, :].rearrange("p a b -> p (a b)"), ACT.Copy)
                            nc.scalar.activation(cs[:, j, :], ps[:, 2:4, :].rearrange("p a b -> p (a b)"),
                                                 ACT.Copy).then_inc(s["ss_rows"], 1)


def lora_ffn(nc, m, name, prefetch=None):
    w = m.w
    with ExitStack() as own:
        def sb(n, shape, dt=F32):
            return own.enter_context(nc.sbuf_tensor(f"{name}_{n}", shape, dt))

        logits_t = sb("logits_t", [P, BANK])
        down_t = sb("lora_down_t", [P, BANK])
        logits = sb("logits", [P, TILES, EXP])
        best = sb("best", [P, TILES])
        hot = sb("hot", [P, TILES, EXP])
        hot_wide = sb("hot_wide", [P, GT, GROUPS, ER])
        order = sb("order", [P, EXP])
        h = sb("h", [P, 2, FT, BANK])
        k = sems(nc, own, "order g lc dc lt st hot ht dt hp h o x", f"{name}_")
        ps = m.ps
        DOWN, LOG, LOG_TOK, HOT = 0, 1, 2, 3
        hidden_banks = (4, 5, 6, 7, 2, 3)
        HB_N = len(hidden_banks)

        with nc.Block() as block:
            if prefetch:
                @block.sync
                def _(sp):
                    prefetch(sp)

            @block.gpsimd
            def _(pool):
                nc.gpsimd.iota(order[:], [[-1, EXP]], base=EXP, channel_multiplier=0,
                               allow_small_or_imprecise_dtypes=True).then_inc(k["order"], 1)
                nc.gpsimd.tensor_tensor(m.x[:], m.x[:], w.wo_b[:].rearrange("p (a d) -> p a d", a=1)
                                        .to_broadcast([P, TILES, DIM]), ALU.add).then_inc(k["order"], 1)

            def up(g, f):
                bank = hidden_banks[(g * FT + f) % HB_N]
                nc.tensor.matmul(ps[:, bank, :], w.wi[:, f * P:(f + 1) * P], m.xt[:, 2 * g:2 * g + 2, PAD:],
                                 start=True, stop=False, skip_group_check=True)

            def lora(g, f):
                bank = hidden_banks[(g * FT + f) % HB_N]
                nc.tensor.matmul(ps[:, bank, :], w.lora_b[:, g, f * P:(f + 1) * P], down_t[:], start=False, stop=True,
                                 skip_group_check=True).then_inc(k["hp"], 1)

            def second(pe, g):
                pe.wait_ge(k["h"], FT * (g + 1))
                if g >= 2:
                    pe.wait_ge(k["x"], g - 1)
                for t in range(GT):
                    for f in range(FT):
                        ins = nc.tensor.matmul(ps[:, g % 2, t * P:(t + 1) * P], h[:, g % 2, f, t * P:(t + 1) * P],
                                               w.wo[:, f, :], start=(t == 0 and f == 0), stop=(f == FT - 1),
                                               skip_group_check=True)
                ins.then_inc(k["o"], 1)

            @block.tensor
            def _(pe):
                for bank, first in ((LOG, ER), (DOWN, 0)):
                    for g in range(GROUPS):
                        ins = nc.tensor.matmul(ps[32 * g:32 * g + 32, bank, :], w.gate[:, first:first + 32],
                                               m.xt[:, 2 * g:2 * g + 2, PAD:], start=True, stop=True,
                                               skip_group_check=True)
                    ins.then_inc(k["g"], 1)
                up(0, 0)
                up(0, 1)
                pe.wait_ge(k["lc"], 1)
                for c in range(GT):
                    ins = nc.tensor.transpose(ps[:, LOG_TOK, c * P:(c + 1) * P], logits_t[:, c * P:(c + 1) * P], m.ident[:])
                ins.then_inc(k["lt"], 1)
                up(0, 2)
                up(0, 3)
                pe.wait_ge(k["hot"], 1)
                for c in range(GT):
                    ins = nc.tensor.transpose(ps[:, HOT, c * P:(c + 1) * P],
                                              hot_wide[:, c].rearrange("p g r -> p (g r)"), m.ident[:])
                ins.then_inc(k["ht"], 1)
                pe.wait_ge(k["dt"], 1)
                for g in range(GROUPS):
                    for f in range(FT):
                        n = g * FT + f
                        if g:
                            if n >= HB_N:
                                pe.wait_ge(k["h"], n - HB_N + 1)
                            up(g, f)
                        lora(g, f)
                    if g:
                        second(pe, g - 1)
                second(pe, GROUPS - 1)

            @block.scalar
            def _(act):
                act.wait_ge(k["g"], 1)
                nc.scalar.activation(logits_t[:], ps[:, LOG, :], ACT.Copy).then_inc(k["lc"], 1)
                act.wait_ge(k["g"], 2)
                nc.scalar.activation(down_t[:], ps[:, DOWN, :], ACT.Copy).then_inc(k["dc"], 1)
                for g in range(GROUPS):
                    for f in range(FT):
                        n = g * FT + f
                        act.wait_ge(k["hp"], n + 1)
                        if g >= 2 and f == 0:
                            act.wait_ge(k["o"], g - 1)
                        nc.scalar.activation(h[:, g % 2, f, :], ps[:, hidden_banks[n % HB_N], :], ACT.Relu,
                                             bias=w.wi_b[:, f:f + 1]).then_inc(k["h"], 1)

            @block.vector
            def _(dve):
                dve.wait_ge(k["lt"], 1)
                by_tile = ps[:, LOG_TOK, :].rearrange("p (c g e) -> p c g e", c=GT, e=32)
                for c in range(GT):
                    ins = nc.vector.tensor_tensor(
                        logits[:].rearrange("p (g c) e -> p c g e", c=GT)[:, c], by_tile[:, c, :, 0:EXP],
                        w.gate_b[:].rearrange("p (a e) -> p a e", a=1).to_broadcast([P, GROUPS, EXP]), ALU.add)
                ins.then_inc(k["st"], 1)
                pick_first(nc, dve, k["st"], 1, k["order"], logits, best, hot, order)
                for c in range(GT):
                    ins = nc.vector.tensor_copy(
                        hot_wide[:, c].rearrange("p g (e r) -> p g e r", r=RANK),
                        hot[:].rearrange("p (g c) e -> p c g e", c=GT)[:, c].rearrange("p g (e a) -> p g e a", a=1)
                        .to_broadcast([P, GROUPS, EXP, RANK]))
                ins.then_inc(k["hot"], 1)
                dve.wait_ge(k["ht"], 1)
                dve.wait_ge(k["dc"], 1)
                nc.vector.tensor_tensor(down_t[:], down_t[:], ps[:, HOT, :], ALU.mult).then_inc(k["dt"], 1)
                dve.wait_ge(k["order"], 2)
                for g in range(GROUPS):
                    dve.wait_ge(k["o"], g + 1)
                    xg = m.x[:, g * GT:(g + 1) * GT, :].rearrange("p t d -> p (t d)")
                    nc.vector.tensor_tensor(xg, xg, ps[:, g % 2, :], ALU.add).then_inc(k["x"], 1)


def pick_first(nc, dve, step, n, order_ready, logits, best, hot, order):
    wide = [P, TILES, EXP]

    def over(t):
        return t[:].rearrange("p (t a) -> p t a", a=1).to_broadcast(wide)

    dve.wait_ge(step, n)
    nc.vector.tensor_reduce(best[:], logits[:], AX.X, ALU.max).then_inc(step, 1)
    dve.wait_ge(step, n + 1)
    nc.vector.tensor_tensor(hot[:], logits[:], over(best), ALU.is_equal).then_inc(step, 1)
    dve.wait_ge(step, n + 2)
    dve.wait_ge(order_ready, 1)
    nc.vector.tensor_tensor(hot[:], hot[:], order[:].rearrange("p (a e) -> p a e", a=1).to_broadcast(wide),
                            ALU.mult).then_inc(step, 1)
    dve.wait_ge(step, n + 3)
    nc.vector.tensor_reduce(best[:], hot[:], AX.X, ALU.max).then_inc(step, 1)
    dve.wait_ge(step, n + 4)
    nc.vector.tensor_tensor(hot[:], hot[:], over(best), ALU.is_equal).then_inc(step, 1)
    dve.wait_ge(step, n + 5)


def load_toeplitz(sp, m):
    n = DIM // TOEPLITZ_LOADS
    sp.wait_ge(m.kernels_stored, 16)
    for c in range(TOEPLITZ_LOADS):
        src = bass.AP(m.kernel_dram.tensor, c * n * 2 * P, [[1, P], [2 * P, n], [1, P]])
        sp.dma_start(m.toeplitz[:, c * n:(c + 1) * n, :], src).then_inc(m.toeplitz_loaded, 16)


def long_conv(nc, m):
    w = m.w
    with ExitStack() as own:
        def sb(name, shape, dt=F32):
            return own.enter_context(nc.sbuf_tensor(name, shape, dt))

        ud = sb("lc_skip", [P, TILES, DIM])
        state = sb("lc_state", [LNST, DIM, BATCH])
        y = sb("lc_y", [P, TILES, DIM])
        back = sb("lc_reversed", [P, 32, DIM])
        yt = sb("lc_y_t", [P, 2, BANK])
        flip = sb("lc_flip", [P, P])
        k = sems(nc, own, "lc_zero lc_fz lc_flip lc_bp lc_back lc_ud lc_hp lc_hc lc_yp lc_y lc_tp lc_tc lc_st lc_stats lc_pow lc_shift "
                          "lc_xn lc_gain lc_beta")
        ps = m.ps
        step = k["lc_st"]
        BANKS = 8
        CB = DIM // BANKS
        with nc.Block() as block:
            def row(w, i, tiles=TILES):
                return w.lc_rows[:, i:i + 1, :].to_broadcast([P, tiles, DIM])

            @block.gpsimd
            def _(pool):
                nc.gpsimd.memset(flip[:], 0.0).then_inc(k["lc_zero"], 1)
                pool.wait_ge(k["lc_zero"], 1)
                nc.gpsimd.affine_select(out=flip[:], in_=flip[:], compare_op=ALU.not_equal, fill=1.0, base=1 - P,
                                        pattern=[[1, P]], channel_multiplier=1).then_inc(k["lc_flip"], 1)
                nc.gpsimd.tensor_tensor(ud[:], m.xn[:], row(w, 0), ALU.mult).then_inc(k["lc_ud"], 1)
                nc.gpsimd.tensor_tensor(m.x[:], m.x[:], row(w, 4), ALU.add).then_inc(k["lc_beta"], 1)
                for g in range(GROUPS):
                    group_power(nc, pool, m, g, k["lc_stats"], k["lc_pow"])
                    group_shift(nc, pool, m, g, k["lc_pow"], k["lc_shift"])

            @block.tensor
            def _(pe):
                first = m.xn[:].rearrange("p (b h) d -> p h b d", h=2)[:, 0]
                for i in range(2):
                    ins = nc.tensor.matmul(ps[0:LNST, 4 + i, :], m.lc_powt[:], first[:, 4 * i:4 * i + 4, :], start=True, stop=True)
                ins.then_inc(k["lc_hp"], 1)
                pe.wait_ge(k["lc_flip"], 1)
                for g in range(GROUPS):
                    nc.tensor.matmul(ps[:, g, :], flip[:], m.xn[:, g * GT:(g + 1) * GT, :], start=True,
                                     stop=True).then_inc(k["lc_bp"], 1)
                pe.wait_ge(m.toeplitz_loaded, 16 * TOEPLITZ_LOADS)
                pe.wait_ge(k["lc_back"], GROUPS)
                pe.wait_ge(k["lc_fz"], 1)

                def turn(q):
                    pe.wait_ge(k["lc_tc"], q + 1)
                    if q == 0:
                        pe.wait_ge(k["lc_hc"], 1)
                    for block in range(4):
                        nc.tensor.matmul(ps[:, q, block * P:(block + 1) * P], yt[:, q % 2, block * P:(block + 1) * P],
                                         m.ident[:], start=(block == 0), stop=False, skip_group_check=True)
                    out = ps[:, q, :].rearrange("p (d b h) -> p d b h", b=16, h=2)[:, :, 0:BATCH, 1]
                    nc.tensor.matmul(out, m.lc_pow[:, 1:], state[:, CB * q:CB * q + CB, :], start=False, stop=True,
                                     skip_group_check=True).then_inc(k["lc_yp"], 1)

                for q in range(BANKS):
                    if q == 4:
                        pe.wait_ge(k["lc_hc"], 1)
                    for i in range(CB):
                        d, rows, block = CB * q + i, slice(32 * (i % 4), 32 * (i % 4) + 32), i // 4
                        ins = nc.tensor.matmul(ps[rows, q, block * P:(block + 1) * P], back[:, :, d],
                                               m.toeplitz[:, d, :], start=(block == 0), stop=True,
                                               skip_group_check=True)
                    ins.then_inc(k["lc_tp"], 1)
                    if q:
                        turn(q - 1)
                turn(BANKS - 1)

            @block.scalar
            def _(act):
                for g in range(GROUPS):
                    act.wait_ge(k["lc_bp"], g + 1)
                    nc.scalar.activation(back[:, g * GT:(g + 1) * GT, :].rearrange("p t d -> p (t d)"), ps[:, g, :],
                                         ACT.Copy).then_inc(k["lc_back"], 1)
                for q in range(BANKS):
                    act.wait_ge(k["lc_tp"], q + 1)
                    if q >= 2:
                        act.wait_ge(k["lc_yp"], q - 1)
                    nc.scalar.activation(yt[:, q % 2, :], ps[:, q, :], ACT.Copy).then_inc(k["lc_tc"], 1)
                for g in range(GROUPS):
                    group_scale_by_act(nc, act, m, y, y, g, k["lc_shift"], k["lc_xn"])

            @block.vector
            def _(dve):
                nc.vector.memset(back[:, TILES:, :], 0.0).then_inc(k["lc_fz"], 1)
                dve.wait_ge(k["lc_hp"], 1)
                src = ps[0:LNST, 4:6, :].rearrange("n a (b d) -> n d (a b)", b=4)
                nc.vector.tensor_tensor(state[:], src, w.lc_ct[:].rearrange("n (d a) -> n d a", a=1)
                                        .to_broadcast([LNST, DIM, BATCH]), ALU.mult).then_inc(k["lc_hc"], 1)
                dve.wait_ge(k["lc_ud"], 1)
                for q in range(BANKS):
                    dve.wait_ge(k["lc_yp"], q + 1)
                    chans = slice(CB * q, CB * q + CB)
                    ins = nc.vector.tensor_tensor(
                        y[:, :, chans], ps[:, q, :].rearrange("p (d t) -> p t d", t=32)[:, 0:TILES, :],
                        ud[:, :, chans], ALU.add)
                ins.then_inc(step, 1)
                dve.wait_ge(step, 1)
                y0 = y[0:1].rearrange("p (b h) d -> p h b d", h=2)[:, 0]
                nc.vector.tensor_tensor(y0, y0, w.lc_rows[0:1, 2:3, :].to_broadcast([1, BATCH, DIM]),
                                        ALU.add).then_inc(step, 1)
                dve.wait_ge(step, 2)

                def finish(g):
                    tiles = slice(g * GT, (g + 1) * GT)
                    dve.wait_ge(k["lc_xn"], g + 1)
                    nc.vector.tensor_tensor(y[:, tiles, :], y[:, tiles, :], row(w, 3, GT), ALU.mult)\
                        .then_inc(k["lc_gain"], 1)
                    dve.wait_ge(k["lc_gain"], g + 1)
                    nc.vector.tensor_tensor(m.x[:, tiles, :], m.x[:, tiles, :], y[:, tiles, :], ALU.add)

                dve.wait_ge(k["lc_beta"], 1)
                for g in range(GROUPS):
                    group_stats(nc, dve, m, y, g, k["lc_stats"])
                    if g >= 2:
                        finish(g - 2)
                finish(GROUPS - 2)
                finish(GROUPS - 1)


def allowed_pairs():
    pos = np.arange(SEQ)
    chunk = pos // CHUNK_FRAMES
    return (chunk[None, :] <= chunk[:, None]) | (pos[None, :] <= pos[:, None] + LOOKAHEAD)


def attention(nc, m, name, dram, a, rope):
    JS, GS = 4, HEADS // 4
    KT = SEQ // P
    PARTS = 3
    STACK = PARTS * PARTS * HD
    MAX_ROW = 96
    ROWS = MAX_ROW + PARTS * GS
    PUT, GOT = 16 * 2 * PARTS, 16 * (PARTS + 1)
    SCALE = float(HD) ** -0.5
    MASKED = not rope
    hidden = ~allowed_pairs()
    first_key = [int(np.flatnonzero(hidden[i * P:(i + 1) * P].any(0))[0]) for i in range(KT)]
    end_query = [int(np.flatnonzero(hidden[:, i * P:(i + 1) * P].any(1))[-1]) + 1 for i in range(KT)]
    with ExitStack() as own:
        def sb(n, shape, dt=F32):
            return own.enter_context(nc.sbuf_tensor(f"{name}_{n}", shape, dt))

        xb = sb("xb", [P, 2, SEQ])
        t1 = sb("rot1", [P, 2, SEQ])
        t2 = sb("rot2", [P, 2, SEQ])
        qk = sb("qk", [P, 2, SEQ])
        qk_rest = sb("qk_rest", [P, 2, SEQ])
        parts = sb("qk_parts", [P, PARTS, 2, SEQ], BF16)
        q_stack = sb("q_stack", [ROWS, 2, HEADS, SEQ], BF16)
        k_stack = sb("k_stack", [ROWS, 2, HEADS, SEQ], BF16)
        v = sb("v", [P, 2, KT, HEADS, 32])
        mx = sb("max", [P, KT, GS])
        res = sb("max_rest", [P, KT, GS])
        split = sb("max_split", [P, KT, 3, GS], BF16)
        e = sb("e", [P, 2, KT, GS, SEQ])
        o_heads = sb("o_heads", [P, SEQ])
        rs = sb("rsum", [P, KT, GS])
        on = sb("o", [P, 2, KT, DIM])
        ont = sb("o_t", [P, SEQ])
        k = sems(nc, own, "part sel zr vz bias xb qp kp vp qd kd p1 p2 pt put got v sq mx ms mtp mtc st ex pv oc to rs nm tu tc out xa",
                 f"{name}_")
        scratch = nc.dram_tensor(f"{name}_parts", (2, PARTS, HD, HEADS, SEQ), BF16, kind="Internal").ap()
        ps = m.ps
        SQ, ST, OB, MISC = (0, 1), (2, 4), 6, 7
        misc = ps[:, MISC, :]
        mtp = ps[MAX_ROW:ROWS, MISC, 0:SEQ // 2].bitcast(BF16)
        o_psum = ps[:, OB, 0:SEQ]
        turned = ps[:, OB, SEQ:].rearrange("p (i g c) -> p i g c", i=KT, g=GS)

        def pe_qk(pe, b, r, ws, done):
            for n, wt in enumerate(ws):
                ins = nc.tensor.matmul(misc[:, n * SEQ:(n + 1) * SEQ], wt[:], xb[:, r, :], start=(n == 0), stop=True,
                                       skip_group_check=True)
            ins.then_inc(done, 1)

        def pe_q(pe, b, r):
            pe.wait_ge(k["xb"], b + 1)
            pe_qk(pe, b, r, (a.wq1, a.wq2) if rope else (a.wq1,), k["qp"])

        def pe_k(pe, b, r):
            pe_qk(pe, b, r, (a.wk1, a.wk2) if rope else (a.wk1,), k["kp"])

        def pe_v(pe, b, r):
            for i in range(KT):
                ins = nc.tensor.matmul(misc[:, i * P:(i + 1) * P], xb[:, r, i * P:(i + 1) * P], a.wv[:],
                                       start=(i == 0), stop=True, skip_group_check=True)
            ins.then_inc(k["vp"], 1)

        def pe_sq(pe, s, j, r, i):
            qt, pair = i // 2, i % 2
            if not (isinstance(s, int) and s == 0 and i < 2):
                pe.wait_ge(k["mx"], s * 4 + i - 1)
            bank = ps[:, SQ[i % 2], :]
            if MASKED:
                lo = first_key[qt]
                nc.tensor.matmul(bank.rearrange("p (c t) -> p c t", c=2)[:, :, lo:], m.identb[:],
                                 a.mask_q[:, qt:qt + 1, lo:].to_broadcast([P, 2, SEQ - lo]), start=True, stop=False,
                                 skip_group_check=True)
            for c in range(2):
                h = 4 * j + 2 * pair + c
                ins = nc.tensor.matmul(bank[:, c * SEQ:(c + 1) * SEQ], q_stack[0:STACK, r, h, qt * P:(qt + 1) * P],
                                       k_stack[0:STACK, r, h, :], start=(c == 0 and not MASKED), stop=True,
                                       skip_group_check=True)
            ins.then_inc(k["sq"], 1)

        def pe_mt(pe, s):
            pe.wait_ge(k["ms"], s + 1)
            for i in range(KT):
                ins = nc.tensor.transpose(mtp[:, i * P:(i + 1) * P], split[:, i, :, :].rearrange("p c g -> p (c g)"),
                                          m.identb[:])
            ins.then_inc(k["mtp"], 1)

        def pe_st(pe, s, j, r, i):
            if not (isinstance(s, int) and s == 0):
                pe.wait_ge(k["ex"], s * KT + i - 1)
            banks = ps[:, ST[i]:ST[i] + 2, :]
            if MASKED:
                hi = end_query[i]
                for c in range(2):
                    nc.tensor.matmul(banks[:, c, :].rearrange("p (g t) -> p g t", g=2)[:, :, 0:hi], m.identb[:],
                                     a.mask_k[:, i:i + 1, 0:hi].to_broadcast([P, 2, hi]), start=True, stop=False,
                                     skip_group_check=True)
            for g in range(GS):
                h = 4 * j + g
                ins = nc.tensor.matmul(banks[:, g // 2, (g % 2) * SEQ:(g % 2 + 1) * SEQ],
                                       k_stack[:, r, h, i * P:(i + 1) * P], q_stack[:, r, h, :],
                                       start=(g % 2 == 0 and not MASKED), stop=True, skip_group_check=True)
            ins.then_inc(k["st"], 1)

        def pe_pv(pe, s, j, r, between=None):
            if not (isinstance(s, int) and s == 0):
                pe.wait_ge(k["nm"], s)
            for i in range(KT):
                pe.wait_ge(k["ex"], s * KT + i + 1)
                for g in range(GS):
                    ins = nc.tensor.matmul(o_psum[32 * g:32 * g + 32, :], v[:, r, i, 4 * j + g, :],
                                           e[:, j % 2, i, g, :], start=(i == 0), stop=(i == KT - 1),
                                           skip_group_check=True)
                if i == 0 and between:
                    between()
            ins.then_inc(k["pv"], 1)

        def pe_to(pe, s):
            pe.wait_ge(k["oc"], s + 1)
            for i in range(KT):
                ins = nc.tensor.transpose(ps[:, OB, SEQ + i * P:SEQ + (i + 1) * P], o_heads[:, i * P:(i + 1) * P],
                                          m.ident[:])
            ins.then_inc(k["to"], 1)

        def pe_turn(pe, b, r):
            pe.wait_ge(k["nm"], b * JS + JS)
            for i in range(KT):
                ins = nc.tensor.transpose(misc[:, i * P:(i + 1) * P], on[:, r, i, :], m.ident[:])
            ins.then_inc(k["tu"], 1)

        def pe_out(pe, b):
            pe.wait_ge(k["tc"], b + 1)
            for i in range(KT):
                ins = nc.tensor.matmul(misc[:, i * P:(i + 1) * P], ont[:, i * P:(i + 1) * P], a.wo[:],
                                       start=(i == 0), stop=True, skip_group_check=True)
            ins.then_inc(k["out"], 1)

        def pe_step(pe, b, j, r, first, last, project=False):
            s = b * JS + j
            more = not (last and j == JS - 1)
            nj, nr = ((j + 1), r) if j < JS - 1 else (0, 1 - r)
            project_v, finish = j == 1 and not last, j == 2 and not first
            if more:
                if j == JS - 1:
                    pe.wait_ge(k["got"], b * GOT + 2 * GOT)
                pe_sq(pe, s + 1, nj, nr, 0)
                pe_sq(pe, s + 1, nj, nr, 1)
            pe.wait_ge(k["mtc"], s + 1)
            if project:
                pe_q(pe, b + 2, r)
            if project_v:
                pe_v(pe, b + 1, 1 - r)
            if finish:
                pe_turn(pe, b - 1, 1 - r)
            pe_st(pe, s, j, r, 0)
            if more:
                pe_sq(pe, s + 1, nj, nr, 2)
                pe_sq(pe, s + 1, nj, nr, 3)
            if not (first and j <= 1):
                pe_to(pe, s - 2)
            pe_st(pe, s, j, r, 1)
            if project:
                pe.wait_ge(k["qd"], b + 3)
                pe_k(pe, b + 2, r)
            if finish:
                pe_out(pe, b - 1)

            def next_maxima():
                if project:
                    pe.wait_ge(k["kd"], b + 3)
                if project_v:
                    pe.wait_ge(k["v"], b + 2)
                if finish:
                    pe.wait_ge(k["xa"], b)
                pe_mt(pe, s + 1)

            if not (first and j == 0):
                if j == 1:
                    pe.wait_ge(k["v"], b + 1)
                pe_pv(pe, s - 1, (j - 1) % JS, r if j > 0 else 1 - r, next_maxima if more else None)
            else:
                next_maxima()

        def window(step, eng, b, r, first, last):
            if not first:
                step(eng, b - 1, JS - 1, 1 - r, False, False, project=not last)
            for j in range(JS - 1):
                step(eng, b, j, r, first, last)

        def dve_qk(dve, b, n, read):
            if not (isinstance(b, int) and b == 0):
                dve.wait_ge(k["pt"], b)
            if rope:
                nc.vector.tensor_tensor(t1[:, n, :], misc[:, 0:SEQ], a.cos[:], ALU.mult)
                nc.vector.tensor_tensor(t2[:, n, :], misc[:, SEQ:], a.sin[:], ALU.mult).then_inc(read, 1)
            else:
                if not (isinstance(b, int) and b == 0):
                    dve.wait_ge(k["put"], b * PUT)
                for dst in (qk[:, n, :], parts[:, 0, n, :]):
                    if n == 0:
                        ins = nc.vector.tensor_scalar(dst, misc[:, 0:SEQ], a.bq[:, 0:1], None, ALU.add)
                    else:
                        ins = nc.vector.tensor_copy(dst, misc[:, 0:SEQ])
                ins.then_inc(read, 1)

        def dve_q(dve, b):
            dve.wait_ge(k["qp"], b + 1)
            dve_qk(dve, b, 0, k["qd"])

        def dve_k(dve, b):
            dve.wait_ge(k["kp"], b + 1)
            dve_qk(dve, b, 1, k["kd"])

        def dve_v(dve, b, r):
            dve.wait_ge(k["vp"], b + 1)
            if not (isinstance(b, int) and b <= 1):
                dve.wait_ge(k["pv"], (b - 1) * JS)
            for i in range(KT):
                ins = nc.vector.tensor_tensor(
                    v[:, r, i, :, 0:HD], misc[:, i * P:(i + 1) * P].rearrange("p (h e) -> p h e", e=HD),
                    a.bv[:].rearrange("p (h e) -> p h e", e=HD), ALU.add)
            ins.then_inc(k["v"], 1)

        def dve_max(dve, s, i):
            qt, pair = i // 2, i % 2
            dve.wait_ge(k["sq"], s * 4 + i + 1)
            if i == 0 and not (isinstance(s, int) and s == 0):
                dve.wait_ge(k["ms"], s)
            nc.vector.tensor_reduce(mx[:, qt, 2 * pair:2 * pair + 2],
                                    ps[:, SQ[i % 2], :].rearrange("p (c t) -> p c t", c=2), AX.X,
                                    ALU.max).then_inc(k["mx"], 1)

        def dve_split(dve, s):
            if not (isinstance(s, int) and s == 0):
                dve.wait_ge(k["mtp"], s)
            dve.wait_ge(k["mx"], s * 4 + 4)
            nc.vector.tensor_scalar(split[:, :, 0, :], mx[:], -1.0, None, ALU.mult).then_inc(k["part"], 1)
            dve.wait_ge(k["part"], s * 3 + 1)
            nc.vector.scalar_tensor_tensor(out=res[:], in0=mx[:], scalar=-1.0, in1=split[:, :, 0, :], op0=ALU.mult,
                                           op1=ALU.subtract).then_inc(k["part"], 1)
            dve.wait_ge(k["part"], s * 3 + 2)
            nc.vector.tensor_copy(split[:, :, 1, :], res[:]).then_inc(k["part"], 1)
            dve.wait_ge(k["part"], s * 3 + 3)
            nc.vector.tensor_tensor(split[:, :, 2, :], res[:], split[:, :, 1, :], ALU.subtract)\
                .then_inc(k["ms"], 1)

        def dve_norm(dve, s, j, r):
            dve.wait_ge(k["to"], s + 1)
            nc.vector.reciprocal(rs[:], turned[:, :, :, HD]).then_inc(k["rs"], 1)
            dve.wait_ge(k["rs"], s + 1)
            nc.vector.tensor_tensor(on[:, r, :, 32 * j:32 * j + 32].rearrange("p i (g e) -> p i g e", g=GS),
                                    turned[:, :, :, 0:HD],
                                    rs[:].rearrange("p i (g a) -> p i g a", a=1).to_broadcast([P, KT, GS, HD]),
                                    ALU.mult).then_inc(k["nm"], 1)

        def dve_add(dve, b):
            dve.wait_ge(k["out"], b + 1)
            dve.wait_ge(k["bias"], 1)
            xs = m.x[:, bass.ds(b * 2, 2), :] if not isinstance(b, int) else m.x[:, 2 * b:2 * b + 2, :]
            nc.vector.tensor_tensor(xs, xs, misc[:, 0:SEQ].rearrange("p (t d) -> p t d", t=2),
                                    ALU.add).then_inc(k["xa"], 1)

        def dve_step(dve, b, j, r, first, last, project=False):
            s = b * JS + j
            more = not (last and j == JS - 1)
            if more:
                dve_max(dve, s + 1, 0)
                dve_max(dve, s + 1, 1)
            if project:
                dve_q(dve, b + 2)
            if j == 1 and not last and not rope:
                dve_v(dve, b + 1, 1 - r)
            if more:
                dve_max(dve, s + 1, 2)
                dve_max(dve, s + 1, 3)
            if not (first and j <= 1):
                dve_norm(dve, s - 2, (j - 2) % JS, r if j >= 2 else 1 - r)
            if more:
                dve_split(dve, s + 1)
            if project:
                dve_k(dve, b + 2)
            if j == 2 and not first:
                dve_add(dve, b - 1)

        def act_mt(act, s, j, r):
            act.wait_ge(k["mtp"], s + 1)
            nc.scalar.activation(q_stack[MAX_ROW:ROWS, r, 4 * j:4 * j + GS, :],
                                 mtp.rearrange("p (a t) -> p a t", a=1).to_broadcast([PARTS * GS, GS, SEQ]),
                                 ACT.Copy).then_inc(k["mtc"], 1)

        def act_v(act, b, r):
            act.wait_ge(k["vp"], b + 1)
            if not (isinstance(b, int) and b <= 1):
                act.wait_ge(k["pv"], (b - 1) * JS)
            nc.scalar.activation(v[:, r, :, :, 0:HD], misc[:, 0:SEQ].rearrange("p (i h e) -> p i h e", i=KT, e=HD),
                                 ACT.Copy).then_inc(k["v"], 1)

        def act_exp(act, s, j):
            for i in range(KT):
                act.wait_ge(k["st"], s * KT + i + 1)
                if i == 0 and not (isinstance(s, int) and s <= 1):
                    act.wait_ge(k["pv"], s - 1)
                nc.scalar.activation(e[:, j % 2, i, :, :].rearrange("p g t -> p (g t)"),
                                     ps[:, ST[i]:ST[i] + 2, :].rearrange("p a b -> p (a b)"), ACT.Exp,
                                     scale=SCALE).then_inc(k["ex"], 1)

        def act_oc(act, s):
            act.wait_ge(k["pv"], s + 1)
            if not (isinstance(s, int) and s == 0):
                act.wait_ge(k["to"], s)
            nc.scalar.activation(o_heads[:], o_psum, ACT.Copy).then_inc(k["oc"], 1)

        def act_turn(act, b):
            act.wait_ge(k["tu"], b + 1)
            nc.scalar.activation(ont[:], misc[:, 0:SEQ], ACT.Copy).then_inc(k["tc"], 1)

        def act_step(act, b, j, r, first, last, project=False):
            s = b * JS + j
            if j == 1 and not last and rope:
                act_v(act, b + 1, 1 - r)
            if j == 2 and not first:
                act_turn(act, b - 1)
            act_exp(act, s, j)
            if not (last and j == JS - 1):
                act_mt(act, s + 1, (j + 1) % JS, r if j < JS - 1 else 1 - r)
            if not (first and j == 0):
                act_oc(act, s - 1)

        def pool_xb(pool, b, r):
            if not (isinstance(b, int) and b <= 1):
                pool.wait_ge(k["vp"], b - 1)
            src = m.xt[:, b, PAD:] if isinstance(b, int) else \
                m.xt[:, bass.ds(b, 1), PAD:].rearrange("p a t -> p (a t)")
            nc.gpsimd.tensor_copy(xb[:, r, :], src).then_inc(k["xb"], 1)

        def pool_parts(pool, b):
            pool.wait_ge(k["kd"], b + 1)
            if not (isinstance(b, int) and b == 0):
                pool.wait_ge(k["put"], b * PUT)
            if rope:
                nc.gpsimd.tensor_tensor(parts[:, 0, :, :], t1[:], t2[:], ALU.add)
                nc.gpsimd.tensor_tensor(qk[:], t1[:], t2[:], ALU.add).then_inc(k["p1"], 1)
                pool.wait_ge(k["p1"], b + 1)
            nc.gpsimd.tensor_tensor(parts[:, 1, :, :], qk[:], parts[:, 0, :, :], ALU.subtract)
            nc.gpsimd.tensor_tensor(qk_rest[:], qk[:], parts[:, 0, :, :], ALU.subtract).then_inc(k["p2"], 1)
            pool.wait_ge(k["p2"], b + 1)
            nc.gpsimd.tensor_tensor(parts[:, 2, :, :], qk_rest[:], parts[:, 1, :, :], ALU.subtract)\
                .then_inc(k["pt"], 1)

        def sp_stacks(sp, b, r):
            if isinstance(b, int) and b == 1:
                sp.wait_ge(k["got"], GOT)
            for c, ready in enumerate((k["p1"] if rope else k["kd"], k["p2"], k["pt"])):
                sp.wait_ge(ready, b + 1)
                for n in range(2):
                    sp.dma_start(scratch[n, c].rearrange("d h t -> h d t"), parts[:, c, n, :]).then_inc(k["put"], 16)
            sp.wait_ge(k["put"], b * PUT + PUT)
            if not (isinstance(b, int) and b <= 1):
                sp.wait_ge(k["put"], PUT)
                sp.wait_ge(k["st"], (b - 1) * JS * KT)
            row = HEADS * SEQ
            k_part = bass.AP(scratch.tensor, scratch[1].offset, [[0, PARTS], [row, PARTS * HD], [1, row]])
            for c in range(PARTS):
                q_part = bass.AP(scratch.tensor, scratch[0, c].offset, [[0, PARTS], [row, HD], [1, row]])
                rows = slice(c * PARTS * HD, (c + 1) * PARTS * HD)
                sp.dma_start(q_stack[rows, r, :, :].rearrange("p h t -> p (h t)"), q_part).then_inc(k["got"], 16)
            sp.dma_start(k_stack[0:STACK, r, :, :].rearrange("p h t -> p (h t)"), k_part).then_inc(k["got"], 16)

        PAIRS = (BATCH - 2) // 2
        with nc.Block() as block:
            @block.sync
            def _(sp):
                for stack in (q_stack, k_stack):
                    sp.dma_start(stack[STACK:MAX_ROW].bitcast(F32).rearrange("p r h t -> p (r h t)"),
                                 on_all_partitions(dram["zeros"], MAX_ROW - STACK)).then_inc(k["zr"], 16)
                sp_stacks(sp, 0, 0)
                sp_stacks(sp, 1, 1)
                with sp.Fori(0, PAIRS) as pair:
                    sp_stacks(sp, pair * 2 + 2, 0)
                    sp_stacks(sp, pair * 2 + 3, 1)
                sp.wait_ge(k["got"], BATCH * GOT)

            @block.tensor
            def _(pe):
                pe_q(pe, 0, 0)
                pe.wait_ge(k["qd"], 1)
                pe_k(pe, 0, 0)
                pe.wait_ge(k["kd"], 1)
                pe_v(pe, 0, 0)
                pe.wait_ge(k["v"], 1)
                pe_q(pe, 1, 1)
                pe.wait_ge(k["qd"], 2)
                pe_k(pe, 1, 1)
                pe.wait_ge(k["got"], GOT)
                for i in range(4):
                    pe_sq(pe, 0, 0, 0, i)
                pe.wait_ge(k["kd"], 2)
                pe.wait_ge(k["zr"], 32)
                pe.wait_ge(k["sel"], 1)
                pe_mt(pe, 0)
                window(pe_step, pe, 0, 0, True, False)
                with pe.Fori(0, PAIRS) as pair:
                    window(pe_step, pe, pair * 2 + 1, 1, False, False)
                    window(pe_step, pe, pair * 2 + 2, 0, False, False)
                window(pe_step, pe, BATCH - 1, 1, False, True)
                pe_step(pe, BATCH - 1, JS - 1, 1, False, True)
                pe_to(pe, BATCH * JS - 2)
                pe_pv(pe, BATCH * JS - 1, JS - 1, 1)
                pe_to(pe, BATCH * JS - 1)
                pe_turn(pe, BATCH - 1, 1)
                pe_out(pe, BATCH - 1)

            @block.vector
            def _(dve):
                nc.vector.memset(v[:], 0.0).then_inc(k["vz"], 1)
                dve.wait_ge(k["vz"], 1)
                nc.vector.memset(v[:, :, :, :, HD:HD + 1], 1.0).then_inc(k["vz"], 1)
                dve_q(dve, 0)
                dve_k(dve, 0)
                dve.wait_ge(k["vz"], 2)
                if not rope:
                    dve_v(dve, 0, 0)
                for j in range(2 * JS):
                    ins = nc.vector.tensor_copy(
                        k_stack[MAX_ROW:ROWS, j // JS, 4 * (j % JS):4 * (j % JS) + GS, :],
                        a.pick[MAX_ROW:ROWS, :].rearrange("p (g a) -> p g a", a=1).to_broadcast([PARTS * GS, GS, SEQ]))
                ins.then_inc(k["sel"], 1)
                dve_q(dve, 1)
                dve_k(dve, 1)
                for i in range(4):
                    dve_max(dve, 0, i)
                dve_split(dve, 0)
                window(dve_step, dve, 0, 0, True, False)
                with dve.Fori(0, PAIRS) as pair:
                    window(dve_step, dve, pair * 2 + 1, 1, False, False)
                    window(dve_step, dve, pair * 2 + 2, 0, False, False)
                window(dve_step, dve, BATCH - 1, 1, False, True)
                dve_step(dve, BATCH - 1, JS - 1, 1, False, True)
                dve_norm(dve, BATCH * JS - 2, JS - 2, 1)
                dve_norm(dve, BATCH * JS - 1, JS - 1, 1)
                dve_add(dve, BATCH - 1)

            @block.scalar
            def _(act):
                act.wait_ge(k["vz"], 2)
                if rope:
                    act_v(act, 0, 0)
                act_mt(act, 0, 0, 0)
                window(act_step, act, 0, 0, True, False)
                with act.Fori(0, PAIRS) as pair:
                    window(act_step, act, pair * 2 + 1, 1, False, False)
                    window(act_step, act, pair * 2 + 2, 0, False, False)
                window(act_step, act, BATCH - 1, 1, False, True)
                act_step(act, BATCH - 1, JS - 1, 1, False, True)
                act_oc(act, BATCH * JS - 1)
                act_turn(act, BATCH - 1)

            @block.gpsimd
            def _(pool):
                pool_xb(pool, 0, 0)
                pool_xb(pool, 1, 1)
                pool_parts(pool, 0)
                nc.gpsimd.tensor_tensor(m.x[:], m.x[:], a.bo[:].rearrange("p (a d) -> p a d", a=1)
                                        .to_broadcast([P, TILES, DIM]), ALU.add).then_inc(k["bias"], 1)
                pool_parts(pool, 1)
                with pool.Fori(0, PAIRS) as pair:
                    pool_xb(pool, pair * 2 + 2, 0)
                    pool_parts(pool, pair * 2 + 2)
                    pool_xb(pool, pair * 2 + 3, 1)
                    pool_parts(pool, pair * 2 + 3)


def batch_attention(nc, m, name, prefetch=None):
    w = m.w
    SCALE = float(MHD) ** -0.5
    with ExitStack() as own:
        def sb(n, shape, dt=F32):
            return own.enter_context(nc.sbuf_tensor(f"{name}_{n}", shape, dt))

        qt = sb("q_t", [P, BATCH, SEQ])
        km = sb("k_t", [P, MH, BATCH, SEQ])
        kb = sb("k_bias", [P, MH])
        ot = sb("o_t", [P, BATCH, SEQ])
        xg = sb("x_group", [P, 2, P])
        qg = sb("q_group", [P, 2, P])
        v = sb("v", [P, 2, P])
        nb = sb("neg_max", [P, 2, MH])
        sums = sb("sums", [P, 2, MH])
        rec = sb("rec", [P, 2, MH])
        pr = sb("probs", [P, 2, MH, P])
        pt = sb("probs_t", [P, 2, MH, P])
        y = m.xn
        k = sems(nc, own, "qp qe kb qc xc sc vp ve mx nb ex rc nr tp tc pv oe pr r1 st pw nn yt rs gb", f"{name}_")
        ps = m.ps
        SC, VB, PT, OT = 0, 2, 4, 6

        def cols(t, g):
            if isinstance(g, int):
                return t[:, :, g * PG:(g + 1) * PG]
            return t[:, :, bass.ds(g * PG, PG)]

        def pool_q(pool, g, r):
            if not (isinstance(g, int) and g <= 1):
                pool.wait_ge(k["sc"], g - 1)
            nc.gpsimd.tensor_copy(qg[:, r, :].rearrange("p (b t) -> p b t", b=BATCH), cols(qt, g)).then_inc(k["qc"], 1)

        def pool_x(pool, g, r):
            if not (isinstance(g, int) and g <= 1):
                pool.wait_ge(k["vp"], g - 1)
            nc.gpsimd.tensor_copy(xg[:, r, :].rearrange("p (b t) -> p b t", b=BATCH), cols(m.xt[:, :, PAD:], g))\
                .then_inc(k["xc"], 1)

        def pe_v(pe, g, r):
            pe.wait_ge(k["xc"], g + 1)
            if not (isinstance(g, int) and g <= 1):
                pe.wait_ge(k["ve"], g - 1)
            nc.tensor.matmul(ps[:, VB + r, 0:P], xg[:, r, :], w.m_v[:], start=True, stop=True).then_inc(k["vp"], 1)

        def pe_scores(pe, g, r):
            pe.wait_ge(k["qc"], g + 1)
            if not (isinstance(g, int) and g <= 1):
                pe.wait_ge(k["ex"], g - 1)
            nc.tensor.matmul(ps[:, SC + r, :], m.identb[:], w.m_mask[:].rearrange("p (a c) -> p a c", a=1)
                             .to_broadcast([P, MH, P]), start=True, stop=False, skip_group_check=True)
            keys = km[:, :, :, g * PG:(g + 1) * PG] if isinstance(g, int) else km[:, :, :, bass.ds(g * PG, PG)]
            nc.tensor.matmul(ps[:, SC + r, :], qg[:, r, :], keys, start=False, stop=True,
                             skip_group_check=True).then_inc(k["sc"], 1)

        def pe_turn(pe, g, r):
            pe.wait_ge(k["nr"], g + 1)
            if not (isinstance(g, int) and g <= 1):
                pe.wait_ge(k["tc"], g - 1)
            for h in range(MH):
                ins = nc.tensor.transpose(ps[:, PT + r, h * P:(h + 1) * P], pr[:, r, h, :], m.ident[:])
            ins.then_inc(k["tp"], 1)

        def pe_pv(pe, g, r):
            pe.wait_ge(k["tc"], g + 1)
            pe.wait_ge(k["ve"], g + 1)
            pe.wait_ge(k["oe"], g + 1)
            for h in range(MH):
                ins = nc.tensor.matmul(ps[MHD * h:MHD * (h + 1), OT + r, 0:P], v[:, r, MHD * h:MHD * (h + 1)],
                                       pt[:, r, h, :], start=True, stop=True)
            ins.then_inc(k["pv"], 1)

        def pe_step(pe, g, r, last=False):
            if not last:
                pe_scores(pe, g + 1, 1 - r)
            if not (isinstance(g, int) and g == 0):
                pe_turn(pe, g - 1, 1 - r)
                pe_v(pe, g - 1, 1 - r)
            if not (isinstance(g, int) and g <= 1):
                pe_pv(pe, g - 2, r)

        def dve_max(dve, g, r):
            dve.wait_ge(k["sc"], g + 1)
            if not (isinstance(g, int) and g <= 1):
                dve.wait_ge(k["ex"], g - 1)
            nc.vector.tensor_reduce(nb[:, r, :], ps[:, SC + r, :].rearrange("p (h t) -> p h t", h=MH), AX.X,
                                    ALU.max).then_inc(k["mx"], 1)
            dve.wait_ge(k["mx"], g + 1)
            nc.vector.tensor_scalar(nb[:, r, :], nb[:, r, :], -SCALE, None, ALU.mult).then_inc(k["nb"], 1)

        def dve_norm(dve, g, r):
            dve.wait_ge(k["ex"], g + 1)
            nc.vector.reciprocal(rec[:, r, :], sums[:, r, :]).then_inc(k["rc"], 1)
            dve.wait_ge(k["rc"], g + 1)
            nc.vector.tensor_tensor(pr[:, r], pr[:, r], rec[:, r, :].rearrange("p (h a) -> p h a", a=1)
                                    .to_broadcast([P, MH, P]), ALU.mult).then_inc(k["nr"], 1)

        def dve_step(dve, g, r, last):
            if not last:
                dve_max(dve, g + 1, 1 - r)
            dve_norm(dve, g, r)

        def act_exp(act, g, r):
            act.wait_ge(k["nb"], g + 1)
            if not (isinstance(g, int) and g <= 1):
                act.wait_ge(k["tp"], g - 1)
            for h in range(MH):
                ins = nc.scalar.activation(pr[:, r, h, :], ps[:, SC + r, h * P:(h + 1) * P], ACT.Exp,
                                           bias=nb[:, r, h:h + 1], scale=SCALE, accum_out=sums[:, r, h:h + 1])
            ins.then_inc(k["ex"], 1)

        def act_v(act, g, r):
            act.wait_ge(k["vp"], g + 1)
            if not (isinstance(g, int) and g <= 1):
                act.wait_ge(k["pv"], g - 1)
            nc.scalar.activation(v[:, r, :], ps[:, VB + r, 0:P], ACT.Copy).then_inc(k["ve"], 1)

        def act_turn(act, g, r):
            act.wait_ge(k["tp"], g + 1)
            if not (isinstance(g, int) and g <= 1):
                act.wait_ge(k["pv"], g - 1)
            nc.scalar.activation(pt[:, r].rearrange("p h t -> p (h t)"), ps[:, PT + r, :], ACT.Copy)\
                .then_inc(k["tc"], 1)

        def act_out(act, g, r):
            act.wait_ge(k["pv"], g + 1)
            act.wait_ge(k["qe"], 2 * GROUPS)
            nc.scalar.activation(cols(ot, g), ps[:, OT + r, 0:P].rearrange("p (b t) -> p b t", b=BATCH), ACT.Identity,
                                 bias=w.m_bqkv[:, 2:3]).then_inc(k["oe"], 1)

        def act_step(act, g, r, last=False):
            if not last:
                act_exp(act, g + 1, 1 - r)
            if not (isinstance(g, int) and g == 0):
                act_turn(act, g - 1, 1 - r)
                act_v(act, g - 1, 1 - r)
            if not (isinstance(g, int) and g <= 1):
                act_out(act, g - 2, r)

        LOOPS = (NPG - 4) // 2
        with nc.Block() as block:
            if prefetch:
                @block.sync
                def _(sp):
                    prefetch(sp)

            @block.tensor
            def _(pe):
                for i, wt in enumerate((w.m_q, w.m_k)):
                    for g in range(GROUPS):
                        nc.tensor.matmul(ps[:, 4 * i + g, :], wt[:], m.xt[:, 2 * g:2 * g + 2, PAD:], start=True,
                                         stop=True).then_inc(k["qp"], 1)
                pe.wait_ge(k["qe"], 2 * GROUPS)
                pe_scores(pe, 0, 0)
                pe_step(pe, 0, 0)
                pe_step(pe, 1, 1)
                with pe.Fori(0, LOOPS) as i:
                    pe_step(pe, i * 2 + 2, 0)
                    pe_step(pe, i * 2 + 3, 1)
                pe_step(pe, NPG - 2, 0)
                pe_step(pe, NPG - 1, 1, last=True)
                pe_turn(pe, NPG - 1, 1)
                pe_v(pe, NPG - 1, 1)
                pe_pv(pe, NPG - 2, 0)
                pe_pv(pe, NPG - 1, 1)
                pe.wait_ge(k["oe"], NPG + 2)
                for t in range(TILES):
                    ins = nc.tensor.matmul(ps[:, t // GT, (t % GT) * P:(t % GT + 1) * P],
                                           ot[:, t // 2, (t % 2) * P:(t % 2 + 1) * P], w.m_o[:], start=(t % GT == 0),
                                           stop=True, skip_group_check=True)
                    if t % GT == GT - 1:
                        ins.then_inc(k["pr"], 1)
                for g in range(GROUPS):
                    pe.wait_ge(k["nn"], g + 1)
                    for t in range(GT):
                        ins = nc.tensor.transpose(ps[:, 4 + g, t * P:(t + 1) * P], y[:, g * GT + t, :], m.ident[:])
                    ins.then_inc(k["yt"], 1)

            @block.vector
            def _(dve):
                nc.vector.tensor_tensor(kb[:], w.head_rows[:], w.m_bqkv[:, 1:2].to_broadcast([P, MH]),
                                        ALU.mult).then_inc(k["kb"], 1)
                dve.wait_ge(k["kb"], 1)
                for g in range(GROUPS // 2, GROUPS):
                    dve.wait_ge(k["qp"], GROUPS + g + 1)
                    for h in range(MH):
                        ins = nc.vector.tensor_scalar(km[:, h, 2 * g:2 * g + 2, :],
                                                      ps[:, 4 + g, :].rearrange("p (b t) -> p b t", b=2),
                                                      w.head_rows[:, h:h + 1], kb[:, h:h + 1], ALU.mult, ALU.add)
                    ins.then_inc(k["qe"], 1)
                dve_max(dve, 0, 0)
                dve_step(dve, 0, 0, False)
                with dve.Fori(0, LOOPS + 1) as i:
                    dve_step(dve, i * 2 + 1, 1, False)
                    dve_step(dve, i * 2 + 2, 0, False)
                dve_step(dve, NPG - 1, 1, True)
                dve.wait_ge(k["rs"], 1)
                for g in range(GROUPS):
                    dve.wait_ge(k["pr"], g + 1)
                    yg = y[:, g * GT:(g + 1) * GT, :].rearrange("p t d -> p (t d)")
                    nc.vector.tensor_tensor(yg, yg, ps[:, g, :], ALU.add).then_inc(k["r1"], 1)
                    dve.wait_ge(k["r1"], g + 1)
                    group_stats(nc, dve, m, y, g, k["st"])
                    if g:
                        group_scale(nc, dve, m, y, g - 1, k["pw"], k["nn"])
                group_scale(nc, dve, m, y, GROUPS - 1, k["pw"], k["nn"])

            @block.scalar
            def _(act):
                for g in range(GROUPS):
                    act.wait_ge(k["qp"], g + 1)
                    nc.scalar.activation(qt[:, 2 * g:2 * g + 2, :], ps[:, g, :].rearrange("p (b t) -> p b t", b=2),
                                         ACT.Identity, bias=w.m_bqkv[:, 0:1]).then_inc(k["qe"], 1)
                act.wait_ge(k["kb"], 1)
                for g in range(GROUPS // 2):
                    act.wait_ge(k["qp"], GROUPS + g + 1)
                    for h in range(MH):
                        ins = nc.scalar.activation(km[:, h, 2 * g:2 * g + 2, :],
                                                   ps[:, 4 + g, :].rearrange("p (b t) -> p b t", b=2), ACT.Identity,
                                                   bias=kb[:, h:h + 1], scale=w.head_rows[:, h:h + 1])
                    ins.then_inc(k["qe"], 1)
                act.sem_inc(k["oe"], 2)
                act_exp(act, 0, 0)
                act_step(act, 0, 0)
                act_step(act, 1, 1)
                with act.Fori(0, LOOPS) as i:
                    act_step(act, i * 2 + 2, 0)
                    act_step(act, i * 2 + 3, 1)
                act_step(act, NPG - 2, 0)
                act_step(act, NPG - 1, 1, last=True)
                act_turn(act, NPG - 1, 1)
                act_v(act, NPG - 1, 1)
                act_out(act, NPG - 2, 0)
                act_out(act, NPG - 1, 1)
                for g in range(GROUPS):
                    act.wait_ge(k["yt"], g + 1)
                    nc.scalar.activation(m.xt[:, 2 * g:2 * g + 2, PAD:],
                                         ps[:, 4 + g, :].rearrange("p (b t) -> p b t", b=2), ACT.Identity,
                                         scale=w.m_gb[:, 0:1], bias=w.m_gb[:, 1:2])

            @block.gpsimd
            def _(pool):
                pool.wait_ge(k["qe"], 2 * GROUPS)
                pool_q(pool, 0, 0)
                pool_q(pool, 1, 1)
                pool_x(pool, 0, 0)
                pool_q(pool, 2, 0)
                pool_x(pool, 1, 1)
                with pool.Fori(0, LOOPS) as i:
                    pool_q(pool, i * 2 + 3, 1)
                    pool_x(pool, i * 2 + 2, 0)
                    pool_q(pool, i * 2 + 4, 0)
                    pool_x(pool, i * 2 + 3, 1)
                pool_q(pool, NPG - 1, 1)
                pool_x(pool, NPG - 2, 0)
                pool_x(pool, NPG - 1, 1)
                nc.gpsimd.tensor_tensor(y[:], y[:], w.m_rows[:, 0:1, :].to_broadcast([P, TILES, DIM]),
                                        ALU.add).then_inc(k["rs"], 1)
                for g in range(GROUPS):
                    group_power(nc, pool, m, g, k["st"], k["pw"])


def load_experts(nc, m, ctx, dram):
    def sb(name, shape, dt=F32):
        return ctx.enter_context(nc.sbuf_tensor(name, shape, dt))

    e = m.experts = Net()
    e.w1 = sb("e_w1", [P, EXP, FF])
    e.w2 = sb("e_w2", [P, EXP, FT, DIM])
    e.bias = sb("e_bias", [3, EXP * (FF + DIM)], BF16)
    e.ones = sb("e_ones", [3, P], BF16)
    e.loaded = ctx.enter_context(nc.semaphore("experts_loaded"))
    e.sorted_in = nc.dram_tensor("sorted_in", (SORTED * P, DIM), F32, kind="Internal").ap()
    e.sorted_out = nc.dram_tensor("sorted_out", (SORTED * P, DIM), F32, kind="Internal").ap()

    def prefetch(sp):
        sp.dma_start(e.w1[:], dram["m_w1"]).then_inc(e.loaded, 16)
        sp.dma_start(e.w2[:], dram["m_w2"]).then_inc(e.loaded, 16)

    return prefetch


def experts(nc, m, name, dram, first, out=None):
    w, e = m.w, m.experts
    with ExitStack() as own:
        def sb(n, shape, dt=F32):
            return own.enter_context(nc.sbuf_tensor(f"{name}_{n}", shape, dt))

        BR = EXP * (FF + DIM) // P
        logits_t = sb("logits_t", [P, BANK])
        logits = sb("logits", [P, TILES, EXP])
        best = sb("best", [P, TILES])
        hot = sb("hot", [P, TILES, EXP])
        order = sb("order", [P, EXP])
        total = sb("total", [P, EXP, TILES])
        upto = sb("upto", [P, EXP, TILES])
        over = sb("over", [P, EXP, TILES])
        need = sb("need", [P, EXP])
        end = sb("end", [P, EXP])
        at = sb("at", [P, EXP, TILES])
        place = sb("place", [P, TILES, EXP])
        rank = sb("rank", [P, TILES])
        row = sb("row", [P, TILES], mybir.dt.uint32)
        passed = sb("passed", [1, SORTED, EXP])
        idf = sb("tile_expert_f", [1, SORTED])
        ids = sb("tile_expert", [1, SORTED], mybir.dt.int32)
        zeros = sb("zeros", [P, DIM])
        bias_rows = sb("bias_rows", [BR, P])
        bias_rest = sb("bias_rest", [BR, P])
        bias_parts = sb("bias_parts", [BR, 3, P], BF16)
        xs = sb("x_sorted", [P, SORTED, DIM])
        xl = sb("x_tile", [P, 2, DIM])
        xt = sb("x_tile_t", [P, 2, P])
        h = sb("h", [P, 2, FF])
        ht = sb("h_t", [P, 2, FT, P])
        o = sb("o", [P, 2, DIM])
        moe = sb("moe", [P, TILES, DIM])
        y = m.xn
        k = sems(nc, own, "zero cleared bl bz bc order gl lc lg st cnt sorted ids put got got_rest sl xp xc hid rl tp hc od oc even odd "
                          "f0 f1 f2 f3 gb sum nn pw sc g2 formed out", f"{name}_")
        stored, fetched = (k["even"], k["odd"]), [k[f"f{g}"] for g in range(GROUPS)]
        ps = m.ps
        XT, HID, HT, OUT = 0, 2, 4, 6

        def expert_of(i):
            at_i = ids[0:1, i:i + 1] if isinstance(i, int) else ids[0:1, bass.ds(i, 1)]
            return nc.values_load(at_i, engines=[mybir.EngineType.PE], min_val=0, max_val=EXP - 1)

        def pe_turn_x(pe, i, r):
            if not (isinstance(i, int) and i <= 1):
                pe.wait_ge(k["xc"], i - 1)
            pe.wait_ge(k["sl"], i + 1)
            nc.tensor.transpose(ps[:, XT + r, 0:P], xl[:, r, :], m.ident[:]).then_inc(k["xp"], 1)

        def pe_hidden(pe, i, r):
            ex = expert_of(i)
            if not (isinstance(i, int) and i <= 1):
                pe.wait_ge(k["rl"], i - 1)
            pe.wait_ge(k["xc"], i + 1)
            nc.tensor.matmul(ps[:, HID + r, :], e.ones[:], e.bias[:, bass.ds(ex * FF, FF)], start=True, stop=False,
                             skip_group_check=True)
            nc.tensor.matmul(ps[:, HID + r, :], xt[:, r, :], e.w1[:, bass.ds(ex, 1), :].rearrange("p a f -> p (a f)"),
                             start=False, stop=True, skip_group_check=True).then_inc(k["hid"], 1)

        def pe_turn_h(pe, i, r):
            if not (isinstance(i, int) and i <= 1):
                pe.wait_ge(k["hc"], i - 1)
            pe.wait_ge(k["rl"], i + 1)
            for f in range(FT):
                ins = nc.tensor.transpose(ps[:, HT + r, f * P:(f + 1) * P], h[:, r, f * P:(f + 1) * P], m.ident[:])
            ins.then_inc(k["tp"], 1)

        def pe_second(pe, i, r):
            ex = expert_of(i)
            if not (isinstance(i, int) and i <= 1):
                pe.wait_ge(k["oc"], i - 1)
            pe.wait_ge(k["hc"], i + 1)
            nc.tensor.matmul(ps[:, OUT + r, 0:DIM], e.ones[:], e.bias[:, bass.ds(ex * DIM + EXP * FF, DIM)], start=True,
                             stop=False, skip_group_check=True)
            for f in range(FT):
                ins = nc.tensor.matmul(ps[:, OUT + r, 0:DIM], ht[:, r, f, :],
                                       e.w2[:, bass.ds(ex, 1), f, :].rearrange("p a d -> p (a d)"), start=False,
                                       stop=(f == FT - 1), skip_group_check=True)
            ins.then_inc(k["od"], 1)

        def pe_step(pe, i, r):
            if not (isinstance(i, int) and i >= SORTED - 1):
                pe_hidden(pe, i + 1, 1 - r)
            if not (isinstance(i, int) and i == 0):
                pe_second(pe, i - 1, 1 - r)
            if not (isinstance(i, int) and i >= SORTED - 2):
                pe_turn_x(pe, i + 2, r)
            pe_turn_h(pe, i, r)

        def dve_x(dve, i, r):
            dve.wait_ge(k["xp"], i + 1)
            if not (isinstance(i, int) and i <= 1):
                dve.wait_ge(k["hid"], i - 1)
            nc.vector.tensor_copy(xt[:, r, :], ps[:, XT + r, 0:P]).then_inc(k["xc"], 1)

        def dve_h(dve, i, r):
            dve.wait_ge(k["tp"], i + 1)
            if not (isinstance(i, int) and i <= 1):
                dve.wait_ge(k["od"], i - 1)
            nc.vector.tensor_copy(ht[:, r].rearrange("p f t -> p (f t)"), ps[:, HT + r, :]).then_inc(k["hc"], 1)

        def dve_step(dve, i, r):
            if not (isinstance(i, int) and i >= SORTED - 2):
                dve_x(dve, i + 2, r)
            dve_h(dve, i, r)

        def act_relu(act, i, r):
            act.wait_ge(k["hid"], i + 1)
            if not (isinstance(i, int) and i <= 1):
                act.wait_ge(k["tp"], i - 1)
            nc.scalar.activation(h[:, r, :], ps[:, HID + r, :], ACT.Relu).then_inc(k["rl"], 1)

        def act_out(act, i, r, turn):
            act.wait_ge(k["od"], i + 1)
            if not (isinstance(turn, int) and turn == 0):
                act.wait_ge(stored[r], turn * 16)
            nc.scalar.activation(o[:, r, :], ps[:, OUT + r, 0:DIM], ACT.Copy).then_inc(k["oc"], 1)

        def act_step(act, i, r, half):
            if not (isinstance(i, int) and i >= SORTED - 1):
                act_relu(act, i + 1, 1 - r)
            if not (isinstance(i, int) and i == 0):
                act_out(act, i - 1, 1 - r, half if r else half - 1)

        def pool_x(pool, i, r):
            if not (isinstance(i, int) and i <= 1):
                pool.wait_ge(k["xp"], i - 1)
            src = xs[:, i, :] if isinstance(i, int) else xs[:, bass.ds(i, 1), :].rearrange("p a d -> p (a d)")
            nc.gpsimd.tensor_copy(xl[:, r, :], src).then_inc(k["sl"], 1)

        def sp_store(sp, i, r):
            sp.wait_ge(k["oc"], i + 1)
            dst = e.sorted_out[bass.ds(i * P, P), :] if not isinstance(i, int) else e.sorted_out[i * P:(i + 1) * P, :]
            sp.dma_start(dst, o[:, r, :]).then_inc(stored[r], 16)

        LOOPS = (SORTED - 5) // 2
        with nc.Block() as block:
            @block.sync
            def _(sp):
                if first:
                    sp.dma_start(bias_rows[:], dram["m_bias"]).then_inc(k["bl"], 16)
                    sp.wait_ge(k["zero"], 1)
                    sp.dma_start(e.sorted_in.rearrange("(n p) d -> p n d", p=P),
                                 zeros[:].rearrange("p (a d) -> p a d", a=1).to_broadcast([P, SORTED, DIM]))\
                        .then_inc(k["cleared"], 16)
                    sp.wait_ge(k["bz"], 4)
                    for c in range(3):
                        sp.dma_start(e.bias[c:c + 1, :], bias_parts[:, c, :]).then_inc(k["bc"], 16)
                sp.wait_ge(k["put"], 16 * TILES)
                by_tile = e.sorted_in.rearrange("(n p) d -> p n d", p=P)
                sp.dma_start(xs[:, 0:3, :], by_tile[:, 0:3, :]).then_inc(k["got"], 16)
                sp.dma_start(xs[:, 3:, :], by_tile[:, 3:, :]).then_inc(k["got_rest"], 16)
                for i in range(3):
                    sp_store(sp, i, i % 2)
                with sp.Fori(0, LOOPS) as i:
                    sp_store(sp, i * 2 + 3, 1)
                    sp_store(sp, i * 2 + 4, 0)
                sp_store(sp, SORTED - 2, 1)
                sp_store(sp, SORTED - 1, 0)
                if out is not None:
                    by_token = out.rearrange("b (h p) d -> p (b h) d", p=P)
                    for g in range(GROUPS):
                        tiles = slice(g * GT, (g + 1) * GT)
                        sp.wait_ge(k["formed"], g + 1)
                        sp.dma_start(by_token[:, tiles, :], m.x[:, tiles, :]).then_inc(k["out"], 16)
                    sp.wait_ge(k["out"], 16 * GROUPS)

            @block.tensor
            def _(pe):
                for g in range(GROUPS):
                    ins = nc.tensor.matmul(ps[32 * g:32 * g + 32, 5, :], w.m_gate[:], m.xt[:, 2 * g:2 * g + 2, PAD:],
                                           start=True, stop=True, skip_group_check=True)
                ins.then_inc(k["gl"], 1)
                pe.wait_ge(k["lc"], 1)
                for c in range(GT):
                    ins = nc.tensor.transpose(ps[:, 6, c * P:(c + 1) * P], logits_t[:, c * P:(c + 1) * P], m.ident[:])
                ins.then_inc(k["lg"], 1)
                pe.wait_ge(k["st"], 6)
                choices = hot[:].rearrange("p t e -> p (t e)")
                nc.tensor.matmul(ps[:, 7, 0:P], w.before[:], choices, start=True, stop=True)
                nc.tensor.matmul(ps[:, 7, P:2 * P], m.ones[:], choices, start=False, stop=True,
                                 skip_group_check=True).then_inc(k["cnt"], 1)
                pe.wait_ge(e.loaded, 32)
                if first:
                    pe.wait_ge(k["bc"], 48)
                pe.wait_ge(k["ids"], 1)
                pe_turn_x(pe, 0, 0)
                pe_turn_x(pe, 1, 1)
                pe_hidden(pe, 0, 0)
                for i in range(3):
                    pe_step(pe, i, i % 2)
                with pe.Fori(0, LOOPS) as i:
                    pe_step(pe, i * 2 + 3, 1)
                    pe_step(pe, i * 2 + 4, 0)
                pe_step(pe, SORTED - 2, 1)
                pe_step(pe, SORTED - 1, 0)
                pe_second(pe, SORTED - 1, 0)

            @block.scalar
            def _(act):
                act.wait_ge(k["gl"], 1)
                nc.scalar.activation(logits_t[:], ps[:, 5, :], ACT.Copy).then_inc(k["lc"], 1)
                act_relu(act, 0, 0)
                for i in range(3):
                    act_step(act, i, i % 2, i // 2)
                with act.Fori(0, LOOPS) as i:
                    act_step(act, i * 2 + 3, 1, i + 1)
                    act_step(act, i * 2 + 4, 0, i + 2)
                act_step(act, SORTED - 2, 1, SORTED // 2 - 1)
                act_step(act, SORTED - 1, 0, SORTED // 2)
                act_out(act, SORTED - 1, 0, SORTED // 2)

            @block.vector
            def _(dve):
                dve.wait_ge(k["lg"], 1)
                nc.vector.tensor_copy(logits[:].rearrange("p (g c) e -> p c g e", c=GT),
                                      ps[:, 6, :].rearrange("p (c g e) -> p c g e", c=GT, e=32)[:, :, :, 0:EXP])\
                    .then_inc(k["st"], 1)
                pick_first(nc, dve, k["st"], 1, k["order"], logits, best, hot, order)
                dve.wait_ge(k["cnt"], 1)
                before_p = ps[:, 7, 0:P].rearrange("p (t e) -> p t e", e=EXP)
                in_tile = ps[:, 7, P:2 * P].rearrange("p (t e) -> p e t", e=EXP)
                nc.vector.tensor_copy(total[:], in_tile).then_inc(k["sorted"], 1)
                dve.wait_ge(k["sorted"], 1)
                nc.vector.tensor_tensor_scan(upto[:].rearrange("p e t -> p (e t)"), w.sort_not_first[:],
                                             total[:].rearrange("p e t -> p (e t)"), 0.0, ALU.mult, ALU.add)\
                    .then_inc(k["sorted"], 1)
                dve.wait_ge(k["sorted"], 2)
                nc.vector.tensor_tensor(over[:], upto[:, :, TILES - 1:TILES].to_broadcast([P, EXP, TILES]),
                                        w.sort_multiples[:].rearrange("p (a t) -> p a t", a=1)
                                        .to_broadcast([P, EXP, TILES]), ALU.is_gt).then_inc(k["sorted"], 1)
                nc.vector.tensor_tensor(at[:], upto[:], total[:], ALU.subtract).then_inc(k["sorted"], 1)
                dve.wait_ge(k["sorted"], 3)
                nc.vector.tensor_reduce(need[:], over[:], AX.X, ALU.add).then_inc(k["sorted"], 1)
                dve.wait_ge(k["sorted"], 5)
                nc.vector.tensor_tensor_scan(end[:], m.ones[:, 0:EXP], need[:], 0.0, ALU.mult, ALU.add)\
                    .then_inc(k["sorted"], 1)
                dve.wait_ge(k["sorted"], 6)
                nc.vector.tensor_tensor(need[:], end[:], need[:], ALU.subtract).then_inc(k["sorted"], 1)
                dve.wait_ge(k["sorted"], 7)
                nc.vector.scalar_tensor_tensor(out=at[:], in0=need[:].rearrange("p (e a) -> p e a", a=1)
                                               .to_broadcast([P, EXP, TILES]), scalar=float(P), in1=at[:],
                                               op0=ALU.mult, op1=ALU.add).then_inc(k["sorted"], 1)
                dve.wait_ge(k["sorted"], 8)
                nc.vector.tensor_tensor(place[:], at[:].rearrange("p e t -> p t e"), before_p, ALU.add)\
                    .then_inc(k["sorted"], 1)
                dve.wait_ge(k["sorted"], 9)
                nc.vector.tensor_tensor(place[:], place[:], hot[:], ALU.mult).then_inc(k["sorted"], 1)
                dve.wait_ge(k["sorted"], 10)
                nc.vector.tensor_reduce(rank[:], place[:], AX.X, ALU.add).then_inc(k["sorted"], 1)
                dve.wait_ge(k["sorted"], 11)
                nc.vector.tensor_copy(row[:], rank[:]).then_inc(k["sorted"], 1)
                nc.vector.tensor_tensor(passed[:], end[0:1, :].rearrange("p (a e) -> p a e", a=1)
                                        .to_broadcast([1, SORTED, EXP]),
                                        w.sort_tiles[0:1, :].rearrange("p (t a) -> p t a", a=1)
                                        .to_broadcast([1, SORTED, EXP]), ALU.is_le).then_inc(k["sorted"], 1)
                dve.wait_ge(k["sorted"], 13)
                nc.vector.tensor_reduce(idf[:], passed[:], AX.X, ALU.add).then_inc(k["sorted"], 1)
                dve.wait_ge(k["sorted"], 14)
                nc.vector.tensor_scalar(ids[:], idf[:], float(EXP - 1), None, ALU.min).then_inc(k["ids"], 1)
                if first:
                    dve.wait_ge(k["bl"], 16)
                    nc.vector.tensor_copy(bias_parts[:, 0, :], bias_rows[:]).then_inc(k["bz"], 1)
                    dve.wait_ge(k["bz"], 1)
                    nc.vector.tensor_tensor(bias_rest[:], bias_rows[:], bias_parts[:, 0, :], ALU.subtract)\
                        .then_inc(k["bz"], 1)
                    dve.wait_ge(k["bz"], 2)
                    nc.vector.tensor_copy(bias_parts[:, 1, :], bias_rest[:]).then_inc(k["bz"], 1)
                    dve.wait_ge(k["bz"], 3)
                    nc.vector.tensor_tensor(bias_parts[:, 2, :], bias_rest[:], bias_parts[:, 1, :], ALU.subtract)\
                        .then_inc(k["bz"], 1)
                dve_x(dve, 0, 0)
                dve_x(dve, 1, 1)
                for i in range(3):
                    dve_step(dve, i, i % 2)
                with dve.Fori(0, LOOPS) as i:
                    dve_step(dve, i * 2 + 3, 1)
                    dve_step(dve, i * 2 + 4, 0)
                dve_step(dve, SORTED - 2, 1)
                dve_step(dve, SORTED - 1, 0)
                dve.wait_ge(k["order"], 2)

                def finish(g):
                    tiles = slice(g * GT, (g + 1) * GT)
                    group_scale(nc, dve, m, y, g, k["pw"], k["sc"])
                    dve.wait_ge(k["sc"], g + 1)
                    nc.vector.tensor_tensor(y[:, tiles, :], y[:, tiles, :], w.m_rows[:, 3:4, :]
                                            .to_broadcast([P, GT, DIM]), ALU.mult).then_inc(k["g2"], 1)
                    dve.wait_ge(k["g2"], g + 1)
                    nc.vector.tensor_tensor(m.x[:, tiles, :], m.x[:, tiles, :], y[:, tiles, :], ALU.add)\
                        .then_inc(k["formed"], 1)

                for g in range(GROUPS):
                    dve.wait_ge(fetched[g], 16 * GT)
                    tiles = slice(g * GT, (g + 1) * GT)
                    nc.vector.tensor_tensor(y[:, tiles, :], y[:, tiles, :], moe[:, tiles, :], ALU.add)\
                        .then_inc(k["sum"], 1)
                    dve.wait_ge(k["sum"], g + 1)
                    group_stats(nc, dve, m, y, g, k["nn"])
                    if g:
                        finish(g - 1)
                finish(GROUPS - 1)

            @block.gpsimd
            def _(pool):
                nc.gpsimd.iota(order[:], [[-1, EXP]], base=EXP, channel_multiplier=0,
                               allow_small_or_imprecise_dtypes=True).then_inc(k["order"], 1)
                if first:
                    nc.gpsimd.memset(e.ones[:], 1.0)
                    nc.gpsimd.memset(zeros[:], 0.0).then_inc(k["zero"], 1)
                nc.gpsimd.tensor_tensor(y[:], y[:], w.m_rows[:, 1:2, :].to_broadcast([P, TILES, DIM]),
                                        ALU.mult).then_inc(k["gb"], 1)
                pool.wait_ge(k["gb"], 1)
                nc.gpsimd.tensor_tensor(y[:], y[:], w.m_rows[:, 2:3, :].to_broadcast([P, TILES, DIM]),
                                        ALU.add).then_inc(k["gb"], 1)
                if first:
                    pool.wait_ge(k["cleared"], 16)
                pool.wait_ge(k["gb"], 2)
                pool.wait_ge(k["sorted"], 12)
                for t in range(TILES):
                    nc.gpsimd.indirect_dma_start(e.sorted_in, bass.IndirectOffsetOnAxis(ap=row[:, t:t + 1], axis=0),
                                                 y[:, t, :], None).then_inc(k["put"], 16)
                pool.wait_ge(k["got"], 16)
                pool_x(pool, 0, 0)
                pool_x(pool, 1, 1)
                pool_x(pool, 2, 0)
                pool.wait_ge(k["got_rest"], 16)
                with pool.Fori(0, LOOPS + 1) as i:
                    pool_x(pool, i * 2 + 3, 1)
                    pool_x(pool, i * 2 + 4, 0)
                nc.gpsimd.tensor_tensor(m.x[:], m.x[:], w.m_rows[:, 4:5, :].to_broadcast([P, TILES, DIM]),
                                        ALU.add).then_inc(k["order"], 1)
                pool.wait_ge(stored[0], 16 * ((SORTED + 1) // 2))
                pool.wait_ge(stored[1], 16 * (SORTED // 2))
                for g in range(GROUPS):
                    for t in range(g * GT, (g + 1) * GT):
                        nc.gpsimd.indirect_dma_start(moe[:, t, :], None, e.sorted_out,
                                                     bass.IndirectOffsetOnAxis(ap=row[:, t:t + 1], axis=0))\
                            .then_inc(fetched[g], 16)
                    if g:
                        group_power(nc, pool, m, g - 1, k["nn"], k["pw"])
                group_power(nc, pool, m, GROUPS - 1, k["nn"], k["pw"])


def network(nc, dram, out):
    with ExitStack() as ctx:
        m = open_memory(nc, ctx)
        setup(nc, m, ctx, dram)
        layernorm(nc, m, "ln0")
        state_space(nc, m)
        with ExitStack() as conv:
            m.toeplitz = conv.enter_context(nc.sbuf_tensor("toeplitz", [P, DIM, P], F32))
            layernorm(nc, m, "ln1")
            lora_ffn(nc, m, "f1", prefetch=lambda sp: load_toeplitz(sp, m))
            layernorm(nc, m, "ln2", transposed=False)
            long_conv(nc, m)
        layernorm(nc, m, "ln3")
        lora_ffn(nc, m, "f2")
        layernorm(nc, m, "ln4")
        attention(nc, m, "at1", dram, m.w.a1, True)
        layernorm(nc, m, "ln5")
        batch_attention(nc, m, "ba1", prefetch=load_experts(nc, m, ctx, dram))
        experts(nc, m, "ex1", dram, True)
        layernorm(nc, m, "ln6")
        attention(nc, m, "at2", dram, m.w.a2, False)
        layernorm(nc, m, "ln7")
        batch_attention(nc, m, "ba2")
        experts(nc, m, "ex2", dram, False, out)


def lay_out(inputs):
    g = {k: np.asarray(v) for k, v in inputs.items()}

    def cols(a):
        return a.reshape(-1, P).T

    def rows(a):
        return a.reshape(-1, P, a.shape[-1]).transpose(1, 0, 2)

    d = {
        "x": g["L0_attn_a_x"],
        "in_w": g["L0_attn_a_W_in"],
        "conv_rows": g["L0_attn_a_conv_w"][:, 0, :].T,
        "conv_b": cols(g["L0_attn_a_conv_b"]),
        "x_w": rows(g["L0_attn_a_W_x"]),
        "dt_w": g["L0_attn_a_W_dt"],
        "dt_b": cols(g["L0_attn_a_b_dt"]),
        "a_log": rows(g["L0_attn_a_A_log"]),
        "d_skip": cols(g["L0_attn_a_D"]),
        "out_w": rows(g["L0_attn_a_W_out"]),
        "lc_a": g["L0_attn_b_A_log"].reshape(-1, 1),
        "lc_arow": g["L0_attn_b_A_log"],
        "lc_ct": g["L0_attn_b_C"].T,
        "lc_align": cols(g["L0_attn_b_freq_align"]),
        "lc_delta": g["L0_attn_b_delta"][0:1],
        "lc_rows": np.stack([g[f"L0_attn_b_{n}"] for n in ("D", "freq_align", "reward", "gamma", "beta")]),
        "gate": np.concatenate([g["L0_ffn_lora_A"].reshape(ER, DIM).T, g["L0_ffn_gate_W"].T,
                                np.zeros((DIM, 32 - EXP), np.float32)], axis=1),
        "gate_b": g["L0_ffn_gate_b"],
        "wi": g["L0_ffn_wi_W"].T,
        "wi_b": cols(g["L0_ffn_wi_b"]),
        "wo": rows(np.ascontiguousarray(g["L0_ffn_wo_W"].T)),
        "wo_b": g["L0_ffn_wo_b"],
        "lora_b": np.concatenate([np.pad(g["L0_ffn_lora_B"].transpose(0, 2, 1).reshape(ER, FF),
                                         ((32 * i, P - 32 - 32 * i), (0, 0)))[:, None] for i in range(GROUPS)], axis=1),
    }
    straight = np.concatenate([h * HD + np.r_[0:HD:2, 1:HD:2] for h in range(HEADS)])
    crossed = np.concatenate([h * HD + np.r_[1:HD:2, 0:HD:2] for h in range(HEADS)])
    wq, wk, wv = np.split(g["L1_attn_a_w_qkv"], 3, axis=0)

    half = (np.arange(0, HD, 2, dtype=np.float32) / np.float32(HD)).astype(np.float32)
    inv = (np.float32(1) / np.power(np.float32(10000), half)).astype(np.float32)
    angle = np.outer(inv, np.arange(SEQ, dtype=np.float32)).astype(np.float32)
    cos, sin = np.cos(angle), np.sin(angle)
    mask = np.where(allowed_pairs(), 0, NEG).astype(np.float32)
    same = np.arange(P) % PG
    d.update({
        "a1_wq1": wq[straight].T, "a1_wq2": wq[crossed].T, "a1_wk1": wk[straight].T, "a1_wk2": wk[crossed].T,
        "a1_wv": wv.T, "a1_wo": g["L1_attn_a_w_out"].T, "a1_bo": g["L1_attn_a_b_out"],
        "a1_cos": np.tile(np.concatenate([cos, cos]), (HEADS, 1)),
        "a1_sin": np.tile(np.concatenate([-sin, sin]), (HEADS, 1)),
        "a2_wq": g["L1_attn_b_Wq"], "a2_wk": g["L1_attn_b_Wk"], "a2_wv": g["L1_attn_b_Wv"],
        "a2_wo": g["L1_attn_b_Wo"],
        "a2_bq": g["L1_attn_b_bq"].reshape(P, 1),
        "a2_bo": g["L1_attn_b_bo"],
        "a2_bv": g["L1_attn_b_bv"],
        "head_rows": (np.arange(P)[:, None] // MHD == np.arange(MH)[None, :]).astype(np.float32),
        "pick_max": (np.arange(P)[:, None] % 4 == np.arange(4)[None, :]).astype(np.float32),
        "zeros": np.zeros(HEADS * SEQ, np.float32),
        "mask_q": mask.reshape(2, P, SEQ).transpose(1, 0, 2),
        "mask_k": mask.T.reshape(2, P, SEQ).transpose(1, 0, 2),
        "m_q": g["L1_ffn_Wqkv"][0:DIM].T, "m_k": g["L1_ffn_Wqkv"][DIM:2 * DIM].T, "m_v": g["L1_ffn_Wqkv"][2 * DIM:].T,
        "m_o": g["L1_ffn_Wo"].T, "m_bqkv": cols(g["L1_ffn_bqkv"]),
        "m_gb": np.stack([g["L1_ffn_g1"], g["L1_ffn_be1"]], axis=1),
        "m_rows": np.stack([g[f"L1_ffn_{n}"] for n in ("bo", "g1", "be1", "g2", "be2")]),
        "m_gate": np.pad(g["L1_ffn_Wg"].T, ((0, 0), (0, 32 - EXP))),
        "m_mask": np.where(same[:, None] == same[None, :], 0, NEG).astype(np.float32),
        "m_w1": g["L1_ffn_W1"].transpose(1, 0, 2),
        "m_w2": g["L1_ffn_W2"].reshape(EXP, FT, P, DIM).transpose(2, 0, 1, 3),
        "m_bias": np.concatenate([g["L1_ffn_b1"].reshape(-1, P), g["L1_ffn_b2"].reshape(-1, P)]),
        "sort_before": np.triu(np.ones((P, P), np.float32), 1),
        "sort_not_first": (np.arange(EXP * TILES) % TILES > 0).astype(np.float32),
        "sort_multiples": (np.arange(TILES) * P).astype(np.float32),
        "sort_tiles": np.arange(SORTED).astype(np.float32),
    })
    for pack, names in PACKS.items():
        parts = [d.pop(name) for name in names.split()]
        if pack.startswith("rows_"):
            d[pack] = np.concatenate([a.reshape(-1) for a in parts])
        else:
            d[pack] = np.concatenate([a.reshape(a.shape[0], -1) for a in parts], axis=1)
    return {k: np.ascontiguousarray(v) for k, v in d.items()}


def kernel(**inputs):
    import concourse.bacc as bacc
    from concourse.bass_utils import run_bass_kernel_spmd as run

    nc = bacc.Bacc("TRN2", target_bir_lowering=False, num_devices=1)
    arrays, dram = {}, {}
    for name, a in lay_out(inputs).items():
        arrays[f"in_{name}_dram"] = a
        dram[name] = nc.dram_tensor(f"in_{name}_dram", a.shape, mybir.dt.from_np(a.dtype), kind="ExternalInput").ap()
    out = nc.dram_tensor("out_0_dram", (BATCH, SEQ, DIM), F32, kind="ExternalOutput").ap()
    network(nc, dram, out)
    return run(nc, [arrays], core_ids=[0]).results[0]["out_0_dram"]
```
